# Optimizing a Trainium2 kernel written in Bass

```python
import numpy as np
import jax
import jax.numpy as jnp

def _softmax(x, axis=-1):
    return jax.nn.softmax(x, axis=axis)

def _gelu(x):
    return jax.nn.gelu(x, approximate=True)

def _silu(x):
    return jax.nn.silu(x)

def _sigmoid(x):
    return jax.nn.sigmoid(x)

def _layernorm(x, axis=-1, eps=1e-05):
    m = jnp.mean(x, axis=axis, keepdims=True)
    v = jnp.var(x, axis=axis, keepdims=True)
    return (x - m) / jnp.sqrt(v + eps)

def _scatter_add(tgt, idx, src, axis=0):
    return tgt.at[idx].add(src)

def _segment_sum(src, seg, n):
    return jax.ops.segment_sum(src, seg, n)
kernel_name = 'mk_flamingo_gated_d2_seqx_r8_3fdc34'

def setup_inputs(seed: int=0):
    np.random.seed(seed)
    _w = jnp.asarray

    def _rec_inputs():
        import jax
        import jax.numpy as jnp
        _rk = jax.random.key(seed)
        x = -0.000125 + 0.9999 * jax.random.normal(jax.random.fold_in(_rk, 1), (4, 256, 256), jnp.float32)
        _lenS = 256 - jax.random.randint(jax.random.fold_in(_rk, 7), (4,), 0, max(1, 256 // 4) + 1, jnp.int32)
        _lenS2 = 256 - jax.random.randint(jax.random.fold_in(_rk, 8), (4,), 0, max(1, 256 // 4) + 1, jnp.int32)
        itok_BxS_13_99985 = jax.random.randint(jax.random.fold_in(_rk, 11), (4, 256), 13, 99986, jnp.int32)
        _ctx_2048P = jax.random.normal(jax.random.fold_in(_rk, 12), (4, 16, 256), jnp.float32)
        _ctx_2048c = jax.random.dirichlet(jax.random.fold_in(_rk, 512), 0.3 * jnp.ones((16,), jnp.float32), (4, 256))
        _ctx_2048t = jnp.einsum('bsk,bkd->bsd', _ctx_2048c, _ctx_2048P)
        _ctx_2048t = _ctx_2048t * jax.lax.rsqrt(jnp.mean(jnp.square(_ctx_2048t)) + 1e-12) * 0.953939
        ctx_2048 = 6.82029e-06 + 0.0200006 * (_ctx_2048t + 0.3 * jax.random.normal(jax.random.fold_in(_rk, 612), (4, 256, 256), jnp.float32))
        _validS = jnp.arange(256)[None, :] < _lenS[:, None]
        _validS2 = jnp.arange(256)[None, :] < _lenS2[:, None]
        _causal = jnp.tril(jnp.ones((256, 256), dtype=bool))
        mask_BxSxS2_ff0 = jnp.where(jnp.ones((4, 256, 256), dtype=bool), 0.0, -1000000000.0).astype(jnp.float32)
        _g = jax.random.normal(jax.random.fold_in(_rk, 9001), (2, 2), jnp.float32)
        _g = jnp.sign(_g) * jnp.maximum(jnp.abs(_g), 1.0) + (_g == 0) * 1.0
        g_xattn = _g[0]
        g_ffn = _g[1]
        return (x, itok_BxS_13_99985, ctx_2048, mask_BxSxS2_ff0, g_xattn, g_ffn)
    x, itok_BxS_13_99985, ctx_2048, mask_BxSxS2_ff0, g_xattn, g_ffn = _rec_inputs()

    def _L0_xattn_setup():
        import jax, jax.numpy as jnp
        import numpy as np
        B, S, D = (4, 512, 256)
        E = 4
        F = 1024 // E
        VOCAB = 12500
        key = jax.random.key(seed)
        k1, k2, k3, k4, k5 = jax.random.split(key, 5)
        hidden_states = jax.random.normal(k1, (B, S, D), dtype=jnp.float32)
        token_ids = jax.random.randint(k2, (B, S), 0, VOCAB, dtype=jnp.int64)
        Wg = jax.random.normal(k3, (E, F, D), dtype=jnp.float32) * 0.02
        Wu = jax.random.normal(k4, (E, F, D), dtype=jnp.float32) * 0.02
        Wd = jax.random.normal(k5, (E, D, F), dtype=jnp.float32) * 0.02
        return {'hidden_states': hidden_states, 'token_ids': token_ids, 'Wg': Wg, 'Wu': Wu, 'Wd': Wd}
    _L0_xattn_all = _L0_xattn_setup()
    _L0_xattn_in = {k: v for k, v in _L0_xattn_all.items() if k in ()}
    del _L0_xattn_all

    def _L0_ffn_setup():
        import jax, jax.numpy as jnp
        import numpy as np
        EPS = 1e-05

        def _quant_weight(w):
            scale = jnp.mean(jnp.abs(w)) + EPS
            wq = jnp.clip(jnp.round(w / scale), -1.0, 1.0)
            return (wq, scale)

        def _quant_act(x):
            s = jnp.max(jnp.abs(x), axis=-1, keepdims=True) / 127.0 + EPS
            xq = jnp.clip(jnp.round(x / s), -128.0, 127.0)
            return (xq, s)

        def _qlinear(x, w):
            wq, ws = _quant_weight(w)
            xq, xs = _quant_act(x)
            y = jnp.einsum('bsi,oi->bso', xq, wq)
            return y * xs * ws
        key = jax.random.key(seed)
        k1, k2, k3, k4 = jax.random.split(key, 4)
        H, I = (256, 1024)
        x = jax.random.normal(k1, (4, 512, H), dtype=jnp.float32)
        w_gate = jax.random.normal(k2, (I, H), dtype=jnp.float32) * (1.0 / np.sqrt(H))
        w_up = jax.random.normal(k3, (I, H), dtype=jnp.float32) * (1.0 / np.sqrt(H))
        w_down = jax.random.normal(k4, (H, I), dtype=jnp.float32) * (1.0 / np.sqrt(I))
        return {'x': x, 'w_gate': w_gate, 'w_up': w_up, 'w_down': w_down}
    _L0_ffn_all = _L0_ffn_setup()
    _L0_ffn_in = {k: v for k, v in _L0_ffn_all.items() if k in ('w_gate', 'w_up', 'w_down')}
    del _L0_ffn_all

    def _L1_xattn_setup():
        import jax, jax.numpy as jnp
        import numpy as np
        NUM_HEADS = 16
        EPS = 1e-08

        def _dyn_quant(x):
            s = jnp.maximum(jnp.max(jnp.abs(x), axis=-1, keepdims=True) / 127.0, EPS)
            q = jnp.clip(jnp.round(x / s), -127.0, 127.0)
            return (q, s)

        def _quant_weight(w):
            s = jnp.maximum(jnp.max(jnp.abs(w), axis=1, keepdims=True) / 127.0, EPS)
            q = jnp.clip(jnp.round(w / s), -127.0, 127.0)
            return (q, s)

        def _w8a8_linear(x, w, b):
            qx, sx = _dyn_quant(x)
            qw, sw = _quant_weight(w)
            y = jnp.einsum('bnc,oc->bno', qx, qw) * (sx * sw[:, 0])
            return y + b
        key = jax.random.key(seed)
        ks = jax.random.split(key, 9)
        B, N, L, C = (2, 512, 64, 256)
        sc = 0.02
        return {'x': jax.random.normal(ks[0], (B, N, C), jnp.float32), 'cond': jax.random.normal(ks[1], (B, L, C), jnp.float32), 'mask': jnp.zeros((B, N, L), jnp.float32), 'wq': jax.random.normal(ks[2], (C, C), jnp.float32) * sc, 'bq': jnp.zeros((C,), jnp.float32), 'wk': jax.random.normal(ks[3], (C, C), jnp.float32) * sc, 'bk': jnp.zeros((C,), jnp.float32), 'wv': jax.random.normal(ks[4], (C, C), jnp.float32) * sc, 'bv': jnp.zeros((C,), jnp.float32), 'wo': jax.random.normal(ks[5], (C, C), jnp.float32) * sc, 'bo': jnp.zeros((C,), jnp.float32)}
    _L1_xattn_all = _L1_xattn_setup()
    _L1_xattn_in = {k: v for k, v in _L1_xattn_all.items() if k in ('wq', 'bq', 'wk', 'bk', 'wv', 'bv', 'wo', 'bo')}
    del _L1_xattn_all

    def _L1_ffn_setup():
        import jax, jax.numpy as jnp
        import numpy as np
        H = 256
        NH = 16
        NOPE = 128
        ROPE = 64
        VD = 128
        QHD = NOPE + ROPE
        E = 16
        I = 176
        TOPK = 4
        NSH = 2
        SHI = I * NSH
        EPS = 1e-06
        B, S = (2, 128)

        def rmsnorm(x, w):
            return x * jax.lax.rsqrt(jnp.mean(x * x, axis=-1, keepdims=True) + EPS) * w
        key = jax.random.key(seed)
        ks = jax.random.split(key, 12)
        sd = lambda fan_in: 1.0 / np.sqrt(fan_in)
        return {'hidden_states': jax.random.normal(ks[0], (B, S, H), jnp.float32), 'positions': jnp.broadcast_to(jnp.arange(S, dtype=jnp.int32), (B, S)), 'ln1_w': jnp.ones((H,), jnp.float32), 'ln2_w': jnp.ones((H,), jnp.float32), 'q_w': jax.random.normal(ks[1], (NH * QHD, H), jnp.float32) * sd(H), 'kv_w': jax.random.normal(ks[2], (NH * (NOPE + VD) + ROPE, H), jnp.float32) * sd(H), 'o_w': jax.random.normal(ks[3], (H, NH * VD), jnp.float32) * sd(NH * VD), 'gate_w': jax.random.normal(ks[4], (E, H), jnp.float32) * sd(H), 'w1': jax.random.normal(ks[5], (E, 2 * I, H), jnp.float32) * sd(H), 'w2': jax.random.normal(ks[6], (E, H, I), jnp.float32) * sd(I), 'sh_gu_w': jax.random.normal(ks[7], (2 * SHI, H), jnp.float32) * sd(H), 'sh_down_w': jax.random.normal(ks[8], (H, SHI), jnp.float32) * sd(SHI)}
    _L1_ffn_all = _L1_ffn_setup()
    _L1_ffn_in = {k: v for k, v in _L1_ffn_all.items() if k in ('positions', 'ln1_w', 'ln2_w', 'q_w', 'kv_w', 'o_w', 'gate_w', 'w1', 'w2', 'sh_gu_w', 'sh_down_w')}
    del _L1_ffn_all
    return {'x': x, 'itok_BxS_13_99985': itok_BxS_13_99985, 'ctx_2048': ctx_2048, 'mask_BxSxS2_ff0': mask_BxSxS2_ff0, 'g_xattn': g_xattn, 'g_ffn': g_ffn, 'L0_ffn_w_gate': _L0_ffn_in['w_gate'], 'L0_ffn_w_up': _L0_ffn_in['w_up'], 'L0_ffn_w_down': _L0_ffn_in['w_down'], 'L1_xattn_wq': _L1_xattn_in['wq'], 'L1_xattn_bq': _L1_xattn_in['bq'], 'L1_xattn_wk': _L1_xattn_in['wk'], 'L1_xattn_bk': _L1_xattn_in['bk'], 'L1_xattn_wv': _L1_xattn_in['wv'], 'L1_xattn_bv': _L1_xattn_in['bv'], 'L1_xattn_wo': _L1_xattn_in['wo'], 'L1_xattn_bo': _L1_xattn_in['bo'], 'L1_ffn_positions': _L1_ffn_in['positions'], 'L1_ffn_ln1_w': _L1_ffn_in['ln1_w'], 'L1_ffn_ln2_w': _L1_ffn_in['ln2_w'], 'L1_ffn_q_w': _L1_ffn_in['q_w'], 'L1_ffn_kv_w': _L1_ffn_in['kv_w'], 'L1_ffn_o_w': _L1_ffn_in['o_w'], 'L1_ffn_gate_w': _L1_ffn_in['gate_w'], 'L1_ffn_w1': _L1_ffn_in['w1'], 'L1_ffn_w2': _L1_ffn_in['w2'], 'L1_ffn_sh_gu_w': _L1_ffn_in['sh_gu_w'], 'L1_ffn_sh_down_w': _L1_ffn_in['sh_down_w']}

def reference(x, itok_BxS_13_99985, ctx_2048, mask_BxSxS2_ff0, g_xattn, g_ffn, L0_ffn_w_gate, L0_ffn_w_up, L0_ffn_w_down, L1_xattn_wq, L1_xattn_bq, L1_xattn_wk, L1_xattn_bk, L1_xattn_wv, L1_xattn_bv, L1_xattn_wo, L1_xattn_bo, L1_ffn_positions, L1_ffn_ln1_w, L1_ffn_ln2_w, L1_ffn_q_w, L1_ffn_kv_w, L1_ffn_o_w, L1_ffn_gate_w, L1_ffn_w1, L1_ffn_w2, L1_ffn_sh_gu_w, L1_ffn_sh_down_w):
    import jax
    import jax.numpy as jnp

    def _L0_xattn_ref(hidden_states, token_ids, Wg, Wu, Wd):
        import jax, jax.numpy as jnp
        import numpy as np
        B, S, D = (4, 512, 256)
        E = 4
        F = 1024 // E
        VOCAB = 12500
        tokens_per_expert = VOCAB // E
        tid = jnp.clip(token_ids, 0, VOCAB - 1)
        expert_ids = jnp.minimum(tid // tokens_per_expert, E - 1)
        out = jnp.zeros_like(hidden_states)
        for e in range(E):
            g = jax.nn.silu(jnp.einsum('bsd,fd->bsf', hidden_states, Wg[e]))
            u = jnp.einsum('bsd,fd->bsf', hidden_states, Wu[e])
            y = jnp.einsum('bsf,df->bsd', g * u, Wd[e])
            out = jnp.where((expert_ids == e)[..., None], y, out)
        return out

    def _L0_ffn_ref(x, w_gate, w_up, w_down):
        import jax, jax.numpy as jnp
        import numpy as np
        EPS = 1e-05

        def _quant_weight(w):
            scale = jnp.mean(jnp.abs(w)) + EPS
            wq = jnp.clip(jnp.round(w / scale), -1.0, 1.0)
            return (wq, scale)

        def _quant_act(x):
            s = jnp.max(jnp.abs(x), axis=-1, keepdims=True) / 127.0 + EPS
            xq = jnp.clip(jnp.round(x / s), -128.0, 127.0)
            return (xq, s)

        def _qlinear(x, w):
            wq, ws = _quant_weight(w)
            xq, xs = _quant_act(x)
            y = jnp.einsum('bsi,oi->bso', xq, wq)
            return y * xs * ws
        gate = jax.nn.silu(_qlinear(x, w_gate))
        up = _qlinear(x, w_up)
        return _qlinear(gate * up, w_down)

    def _L1_xattn_ref(x, cond, mask, wq, bq, wk, bk, wv, bv, wo, bo):
        import jax, jax.numpy as jnp
        import numpy as np
        NUM_HEADS = 16
        EPS = 1e-08

        def _dyn_quant(x):
            s = jnp.maximum(jnp.max(jnp.abs(x), axis=-1, keepdims=True) / 127.0, EPS)
            q = jnp.clip(jnp.round(x / s), -127.0, 127.0)
            return (q, s)

        def _quant_weight(w):
            s = jnp.maximum(jnp.max(jnp.abs(w), axis=1, keepdims=True) / 127.0, EPS)
            q = jnp.clip(jnp.round(w / s), -127.0, 127.0)
            return (q, s)

        def _w8a8_linear(x, w, b):
            qx, sx = _dyn_quant(x)
            qw, sw = _quant_weight(w)
            y = jnp.einsum('bnc,oc->bno', qx, qw) * (sx * sw[:, 0])
            return y + b
        B, N, C = x.shape
        L = cond.shape[1]
        H = NUM_HEADS
        D = C // H
        inv_sqrt_d = np.float32(1.0 / np.sqrt(D))
        q = _w8a8_linear(x, wq, bq).reshape(B, N, H, D).transpose(0, 2, 1, 3)
        k = (cond @ wk.T + bk).reshape(B, L, H, D).transpose(0, 2, 1, 3)
        v = (cond @ wv.T + bv).reshape(B, L, H, D).transpose(0, 2, 1, 3)
        scores = jnp.einsum('bhnd,bhld->bhnl', q, k) * inv_sqrt_d + mask[:, None]
        attn = jax.nn.softmax(scores, axis=-1)
        o = jnp.einsum('bhnl,bhld->bhnd', attn, v)
        o = o.transpose(0, 2, 1, 3).reshape(B, N, C)
        return _w8a8_linear(o, wo, bo)

    def _L1_ffn_ref(hidden_states, positions, ln1_w, ln2_w, q_w, kv_w, o_w, gate_w, w1, w2, sh_gu_w, sh_down_w):
        import jax, jax.numpy as jnp
        import numpy as np
        H = 256
        NH = 16
        NOPE = 128
        ROPE = 64
        VD = 128
        QHD = NOPE + ROPE
        E = 16
        I = 176
        TOPK = 4
        NSH = 2
        SHI = I * NSH
        EPS = 1e-06
        B, S = (2, 128)

        def rmsnorm(x, w):
            return x * jax.lax.rsqrt(jnp.mean(x * x, axis=-1, keepdims=True) + EPS) * w
        b, s, h = hidden_states.shape
        x = rmsnorm(hidden_states, ln1_w)
        q = jnp.einsum('bsh,dh->bsd', x, q_w).reshape(b, s, NH, QHD)[..., :NOPE]
        kv = jnp.einsum('bsh,dh->bsd', x, kv_w)
        k = kv[..., :NH * NOPE].reshape(b, s, NH, NOPE)
        v = kv[..., NH * NOPE:NH * (NOPE + VD)].reshape(b, s, NH, VD)
        scale = QHD ** (-0.5)
        scores = jnp.einsum('bqnd,bknd->bnqk', q, k) * scale
        causal = jnp.tril(jnp.ones((s, s), bool))
        scores = jnp.where(causal, scores, -1000000000.0)
        p = jax.nn.softmax(scores, axis=-1)
        attn = jnp.einsum('bnqk,bknd->bqnd', p, v).reshape(b, s, NH * VD)
        attn_out = jnp.einsum('bsd,hd->bsh', attn, o_w)
        hid = hidden_states + attn_out
        x2 = rmsnorm(hid, ln2_w).reshape(-1, h)
        logits = x2 @ gate_w.T
        probs = jax.nn.softmax(logits, axis=-1)
        top_w, top_i = jax.lax.top_k(probs, TOPK)
        top_w = top_w / jnp.sum(top_w, axis=-1, keepdims=True)
        wfull = jnp.sum(jax.nn.one_hot(top_i, E, dtype=x2.dtype) * top_w[..., None], axis=1)
        gu = jnp.einsum('th,eih->tei', x2, w1)
        g, u = (gu[..., :I], gu[..., I:])
        act = jax.nn.silu(g) * u
        down = jnp.einsum('tei,ehi->teh', act, w2)
        routed = jnp.einsum('te,teh->th', wfull, down)
        sgu = x2 @ sh_gu_w.T
        sg, su = (sgu[..., :SHI], sgu[..., SHI:])
        shared = jax.nn.silu(sg) * su @ sh_down_w.T
        return hid + (routed + shared).reshape(b, s, h)
    x = x + jnp.tanh(g_xattn[0]) * _L0_xattn_ref(_layernorm(x, axis=-1), itok_BxS_13_99985, ctx_2048, ctx_2048, ctx_2048)
    x = x + jnp.tanh(g_ffn[0]) * _L0_ffn_ref(_layernorm(x, axis=-1), L0_ffn_w_gate, L0_ffn_w_up, L0_ffn_w_down)
    x = x + jnp.tanh(g_xattn[1]) * _L1_xattn_ref(_layernorm(x, axis=-1), ctx_2048, mask_BxSxS2_ff0, L1_xattn_wq, L1_xattn_bq, L1_xattn_wk, L1_xattn_bk, L1_xattn_wv, L1_xattn_bv, L1_xattn_wo, L1_xattn_bo)
    x = x + jnp.tanh(g_ffn[1]) * _L1_ffn_ref(_layernorm(x, axis=-1), L1_ffn_positions, L1_ffn_ln1_w, L1_ffn_ln2_w, L1_ffn_q_w, L1_ffn_kv_w, L1_ffn_o_w, L1_ffn_gate_w, L1_ffn_w1, L1_ffn_w2, L1_ffn_sh_gu_w, L1_ffn_sh_down_w)
    return x

_drawn_inputs = setup_inputs


def setup_inputs(seed=0):
    import zlib

    import numpy as np

    out = dict(_drawn_inputs(seed))
    spreads = {'g_ffn': (-1.0, 0.2),
     'L1_xattn_bq': (0.0, 2.0),
     'L1_xattn_bk': (0.0, 2.0),
     'L1_xattn_bv': (0.0, 0.1),
     'L1_xattn_bo': (0.0, 0.1),
     'L1_ffn_ln1_w': (1.0, 0.2),
     'L1_ffn_ln2_w': (1.0, 0.2)}
    factors = {'L1_xattn_wq': 64.0, 'L1_xattn_wk': 64.0, 'L1_xattn_wv': 4.832}
    for name, (base, spread) in spreads.items():
        noise = np.random.default_rng([zlib.crc32(name.encode()), seed]).standard_normal(out[name].shape)
        drawn = base * np.exp(spread * noise) if base else spread * noise
        out[name] = jnp.asarray(drawn.astype(out[name].dtype))
    for name, factor in factors.items():
        out[name] = (out[name] * factor).astype(out[name].dtype)
    return out
```

```python
import concourse.bass as bass
from concourse import mybir
from contextlib import ExitStack

P = 128
B, S, D = 4, 256, 256
T = B * S // P
TB = S // P
C = D // P
E0 = 4
VOCAB = 12500
F0 = 1024
FC = F0 // P
XH, XD = 16, 16
XG = 4
XA = XG * XD + XG
NH, HD, QHD = 16, 128, 192
E1, TOPK, I1 = 16, 4, 176
SHI = 2 * I1
ROUTED = E1 * I1 // P
CH = -(-(E1 * I1 + SHI) // P)
LAST = E1 * I1 + SHI - (CH - 1) * P
WCH = 4 * P + D
MAGIC = 12582912.0
NEG = -3.0e38
SCALE = float(QHD) ** -0.5

def flamingo(nc, x, itok, ctxT, mask, gates, w_gate, w_up, w_down, wq, wkT, wvT, wo, bq, bkc, bv, bo,
             ln1c, ln2c, qwT, kwT, vwT, owT, gate_wT, w_moe, ident_d, tri_d, headmask_d, sel_d, out):
    f32, bf16 = mybir.dt.float32, mybir.dt.bfloat16
    ALU, ACT, AX = mybir.AluOpType, mybir.ActivationFunctionType, mybir.AxisListType
    ctx = ExitStack()
    with ctx:
        def sb(name, shape, dt=f32):
            return ctx.enter_context(nc.sbuf_tensor(name, shape, dt))

        def sem(name):
            return ctx.enter_context(nc.semaphore(name))

        xs = sb("xs", [P, T, D])
        ctxT_sb = sb("ctxT_sb", [P, C, B * S])
        hid = sb("hid", [P, T, D])
        armK = sb("armK", [P, 16384])
        armR = sb("armR", [P, 20992])
        armW = sb("armW", [P, 3072])
        keysm = armK[:, :].rearrange("p (b c h s) -> p b c h s", b=B, c=C, h=8)
        qw = armK[:, 0:4096].rearrange("p (c n) -> p c n", c=C)
        kw = armK[:, 4096:8192].rearrange("p (c n) -> p c n", c=C)
        vw = armK[:, 8192:12288].rearrange("p (c n) -> p c n", c=C)
        ow = armK[:, 12288:16384].rearrange("p (h n) -> p h n", h=NH)
        sel = armK[0:3 * E1, 0:ROUTED * P // 2].bitcast(bf16)
        wTb = armK[0:3 * E1, 2048:2048 + T * P // 2].bitcast(bf16)
        wraw = armR[:, 0:6144].rearrange("p (k n) -> p k n", k=3)
        zbuf = armR[:, 6144:6656].rearrange("p (r n) -> p r n", r=2)
        thA = armR[:, 6656:7168].rearrange("p (r n) -> p r n", r=2)
        ubuf = armR[:, 7168:7680].rearrange("p (r n) -> p r n", r=2)
        gubuf = armR[:, 7680:8192].rearrange("p (r n) -> p r n", r=2)
        thB = armR[:, 0:1024]
        aB = armR[:, 1024:2048]
        pB = armR[:, 2048:3072]
        rB = armR[:, 3072:4096]
        qB = armR[:, 4096:4608].bitcast(bf16)
        qTB = armR[:, 4608:5120].bitcast(bf16).rearrange("p (c n) -> p c n", c=FC)
        scores = armR[:, 0:8192].rearrange("p (r h s) -> p r h s", r=2, h=XH)
        vaug = armR[:, 8192:8192 + T * XH * XA].rearrange("p (t h a) -> p t h a", t=T, h=XH)
        probT = armR[:, 16896:20992].rearrange("p (h l n) -> p h l n", h=XH, l=TB)
        kraw = armR[:, 16896:18944].rearrange("p (c n) -> p c n", c=C)
        xw = armR[:, 18944:20992].rearrange("p (k c n) -> p k c n", k=4, c=C)
        vals = armR[:, 0:8192].rearrange("p (r l n) -> p r l n", r=2, l=TB)
        attnT = armR[:, 8192:12288].rearrange("p (h n) -> p h n", h=NH)
        FIRST = 11
        place = [12288 + WCH * c for c in range(FIRST)] + [WCH * c for c in range(CH - FIRST)]
        gub = armW[:, 0:2048].bitcast(bf16).rearrange("p (k c n) -> p k c n", k=2, c=C)
        dnb = armW[:, 2048:3072].bitcast(bf16).rearrange("p (c n) -> p c n", c=FC)
        qk = armW[:, 0:1024].rearrange("p (r n) -> p r n", r=2)
        probD = armW[:, 1024:1792].rearrange("p (r n) -> p r n", r=2)
        probDT = armW[:, 1792:2560].rearrange("p (r n) -> p r n", r=2)
        thE = armW[:, 0:1024].rearrange("p (r n) -> p r n", r=2)
        aE = armW[:, 1024:2048].rearrange("p (r n) -> p r n", r=2)
        actE = armW[:, 2048:3072].rearrange("p (r n) -> p r n", r=2)

        ident = sb("ident", [P, P])
        identb = sb("identb", [P, P], bf16)
        ones = sb("ones", [P, P])
        tri = sb("tri", [P, P])
        headmask = sb("headmask", [P, 8])
        maskt = sb("maskt", [P, 2, S])
        hbuf = sb("hbuf", [P, 2, D])
        hT = sb("hT", [P, 2, C, P])
        qb = sb("qb", [P, 2, D], bf16)
        qTb = sb("qTb", [P, 2, C, P], bf16)
        bqb, bvb, bob = sb("bqb", [P, D]), sb("bvb", [P, D]), sb("bob", [P, D])
        swb = sb("swb", [P, 4, P])
        xwb = sb("xwb", [P, 2, C, D], bf16)
        xwT = sb("xwT", [P, 2, C, D], bf16)
        gw = sb("gw", [P, C, E1])
        tok_i = sb("tok_i", [P, T], mybir.dt.int32)
        tok = sb("tok", [P, T])
        ge = sb("ge", [P, 3, T])
        em = sb("em", [P, E0, T])
        ey = sb("ey", [P, E0, T])
        gcol, tg = sb("gcol", [P, 4]), sb("tg", [P, 4])
        bk_sb, ln1_sb, ln2_sb = sb("bk_sb", [P, C]), sb("ln1_sb", [P, C]), sb("ln2_sb", [P, C])
        JOBS = 48
        st, mv = sb("st", [P, 6]), sb("mv", [P, JOBS, 2])
        powin, rstd, nhalf = sb("powin", [P, JOBS]), sb("rstd", [P, JOBS]), sb("nhalf", [P, 1])
        wsum, wsc, thr = sb("wsum", [P, 3]), sb("wsc", [P, 3]), sb("thr", [P, 6])
        cb = sb("cb", [P, T, 8])
        xwc = sb("xwc", [P, 4, 4])
        cc = sb("cc", [P, T, 8])
        mxC, nmC = sb("mxC", [P, 2, XH]), sb("nmC", [P, 2, XH])
        rdC = sb("rdC", [P, XH])
        mxD, nmD, rsD, riD = (sb(n, [P, 2, 2]) for n in ("mxD", "nmD", "rsD", "riD"))
        lg = sb("lg", [P, 2, 8, E1])
        lw = sb("lw", [P, 2, 3 * E1], bf16)

        obuf = armW[:, 0:256]
        oq = armW[:, 256:384].bitcast(bf16)
        oT_sb = armW[0:XA, 512:1024].rearrange("p (g n) -> p g n", g=XG)
        guT = sb("guT", [P, C, P])
        xqT_B = qTb
        oqT = armW[:, 384:512].bitcast(bf16).rearrange("p (c n) -> p c n", c=C)
        qT_sb = hT
        wqo = hid[:, 0:4, :].rearrange("p (k c) n -> p k c n", k=2)
        diag = hid[:, 4:6, :].rearrange("p a (i n) -> p (a i) n", i=2)

        bank = [ctx.enter_context(nc.psum_tensor(f"bank{i}", [P, 512], f32)) for i in range(8)]

        def halfs(i):
            return bank[i][:, :].bitcast(bf16)

        names = ("x0 x1 tok gates ctx wkv consts raw biases wqo cols tri ln gw sel qw kw vw ow").split()
        ld = {n: sem("ld_" + n) for n in names}
        ld_mask = [sem(f"ld_mask{i}") for i in range(2)]
        ld_moe = [sem(f"ld_moe{i}") for i in range(3)]
        st_out = sem("st_out")
        vec_step, pow_in, pow_out = sem("vec_step"), sem("pow_in"), sem("pow_out")
        (identb_ready, tg_ready, ones_ready, vaug_zero, kproj, kraw_ready, keysm_ready, vproj, v_ready, wabs_ready,
         wsum_ready, ternary_ready, xwb_ready, xwT_psum, xwT_ready, diag_ready, swb_psum, swb_ready) = (
            sem(n) for n in ("identb_ready tg_ready ones_ready vaug_zero kproj kraw_ready keysm_ready vproj v_ready "
                             "wabs_ready wsum_ready ternary_ready xwb_ready xwT_psum xwT_ready diag_ready swb_psum "
                             "swb_ready").split())
        a_h, a_hTp, a_hTs, a_z, a_zsel, a_th, a_gu, a_guTp, a_guTs, a_y, a_x1 = (
            sem("a_" + n) for n in "h hTp hTs z zsel th gu guTp guTs y x1".split())
        b_xq, b_xqTp, b_xqTs, b_g, b_u, b_th, b_guse, b_p, b_q, b_qTp, b_qTs, b_d, b_x2 = (
            sem("b_" + n) for n in "xq xqTp xqTs g u th guse p q qTp qTs d x2".split())
        (c_xq, c_xqTp, c_xqTs, c_qp, c_q, c_qTp, c_qTs, c_s, c_sm, c_nm, c_p, c_pTp, c_pTs, c_pv, c_pvs, c_oT, c_o,
         c_oqTp, c_oqTs, c_op, c_x3) = (
            sem("c_" + n) for n in "xq xqTp xqTs qp q qTp qTs s sm nm p pTp pTs pv pvs oT o oqTp oqTs op x3".split())
        (d_h, d_xn, d_vo, d_vofree, d_qkp, d_qs, d_s, d_sm, d_nm, d_e, d_p, d_pTp, d_pTs, d_a, d_as) = (
            sem("d_" + n) for n in "h xn vo vofree qkp qs s sm nm e p pTp pTs a as".split())
        (e_x2, e_x2Tp, e_x2Ts, e_lg, e_lgs, e_ex, e_w, e_wTp, e_wTs, e_gu, e_wb, e_th, e_gud, e_act, e_dn, e_acc, e_yT,
         e_yt, e_out) = (
            sem("e_" + n) for n in "x2 x2Tp x2Ts lg lgs ex w wTp wTs gu wb th gud act dn acc yT yt out".split())

        NV = TB * (NH * HD // 512)
        VO = {}

        def vo_plan():
            n, order = 0, []
            for i in range(B * NH + 4):
                b, h = divmod(i, NH)
                if i == 0:
                    order += [("T", 0, u) for u in range(TB)] + [("V", 0, u) for u in range(NV)]
                if h == 12 and b + 1 < B:
                    order += [("T", b + 1, u) for u in range(TB)] + [("V", b + 1, u) for u in range(NV)]
                if h == 3 and b >= 1:
                    order += [("O", b - 1, u) for u in range(TB)]
            for n, key in enumerate(order):
                VO[key] = n
            return order

        VO_ORDER = vo_plan()
        VO_END = len(VO_ORDER)

        block = ctx.enter_context(nc.Block())

        @block.sync
        def _(sp):
            sp.dma_start(xs[:, 0:2, :], x[:, 0:2, :]).then_inc(ld["x0"], 16)
            sp.dma_start(ctxT_sb[:, :, :], ctxT).then_inc(ld["ctx"], 16)
            sp.dma_start(xw[:, 0:2, :, :], wkT).then_inc(ld["wkv"], 16)
            sp.dma_start(xw[:, 2, :, :], wvT).then_inc(ld["wkv"], 16)
            sp.dma_start(xs[:, 2:T, :], x[:, 2:T, :]).then_inc(ld["x1"], 16)
            for k, w in enumerate((w_gate, w_up, w_down)):
                sp.dma_start(wraw[:, k, :], w).then_inc(ld["raw"], 16)
            sp.dma_start(tri[:, :], tri_d).then_inc(ld["tri"], 16)
            for i in range(2):
                sp.dma_start(maskt[:, i, :], mask[i]).then_inc(ld_mask[i], 16)
            for t in range(2, T):
                sp.wait_ge(c_sm, XH * (t - 1))
                sp.dma_start(maskt[:, t % 2, :], mask[t]).then_inc(ld_mask[t % 2], 16)
                if t % 2 == 1:
                    b = t // 2 - 1
                    sp.wait_ge(c_s, T * (2 * b + 2))
                    dst, src, n = ((qw, qwT, "qw"), (kw, kwT, "kw"), (vw, vwT, "vw"))[b]
                    sp.dma_start(dst, src).then_inc(ld[n], 16)
            sp.wait_ge(c_s, T * T)
            sp.dma_start(ow, owT).then_inc(ld["ow"], 16)
            sp.wait_ge(c_pv, XG * T)
            half = FIRST // 2
            for lo, hi, s in ((0, half, 0), (half, FIRST, 1)):
                sp.dma_start(armR[:, place[lo]:place[lo] + WCH * (hi - lo)],
                             w_moe[:, WCH * lo:WCH * hi]).then_inc(ld_moe[s], 16)
            sp.wait_ge(d_qkp, B * NH)
            sp.dma_start(sel, sel_d).then_inc(ld["sel"], 16)
            sp.wait_ge(d_vo, VO_END)
            sp.dma_start(armR[:, 0:WCH * (CH - FIRST)], w_moe[:, WCH * FIRST:WCH * CH]).then_inc(ld_moe[2], 16)
            for t in range(T):
                sp.wait_ge(e_out, t + 1)
                sp.dma_start(out[:, t, :], xs[:, t, :]).then_inc(st_out, 16)
            sp.wait_ge(st_out, 16 * T)

        @block.gpsimd
        def _(pool):
            nc.gpsimd.memset(nhalf[:, :], -0.5).then_inc(ones_ready, 1)
            nc.gpsimd.memset(ones[:, :], 1.0).then_inc(ones_ready, 1)
            pool.wait_ge(ones_ready, 2)
            for k in range(JOBS):
                pool.wait_ge(pow_in, k + 1)
                nc.gpsimd.tensor_tensor(rstd[:, k:k + 1], powin[:, k:k + 1], nhalf[:, :], ALU.pow).then_inc(pow_out, 1)
                if k == 1:
                    nc.gpsimd.memset(vaug[:, :, :, :], 0.0).then_inc(vaug_zero, 1)
                    pool.wait_ge(vaug_zero, 1)
                    for j in range(XG):
                        v = vaug.rearrange("p t (g j) a -> p t g j a", j=XG)[:, :, :, j, XG * XD + j:XG * XD + j + 1]
                        nc.gpsimd.memset(v, 1.0).then_inc(vaug_zero, 1)
                if 2 <= k < 2 + B * C:
                    b, c = divmod(k - 2, C)
                    pool.wait_ge(kraw_ready, 2 * C)
                    if k == 2:
                        pool.wait_ge(ld["consts"], 32)
                    nc.gpsimd.tensor_tensor(
                        keysm[:, b, c, :, :], kraw[:, c, None, S * b:S * b + S].broadcast_to([P, 8, S]),
                        headmask[:, :, None].broadcast_to([P, 8, S]), ALU.mult).then_inc(keysm_ready, 1)

        @block.vector
        def _(dve):
            steps = [0]

            def run(ins):
                steps[0] += 1
                ins.then_inc(vec_step, 1)

            def settle():
                dve.wait_ge(vec_step, steps[0])

            def step(ins):
                run(ins)
                settle()

            V = nc.vector

            def ln_stats(job, src, eps):
                step(V.bn_stats(st[:, :], src))
                step(V.bn_aggr(mv[:, job, :], st[:, :]))
                V.tensor_scalar(powin[:, job:job + 1], mv[:, job, 1:2], eps, None, ALU.add).then_inc(pow_in, 1)

            def ln_norm(job, src, dst):
                dve.wait_ge(pow_out, job + 1)
                return V.tensor_scalar(dst, src, mv[:, job, 0:1], rstd[:, job:job + 1], ALU.subtract, ALU.mult)

            dve.wait_ge(ld["consts"], 32)
            V.tensor_copy(identb[:, :], ident[:, :]).then_inc(identb_ready, 1)
            dve.wait_ge(ld["x0"], 16)
            ln_stats(0, xs[:, 0, :], 1e-5)
            ln_stats(1, xs[:, 1, :], 1e-5)
            dve.wait_ge(ld["tok"], 16)
            step(V.tensor_copy(tok[:, :], tok_i[:, :]))
            for e in range(1, E0):
                run(V.tensor_scalar(ge[:, e - 1, :], tok[:, :], float(e * (VOCAB // E0)), None, ALU.is_ge))
            settle()
            run(V.tensor_scalar(em[:, 0, :], ge[:, 0, :], -1.0, 1.0, ALU.mult, ALU.add))
            run(V.tensor_tensor(em[:, 1, :], ge[:, 0, :], ge[:, 1, :], ALU.subtract))
            run(V.tensor_tensor(em[:, 2, :], ge[:, 1, :], ge[:, 2, :], ALU.subtract))
            run(V.tensor_copy(em[:, 3, :], ge[:, 2, :]))
            settle()
            dve.wait_ge(tg_ready, 1)
            step(V.tensor_scalar(ey[:, :, :], em[:, :, :], tg[:, 0:1], 0.5, ALU.mult, ALU.mult))
            ln_norm(0, xs[:, 0, :], hbuf[:, 0, :]).then_inc(a_h, 1)
            dve.wait_ge(vaug_zero, 1 + XG)
            dve.wait_ge(ld["biases"], 48)
            for t in range(T):
                dve.wait_ge(vproj, t + 1)
                p, j0 = 6 + t % 2, t
                base = vaug[:, t, :, :].rearrange("p h a -> p (h a)")
                for j in range(XG):
                    o = vaug[:, t, :, :].rearrange("p (g j) a -> p g j a", j=XG)[:, :, j, XD * j:XD * j + XD]
                    i0 = bank[p][:, 0:D].rearrange("p (g j d) -> p g j d", j=XG, d=XD)[:, :, j, :]
                    i1 = bvb[:, :].rearrange("p (g j d) -> p g j d", j=XG, d=XD)[:, :, j, :]
                    V.tensor_tensor(o, i0, i1, ALU.add).then_inc(v_ready, 1)

            def weights_piece(n):
                if n == 1:
                    dve.wait_ge(ld["raw"], 48)
                    for k in range(3):
                        V.tensor_reduce(wsum[:, k:k + 1], wraw[:, k, :], AX.X, ALU.add,
                                        apply_absolute_value=True).then_inc(wabs_ready, 1)
                if n == 3:
                    dve.wait_ge(wsum_ready, 1)
                    step(V.tensor_scalar(wsc[:, :], bank[6][:, 0:3], 1.0 / (F0 * D), 1e-5, ALU.mult, ALU.add))
                    run(V.tensor_scalar(thr[:, 0:3], wsc[:, :], 0.5, None, ALU.mult))
                    run(V.tensor_scalar(thr[:, 3:6], wsc[:, :], -0.5, None, ALU.mult))
                    settle()
                if 3 <= n <= 5:
                    k = n - 3
                    dst = (gub[:, 0, :, :], gub[:, 1, :, :], dnb[:, :, :])[k]
                    src = wraw[:, k, :]
                    dstf = dst.rearrange("p c n -> p (c n)")
                    step(V.tensor_scalar(dstf, src, thr[:, 3 + k:4 + k], None, ALU.is_lt))
                    V.scalar_tensor_tensor(dstf, src, thr[:, k:k + 1], dstf, ALU.is_gt,
                                           ALU.subtract).then_inc(ternary_ready, 1)
                if n == 6:
                    dve.wait_ge(ld["wqo"], 32)
                    for k in range(2):
                        for c in range(C):
                            i = 2 * k + c
                            w = wqo[:, k, c, :]
                            step(V.tensor_reduce(xwc[:, i, 0:1], w, AX.X, ALU.max, apply_absolute_value=True))
                            step(V.tensor_scalar(xwc[:, i, 1:2], xwc[:, i, 0:1], 1.0 / 127, 1e-8, ALU.mult, ALU.max))
                            step(V.reciprocal(xwc[:, i, 2:3], xwc[:, i, 1:2]))
                            step(V.tensor_scalar(w, w, xwc[:, i, 2:3], MAGIC, ALU.mult, ALU.add))
                            V.tensor_scalar(xwb[:, k, c, :], w, MAGIC, None, ALU.subtract).then_inc(xwb_ready, 1)
                            V.tensor_scalar(diag[:, i, :], ident[:, :], xwc[:, i, 1:2], None,
                                            ALU.mult).then_inc(diag_ready, 1)
                if n == 7:
                    dve.wait_ge(swb_psum, 1)
                    V.tensor_scalar(swb[:, 0:2, :], bank[6][:, 0:256], 0.25, None, ALU.mult).then_inc(swb_ready, 1)
                    V.tensor_copy(swb[:, 2:4, :], bank[6][:, 256:512]).then_inc(swb_ready, 1)
                    V.tensor_scalar(bqb[:, :], bqb[:, :], 0.25, None, ALU.mult).then_inc(swb_ready, 1)

            def zsel(t):
                dve.wait_ge(a_z, 2 * t + 2)
                z = zbuf[:, t % 2, :]
                step(V.tensor_scalar(z, bank[0][:, 0:D], em[:, 0, t:t + 1], None, ALU.mult))
                for e in range(1, E0):
                    ins = V.scalar_tensor_tensor(z, bank[e // 2][:, D * (e % 2):D * (e % 2) + D], em[:, e, t:t + 1],
                                                 z, ALU.mult, ALU.add)
                    step(ins) if e < E0 - 1 else ins.then_inc(a_zsel, 1)

            def x1(t):
                dve.wait_ge(a_y, t + 1)
                for e in range(E0):
                    ins = V.scalar_tensor_tensor(xs[:, t, :], bank[2 + e // 2][:, D * (e % 2):D * (e % 2) + D],
                                                 ey[:, e, t:t + 1], xs[:, t, :], ALU.mult, ALU.add)
                    step(ins) if e < E0 - 1 else ins.then_inc(a_x1, 1)

            dve.wait_ge(ld["x1"], 16)
            for t in range(T):
                if t + 1 < T:
                    if t >= 1:
                        dve.wait_ge(a_hTp, t)
                    ln_norm(t + 1, xs[:, t + 1, :], hbuf[:, (t + 1) % 2, :]).then_inc(a_h, 1)
                zsel(t)
                if t + 2 < T:
                    ln_stats(t + 2, xs[:, t + 2, :], 1e-5)
                dve.wait_ge(a_th, t + 1)
                step(V.scalar_tensor_tensor(ubuf[:, t % 2, :], thA[:, t % 2, :], 1.0, zbuf[:, t % 2, :],
                                            ALU.add, ALU.mult))
                if t >= 2:
                    dve.wait_ge(a_guTp, t - 1)
                V.tensor_tensor(gubuf[:, t % 2, :], ubuf[:, t % 2, :], zbuf[:, t % 2, :], ALU.mult).then_inc(a_gu, 1)
                if t >= 1:
                    x1(t - 1)
                weights_piece(t)
            x1(T - 1)

            def quant_scale(h, cols, eps_op, eps):
                step(V.tensor_reduce(cols[:, 0:1], h, AX.X, ALU.max, apply_absolute_value=True))
                step(V.tensor_scalar(cols[:, 1:2], cols[:, 0:1], 1.0 / 127, eps, ALU.mult, eps_op))
                step(V.reciprocal(cols[:, 2:3], cols[:, 1:2]))

            def quant_round(h, cols, dst):
                step(V.tensor_scalar(h, h, cols[:, 2:3], MAGIC, ALU.mult, ALU.add))
                return V.tensor_scalar(dst, h, MAGIC, None, ALU.subtract)

            def b_front(t):
                job = 8 + t
                h = hbuf[:, t % 2, :]
                if t == 0:
                    dve.wait_ge(a_hTp, T)
                step(ln_norm(job, xs[:, t, :], h))
                if t >= 2:
                    dve.wait_ge(b_xqTp, t - 1)
                quant_scale(h, cb[:, t, :], ALU.add, 1e-5)
                run(V.tensor_scalar(cb[:, t, 3:4], wsc[:, 0:1], cb[:, t, 1:2], 0.5, ALU.mult, ALU.mult))
                run(V.tensor_scalar(cb[:, t, 4:5], wsc[:, 1:2], cb[:, t, 1:2], None, ALU.mult))
                quant_round(h, cb[:, t, :], qb[:, t % 2, :]).then_inc(b_xq, 1)
                step(V.tensor_tensor(cb[:, t, 5:6], cb[:, t, 3:4], cb[:, t, 4:5], ALU.mult))

            def b_back(t):
                dve.wait_ge(b_d, t + 1)
                V.scalar_tensor_tensor(xs[:, t, :], bank[6][:, 0:D], cb[:, t, 0:1], xs[:, t, :],
                                       ALU.mult, ALU.add).then_inc(b_x2, 1)

            dve.wait_ge(a_x1, T)
            dve.wait_ge(ternary_ready, 3)
            ln_stats(8, xs[:, 0, :], 1e-5)
            ln_stats(9, xs[:, 1, :], 1e-5)
            b_front(0)
            for t in range(T):
                if t + 2 < T:
                    ln_stats(8 + t + 2, xs[:, t + 2, :], 1e-5)
                if t + 1 < T:
                    b_front(t + 1)
                dve.wait_ge(b_th, t + 1)
                step(V.scalar_tensor_tensor(aB[:, 0:512], thB[:, 0:512], 1.0, bank[0][:, :], ALU.add, ALU.mult))
                V.scalar_tensor_tensor(aB[:, 512:1024], thB[:, 512:1024], 1.0, bank[1][:, :],
                                       ALU.add, ALU.mult).then_inc(b_guse, 1)
                dve.wait_ge(b_guse, t + 1)
                dve.wait_ge(b_u, t + 1)
                step(V.tensor_tensor(pB[:, 0:512], aB[:, 0:512], bank[2][:, :], ALU.mult))
                V.tensor_tensor(pB[:, 512:1024], aB[:, 512:1024], bank[3][:, :], ALU.mult).then_inc(b_p, 1)
                dve.wait_ge(b_p, t + 1)
                col = cb[:, t, :]
                step(V.tensor_reduce(col[:, 6:7], pB, AX.X, ALU.max, apply_absolute_value=True))
                step(V.tensor_scalar(col[:, 6:7], col[:, 6:7], col[:, 5:6], 1.0 / 127, ALU.mult, ALU.mult))
                step(V.tensor_scalar(col[:, 6:7], col[:, 6:7], 1e-5, None, ALU.add))
                step(V.reciprocal(col[:, 7:8], col[:, 6:7]))
                run(V.tensor_scalar(col[:, 7:8], col[:, 7:8], col[:, 5:6], None, ALU.mult))
                step(V.tensor_scalar(col[:, 0:1], col[:, 6:7], wsc[:, 2:3], tg[:, 2:3], ALU.mult, ALU.mult))
                step(V.tensor_scalar(rB, pB, col[:, 7:8], MAGIC, ALU.mult, ALU.add))
                if t >= 1:
                    dve.wait_ge(b_qTp, t)
                V.tensor_scalar(qB, rB, MAGIC, None, ALU.subtract).then_inc(b_q, 1)
                if t >= 1:
                    b_back(t - 1)
            b_back(T - 1)

            def c_front(t):
                h = hbuf[:, t % 2, :]
                step(ln_norm(16 + t, xs[:, t, :], h))
                if t == 0:
                    dve.wait_ge(b_xqTp, T)
                else:
                    dve.wait_ge(c_xqTp, t)
                quant_scale(h, cc[:, t, :], ALU.max, 1e-8)
                quant_round(h, cc[:, t, :], qb[:, t % 2, :]).then_inc(c_xq, 1)

            def c_query(t):
                dve.wait_ge(c_qp, t + 1)
                h = hbuf[:, t % 2, :]
                dve.wait_ge(c_xq, t + 1)
                step(V.scalar_tensor_tensor(h, bank[5][:, 128:128 + D], cc[:, t, 1:2],
                                            swb[:, 0:2, :].rearrange("p a n -> p (a n)"), ALU.mult, ALU.mult))
                V.tensor_tensor(h, h, bqb[:, :], ALU.add).then_inc(c_q, 1)

            def c_scores(t):
                dve.wait_ge(ld_mask[t % 2], 16 * (t // 2 + 1))
                if t >= 2:
                    dve.wait_ge(c_pTp, T * (t - 1))
                for k in range(T):
                    dve.wait_ge(c_s, T * t + k + 1)
                    for i in range(2):
                        h = 2 * k + i
                        V.tensor_tensor_reduce(
                            out=scores[:, t % 2, h, :], in0=bank[k % 2][:, S * i:S * i + S], in1=maskt[:, t % 2, :],
                            scale=1.0, scalar=NEG, op0=ALU.add, op1=ALU.max,
                            accum_out=mxC[:, t % 2, h:h + 1]).then_inc(c_sm, 1)
                    if k % 2 == 1:
                        dve.wait_ge(c_sm, XH * t + 2 * k + 2)
                        V.tensor_scalar(nmC[:, t % 2, 2 * k - 2:2 * k + 2], mxC[:, t % 2, 2 * k - 2:2 * k + 2], -1.0,
                                        None, ALU.mult).then_inc(c_nm, 1)

            def c_out(t):
                dve.wait_ge(c_oT, t + 1)
                o4 = bank[6][:, 0:XG * XA].rearrange("p (g a) -> p g a", g=XG)
                step(V.reciprocal(rdC[:, :].rearrange("p (g j) -> p g j", g=XG), o4[:, :, XG * XD:XA]))
                ot = obuf[:, :]
                for g in range(XG):
                    run(V.tensor_tensor(ot[:, 64 * g:64 * g + 64].rearrange("p (j d) -> p j d", d=XD),
                                        o4[:, g, 0:XG * XD].rearrange("p (j d) -> p j d", d=XD),
                                        rdC[:, 4 * g:4 * g + 4, None].broadcast_to([P, XG, XD]), ALU.mult))
                settle()
                quant_scale(ot, cc[:, t, 4:8], ALU.max, 1e-8)
                quant_round(ot, cc[:, t, 4:8], oq[:, :]).then_inc(c_o, 1)

            def c_back(t):
                dve.wait_ge(c_op, t + 1)
                step(V.scalar_tensor_tensor(obuf[:, :], bank[6][:, 128:128 + D], cc[:, t, 5:6],
                                            swb[:, 2:4, :].rearrange("p a n -> p (a n)"), ALU.mult, ALU.mult))
                step(V.tensor_tensor(obuf[:, :], obuf[:, :], bob[:, :], ALU.add))
                V.scalar_tensor_tensor(xs[:, t, :], obuf[:, :], tg[:, 1:2], xs[:, t, :], ALU.mult,
                                       ALU.add).then_inc(c_x3, 1)

            dve.wait_ge(b_x2, T)
            dve.wait_ge(b_qTp, T)
            dve.wait_ge(swb_ready, 3)
            ln_stats(16, xs[:, 0, :], 1e-5)
            ln_stats(17, xs[:, 1, :], 1e-5)
            c_front(0)
            c_query(0)
            c_scores(0)
            for t in range(T):
                if t + 1 < T:
                    if t + 2 < T:
                        ln_stats(16 + t + 2, xs[:, t + 2, :], 1e-5)
                    c_front(t + 1)
                    c_query(t + 1)
                    c_scores(t + 1)
                c_out(t)
                c_back(t)

            def d_norm(b):
                for t in range(TB * b, TB * b + TB):
                    j = 24 + 2 * t
                    ln_stats(j, xs[:, t, :], 1e-5)
                    step(ln_norm(j, xs[:, t, :], hid[:, t, :]))
                    if t >= 2:
                        dve.wait_ge(d_vo, VO["T", (t - 2) // 2, t % 2] + 1)
                    step(V.tensor_tensor_reduce(out=hbuf[:, t % 2, :], in0=hid[:, t, :], in1=hid[:, t, :],
                                                scale=1.0 / D, scalar=0.0, op0=ALU.mult, op1=ALU.add,
                                                accum_out=mv[:, j + 1, 1:2]))
                    V.tensor_scalar(powin[:, j + 1:j + 2], mv[:, j + 1, 1:2], 1e-6, None,
                                    ALU.add).then_inc(pow_in, 1)
                    dve.wait_ge(pow_out, j + 2)
                    V.tensor_scalar(hbuf[:, t % 2, :], hid[:, t, :], rstd[:, j + 1:j + 2], None,
                                    ALU.mult).then_inc(d_xn, 1)

            def vo_read(key):
                kind, b, u = key
                n = VO[key]
                dve.wait_ge(d_vo, n + 1)
                p = 6 + n % 2
                if kind == "T":
                    t = TB * b + u
                    run(V.tensor_scalar(ctxT_sb[:, 0, P * t:P * t + P], bank[p][:, 0:P], ln1_sb[:, 0:1], None, ALU.mult))
                    V.tensor_scalar(ctxT_sb[:, 1, P * t:P * t + P], bank[p][:, P:2 * P], ln1_sb[:, 1:2], None,
                                    ALU.mult).then_inc(d_vofree, 1)
                elif kind == "V":
                    l, q = divmod(u, NV // TB)
                    V.tensor_copy(vals[:, b % 2, l, 512 * q:512 * q + 512], bank[p][:, :]).then_inc(d_vofree, 1)
                else:
                    t = TB * b + u
                    V.tensor_tensor(hid[:, t, :], hid[:, t, :], bank[p][:, 0:D], ALU.add).then_inc(d_vofree, 1)

            def d_softmax(g):
                r = g % 2
                dve.wait_ge(d_s, g + 1)
                if g >= 2:
                    dve.wait_ge(d_pTp, g - 1)
                V.tensor_tensor_reduce(out=probD[:, r, 0:P], in0=bank[2 + r][:, 0:P], in1=tri[:, :], scale=1.0,
                                       scalar=NEG, op0=ALU.add, op1=ALU.max,
                                       accum_out=mxD[:, r, 0:1]).then_inc(d_sm, 1)
                run(V.tensor_copy(probD[:, r, P:2 * P], bank[2 + r][:, P:2 * P]))
                run(V.tensor_reduce(mxD2[:, r, 0:1], bank[2 + r][:, P:2 * P], AX.X, ALU.max))
                V.tensor_tensor_reduce(out=probD[:, r, 2 * P:3 * P], in0=bank[2 + r][:, 2 * P:3 * P], in1=tri[:, :],
                                       scale=1.0, scalar=NEG, op0=ALU.add, op1=ALU.max,
                                       accum_out=mxD[:, r, 1:2]).then_inc(d_sm, 1)
                settle()
                dve.wait_ge(d_sm, 2 * g + 2)
                step(V.tensor_tensor(mxD[:, r, 1:2], mxD[:, r, 1:2], mxD2[:, r, 0:1], ALU.max))
                V.tensor_scalar(nmD[:, r, :], mxD[:, r, :], -SCALE, None, ALU.mult).then_inc(d_nm, 1)

            def d_normalise(g):
                r = g % 2
                dve.wait_ge(d_e, 2 * g + 2)
                step(V.reciprocal(riD[:, r, :], rsD[:, r, :]))
                run(V.tensor_scalar(probD[:, r, 0:P], probD[:, r, 0:P], riD[:, r, 0:1], None, ALU.mult))
                V.tensor_scalar(probD[:, r, P:3 * P], probD[:, r, P:3 * P], riD[:, r, 1:2], None,
                                ALU.mult).then_inc(d_p, 1)
                settle()

            def d_attn(g):
                dve.wait_ge(d_a, g + 1)
                if g % NH == 0 and g:
                    dve.wait_ge(d_vo, VO["O", g // NH - 1, TB - 1] + 1)
                V.tensor_copy(attnT[:, g % NH, :], bank[5][:, 0:S]).then_inc(d_as, 1)

            mxD2 = rdC[:, 0:4].rearrange("p (r n) -> p r n", r=2)
            dve.wait_ge(c_x3, T)
            dve.wait_ge(ld["tri"], 16)
            dve.wait_ge(ld["ln"], 32)
            d_norm(0)
            G = B * NH
            order = {}
            for i in range(G + 4):
                b, h = divmod(i, NH)
                if i == 0:
                    dve.wait_ge(c_oqTp, T)
                    for u in range(TB):
                        vo_read(("T", 0, u))
                    for u in range(NV):
                        vo_read(("V", 0, u))
                if h == 8 and b + 1 < B:
                    d_norm(b + 1)
                if h == 12 and b + 1 < B:
                    for u in range(TB):
                        vo_read(("T", b + 1, u))
                    for u in range(NV):
                        vo_read(("V", b + 1, u))
                if 1 <= i <= G:
                    d_softmax(i - 1)
                if 3 <= i <= G + 2:
                    d_attn(i - 3)
                if 1 <= i <= G:
                    d_normalise(i - 1)
                if h == 3 and b >= 1:
                    for u in range(TB):
                        vo_read(("O", b - 1, u))

            def e_norm(t):
                j = 40 + t
                if t == 0:
                    dve.wait_ge(d_vo, VO_END)
                    dve.wait_ge(d_vofree, VO_END)
                if t >= 2:
                    dve.wait_ge(e_x2Tp, t - 1)
                step(V.tensor_tensor_reduce(out=hbuf[:, t % 2, :], in0=hid[:, t, :], in1=hid[:, t, :], scale=1.0 / D,
                                            scalar=0.0, op0=ALU.mult, op1=ALU.add, accum_out=mv[:, j, 1:2]))
                V.tensor_scalar(powin[:, j:j + 1], mv[:, j, 1:2], 1e-6, None, ALU.add).then_inc(pow_in, 1)
                dve.wait_ge(pow_out, j + 1)
                V.tensor_scalar(hbuf[:, t % 2, :], hid[:, t, :], rstd[:, j:j + 1], None, ALU.mult).then_inc(e_x2, 1)

            def e_route(t):
                r = t % 2
                dve.wait_ge(e_lg, t + 1)
                L = lg[:, r, :, :]
                mx8, pr, keep, w, r1, r2 = (L[:, i, :] for i in range(6))
                step(V.tensor_reduce(mx8[:, 8:9], bank[5][:, 0:E1], AX.X, ALU.max, negate=True))
                V.tensor_scalar(pr, bank[5][:, 0:E1], mx8[:, 8:9], None, ALU.add).then_inc(e_lgs, 1)
                dve.wait_ge(e_ex, t + 1)
                step(V.tensor_reduce(mx8[:, 9:10], pr, AX.X, ALU.add))
                step(V.reciprocal(mx8[:, 10:11], mx8[:, 9:10]))
                step(V.tensor_scalar(pr, pr, mx8[:, 10:11], None, ALU.mult))
                step(V.max(mx8[:, 0:8], pr))
                step(V.memset(mx8[:, TOPK:8], 2.0))
                step(V.match_replace(out=keep, in_to_replace=mx8[:, 0:8], in_values=pr, imm_value=-1.0))
                step(V.tensor_scalar(keep, keep, 0.0, None, ALU.is_lt))
                step(V.tensor_tensor(w, keep, pr, ALU.mult))
                step(V.tensor_reduce(mx8[:, 9:10], w, AX.X, ALU.add))
                step(V.reciprocal(mx8[:, 10:11], mx8[:, 9:10]))
                step(V.tensor_scalar(w, w, mx8[:, 10:11], None, ALU.mult))
                if t >= 2:
                    dve.wait_ge(e_wTp, t - 1)
                step(V.tensor_copy(lw[:, r, 0:E1], w))
                step(V.tensor_tensor(r1, w, lw[:, r, 0:E1], ALU.subtract))
                step(V.tensor_copy(lw[:, r, E1:2 * E1], r1))
                step(V.tensor_tensor(r2, r1, lw[:, r, E1:2 * E1], ALU.subtract))
                V.tensor_copy(lw[:, r, 2 * E1:3 * E1], r2).then_inc(e_w, 1)

            dve.wait_ge(ld["gw"], 16)
            e_norm(0)
            for t in range(T):
                if t + 1 < T:
                    e_norm(t + 1)
                e_route(t)
            for n in range(2 * CH):
                half, c = divmod(n, CH)
                r, rows = n % 2, P if c < CH - 1 else LAST
                dve.wait_ge(e_th, n + 1)
                step(V.scalar_tensor_tensor(aE[0:rows, r, :], thE[0:rows, r, :], 1.0, bank[2 * r][0:rows, :],
                                            ALU.add, ALU.mult))
                if n >= 2:
                    dve.wait_ge(e_dn, n - 1)
                dst = aE if c < ROUTED else actE
                V.tensor_tensor(dst[0:rows, r, :], aE[0:rows, r, :], bank[2 * r + 1][0:rows, :],
                                ALU.mult).then_inc(e_gud, 1)
                if c < ROUTED:
                    dve.wait_ge(e_gud, n + 1)
                    dve.wait_ge(e_wb, half * ROUTED + c + 1)
                    V.tensor_tensor(actE[:, r, :], aE[:, r, :], bank[4 + r][:, :], ALU.mult).then_inc(e_act, 1)
                else:
                    dve.wait_ge(e_gud, n + 1)
                    V.engine_nop().then_inc(e_act, 1)
            for t in range(T):
                dve.wait_ge(e_yt, t + 1)
                step(V.scalar_tensor_tensor(hid[:, t, :], bank[t % 2][:, 0:D], 0.5, hid[:, t, :], ALU.mult, ALU.add))
                V.scalar_tensor_tensor(xs[:, t, :], hid[:, t, :], tg[:, 3:4], xs[:, t, :], ALU.mult,
                                       ALU.add).then_inc(e_out, 1)

        @block.scalar
        def _(act):
            A = nc.scalar
            for dst, src, n in ((ident[:, :], ident_d, "consts"), (headmask[:, :], headmask_d, "consts"),
                                (gcol[:, :], gates, "gates"), (bk_sb[:, :], bkc, "cols"), (tok_i[:, :], itok, "tok"),
                                (gw[:, :, :], gate_wT, "gw"), (bvb[:, :], bv, "biases"), (bqb[:, :], bq, "biases"),
                                (bob[:, :], bo, "biases"), (ln1_sb[:, :], ln1c, "ln"), (ln2_sb[:, :], ln2c, "ln"),
                                (hid[:, 0:2, :], wq, "wqo"), (hid[:, 2:4, :], wo, "wqo")):
                act.dma_start(dst, src).then_inc(ld[n], 16)
            act.wait_ge(ld["gates"], 16)
            A.activation(tg[:, :], gcol[:, :], ACT.Tanh).then_inc(tg_ready, 1)
            act.wait_ge(ld["cols"], 16)
            for k in range(2 * C):
                c, half = divmod(k, 2)
                act.wait_ge(kproj, k + 1)
                A.activation(kraw[:, c, 512 * half:512 * half + 512], bank[6 + k % 2][:, :], ACT.Identity,
                             bias=bk_sb[:, c:c + 1]).then_inc(kraw_ready, 1)

            def copy(dst, src, s):
                A.copy(dst, src).then_inc(s, 1)

            def a_hT(t):
                act.wait_ge(a_hTp, t + 1)
                if t >= 2:
                    act.wait_ge(a_z, 2 * (t - 1))
                copy(hT[:, t % 2, :, :], bank[4][:, 0:D], a_hTs)

            def a_guT(t):
                act.wait_ge(a_guTp, t + 1)
                if t >= 1:
                    act.wait_ge(a_y, t)
                copy(guT[:, :, :], bank[5][:, 0:D], a_guTs)

            a_hT(0)
            for t in range(T):
                if t >= 1:
                    a_guT(t - 1)
                if t + 1 < T:
                    a_hT(t + 1)
                act.wait_ge(a_zsel, t + 1)
                if t >= 2:
                    act.wait_ge(a_gu, t - 1)
                A.activation(thA[:, t % 2, :], zbuf[:, t % 2, :], ACT.Tanh, scale=0.5).then_inc(a_th, 1)
            a_guT(T - 1)
            act.wait_ge(xwT_psum, 1)
            copy(xwT.rearrange("p k c n -> p (k c n)"), halfs(7)[:, 0:1024], xwT_ready)

            def b_xT(t):
                act.wait_ge(b_xqTp, t + 1)
                if t >= 2:
                    act.wait_ge(b_u, t - 1)
                copy(xqT_B[:, t % 2, :, :], halfs(4)[:, 0:D], b_xqTs)

            def b_qT(t):
                act.wait_ge(b_qTp, t + 1)
                if t >= 1:
                    act.wait_ge(b_d, t)
                copy(qTB, halfs(5)[:, 0:F0], b_qTs)

            act.wait_ge(ternary_ready, 3)
            b_xT(0)
            for t in range(T):
                act.wait_ge(b_g, t + 1)
                act.wait_ge(b_xq, t + 1)
                if t >= 1:
                    act.wait_ge(b_guse, t)
                for i in range(2):
                    ins = A.activation(thB[:, 512 * i:512 * i + 512], bank[i][:, :], ACT.Tanh, scale=cb[:, t, 3:4])
                ins.then_inc(b_th, 1)
                if t + 1 < T:
                    b_xT(t + 1)
                b_qT(t)

            def c_front(t):
                act.wait_ge(c_xqTp, t + 1)
                copy(qTb[:, t % 2, :, :], halfs(5)[:, 0:D], c_xqTs)
                act.wait_ge(c_qTp, t + 1)
                if t >= 2:
                    act.wait_ge(c_s, T * (t - 1))
                copy(qT_sb[:, t % 2, :, :], bank[5][:, 0:D], c_qTs)

            def c_exp(t, g):
                act.wait_ge(c_nm, XG * t + g + 1)
                for h in range(XG * g, XG * g + XG):
                    s = scores[:, t % 2, h, :]
                    ins = A.activation(s, s, ACT.Exp, bias=nmC[:, t % 2, h:h + 1])
                ins.then_inc(c_p, 1)

            def c_pT(t, g):
                for k in range(2):
                    n = 2 * g + k
                    act.wait_ge(c_pTp, T * t + n + 1)
                    if t >= 1:
                        act.wait_ge(c_pv, XG * (t - 1) + g + 1)
                    copy(probT[:, 2 * n:2 * n + 2, :, :], bank[2 + n % 2][:, :], c_pTs)

            act.wait_ge(b_qTs, T)
            c_front(0)
            for g in range(XG):
                c_exp(0, g)
            for t in range(T):
                if t + 1 < T:
                    c_front(t + 1)
                for g in range(XG):
                    c_pT(t, g)
                    if t + 1 < T:
                        c_exp(t + 1, g)
                act.wait_ge(c_pv, XG * (t + 1))
                if t >= 1:
                    act.wait_ge(c_oT, t)
                copy(oT_sb[:, :, :], bank[4][0:XA, :], c_pvs)
                act.wait_ge(c_oqTp, t + 1)
                copy(oqT[:, :, :], halfs(6)[:, 0:D], c_oqTs)

            G = B * NH
            act.wait_ge(ternary_ready, 3)
            for i in range(G + 3):
                if i < G:
                    act.wait_ge(d_qkp, i + 1)
                    if i >= 2:
                        act.wait_ge(d_s, i - 1)
                    copy(qk[:, i % 2, :], bank[i % 2][:, :], d_qs)
                if 2 <= i < G + 2:
                    g = i - 2
                    act.wait_ge(d_pTp, g + 1)
                    if g >= 2:
                        act.wait_ge(d_a, g - 1)
                    copy(probDT[:, g % 2, :], bank[4][:, 0:3 * P], d_pTs)
                if 1 <= i < G + 1:
                    g = i - 1
                    r = g % 2
                    act.wait_ge(d_nm, g + 1)
                    if g == 0:
                        act.wait_ge(ld["consts"], 32)
                        act.wait_ge(ld["ln"], 32)
                    if g >= 2:
                        act.wait_ge(d_p, g - 1)
                    A.activation(probD[:, r, 0:P], probD[:, r, 0:P], ACT.Exp, bias=nmD[:, r, 0:1], scale=SCALE,
                                 accum_out=rsD[:, r, 0:1]).then_inc(d_e, 1)
                    A.activation(probD[:, r, P:3 * P], probD[:, r, P:3 * P], ACT.Exp, bias=nmD[:, r, 1:2], scale=SCALE,
                                 accum_out=rsD[:, r, 1:2]).then_inc(d_e, 1)

            for t in range(T):
                act.wait_ge(e_x2Tp, t + 1)
                for c in range(C):
                    ins = A.activation(ctxT_sb[:, c, P * t:P * t + P], bank[4][:, P * c:P * c + P], ACT.Copy,
                                       scale=ln2_sb[:, c:c + 1])
                ins.then_inc(e_x2Ts, 1)
                if t >= 1:
                    act.wait_ge(e_wTp, t)
                    copy(wTb[:, P * (t - 1):P * t], halfs(6)[0:3 * E1, 0:P], e_wTs)
                act.wait_ge(e_lgs, t + 1)
                A.activation(lg[:, t % 2, 1, :], lg[:, t % 2, 1, :], ACT.Exp).then_inc(e_ex, 1)
            act.wait_ge(e_wTp, T)
            copy(wTb[:, P * (T - 1):P * T], halfs(6)[0:3 * E1, 0:P], e_wTs)
            for n in range(2 * CH):
                half, c = divmod(n, CH)
                r, rows = n % 2, P if c < CH - 1 else LAST
                act.wait_ge(e_gu, n + 1)
                if n >= 2:
                    act.wait_ge(e_gud, n - 1)
                A.activation(thE[0:rows, r, :], bank[2 * r][0:rows, :], ACT.Tanh, scale=0.5).then_inc(e_th, 1)
                if c == CH - 1:
                    act.wait_ge(e_dn, n + 1)
                    for k in range(C):
                        copy(ctxT_sb[:, k, 512 * half:512 * half + 512], bank[6 + k][:, :], e_yT)

        @block.tensor
        def _(pe):
            M = nc.tensor.matmul
            Tr = nc.tensor.transpose

            pe.wait_ge(ld["ctx"], 16)
            pe.wait_ge(ld["wkv"], 32)
            for k in range(2 * C):
                c, half = divmod(k, 2)
                if k >= 2:
                    pe.wait_ge(kraw_ready, k - 1)
                for i in range(C):
                    last = M(bank[6 + k % 2][:, :], xw[:, 0, i, P * c:P * c + P],
                             ctxT_sb[:, i, 512 * half:512 * half + 512], start=i == 0, stop=i == C - 1)
                last.then_inc(kproj, 1)
            for t in range(T):
                if t < 2:
                    pe.wait_ge(kraw_ready, 3 + t)
                else:
                    pe.wait_ge(v_ready, XG * (t - 1))
                for i in range(C):
                    last = M(bank[6 + t % 2][:, 0:D], ctxT_sb[:, i, P * t:P * t + P], xw[:, 2, i, :],
                             start=i == 0, stop=i == C - 1)
                last.then_inc(vproj, 1)

            def a_th(t):
                pe.wait_ge(a_h, t + 1)
                if t >= 1:
                    pe.wait_ge(a_hTs, t)
                for c in range(C):
                    last = Tr(bank[4][:, P * c:P * c + P], hbuf[:, t % 2, P * c:P * c + P], ident[:, :])
                last.then_inc(a_hTp, 1)

            def a_z_half(t, half):
                if half == 0:
                    pe.wait_ge(a_hTs, t + 1)
                    if t >= 1:
                        pe.wait_ge(a_zsel, t)
                for i in range(C):
                    last = M(bank[half][:, :], hT[:, t % 2, i, :], ctxT_sb[:, i, 512 * half:512 * half + 512],
                             start=i == 0, stop=i == C - 1)
                last.then_inc(a_z, 1)

            def a_tgu(t):
                pe.wait_ge(a_gu, t + 1)
                if t >= 1:
                    pe.wait_ge(a_guTs, t)
                for c in range(C):
                    last = Tr(bank[5][:, P * c:P * c + P], gubuf[:, t % 2, P * c:P * c + P], ident[:, :])
                last.then_inc(a_guTp, 1)

            def a_yy(t):
                pe.wait_ge(a_guTs, t + 1)
                if t >= 1:
                    pe.wait_ge(a_x1, t)
                for half in range(2):
                    for i in range(C):
                        last = M(bank[2 + half][:, :], guT[:, i, :], ctxT_sb[:, i, 512 * half:512 * half + 512],
                                 start=i == 0, stop=i == C - 1)
                last.then_inc(a_y, 1)

            pe.wait_ge(identb_ready, 1)
            a_th(0)
            for t in range(T):
                a_z_half(t, 0)
                if t >= 1:
                    a_tgu(t - 1)
                if t + 1 < T:
                    a_th(t + 1)
                a_z_half(t, 1)
                if t >= 1:
                    a_yy(t - 1)
                if t == 2:
                    pe.wait_ge(wabs_ready, 3)
                    pe.wait_ge(ones_ready, 2)
                    pe.wait_ge(v_ready, XG * T)
                    M(bank[6][:, 0:3], ones[:, :], wsum[:, :], start=True, stop=True).then_inc(wsum_ready, 1)
                if t == 7:
                    pe.wait_ge(diag_ready, 4)
                    for i in range(4):
                        last = M(bank[6][:, P * i:P * i + P], ones[:, :], diag[:, i, :], start=True, stop=True)
                    last.then_inc(swb_psum, 1)
            a_tgu(T - 1)
            a_yy(T - 1)
            pe.wait_ge(xwb_ready, 4)
            for k in range(2):
                for c in range(C):
                    for i in range(C):
                        o = 512 * k + D * i + P * c
                        last = Tr(halfs(7)[:, o:o + P], xwb[:, k, c, P * i:P * i + P], identb[:, :])
            last.then_inc(xwT_psum, 1)

            def b_tx(t):
                pe.wait_ge(b_xq, t + 1)
                if t >= 1:
                    pe.wait_ge(b_xqTs, t)
                for c in range(C):
                    last = Tr(halfs(4)[:, P * c:P * c + P], qb[:, t % 2, P * c:P * c + P], identb[:, :])
                last.then_inc(b_xqTp, 1)

            def b_down(t):
                pe.wait_ge(b_q, t + 1)
                if t >= 1:
                    pe.wait_ge(b_qTs, t)
                for c in range(FC):
                    last = Tr(halfs(5)[:, P * c:P * c + P], qB[:, P * c:P * c + P], identb[:, :])
                last.then_inc(b_qTp, 1)
                pe.wait_ge(b_qTs, t + 1)
                if t >= 1:
                    pe.wait_ge(b_x2, t)
                else:
                    pe.wait_ge(swb_ready, 3)
                for c in range(FC):
                    last = M(bank[6][:, 0:D], qTB[:, c, :], dnb[:, c, :], start=c == 0, stop=c == FC - 1)
                last.then_inc(b_d, 1)

            b_tx(0)
            for t in range(T):
                pe.wait_ge(b_xqTs, t + 1)
                for k in range(2):
                    if t >= 1:
                        pe.wait_ge((b_guse, b_p)[k], t)
                    elif k == 0:
                        pe.wait_ge(ternary_ready, 3)
                    for half in range(2):
                        for i in range(C):
                            last = M(bank[2 * k + half][:, :], xqT_B[:, t % 2, i, :],
                                     gub[:, k, i, 512 * half:512 * half + 512], start=i == 0, stop=i == C - 1)
                    last.then_inc((b_g, b_u)[k], 1)
                if t + 1 < T:
                    b_tx(t + 1)
                if t >= 1:
                    b_down(t - 1)
            b_down(T - 1)

            def c_front(t):
                pe.wait_ge(c_xq, t + 1)
                if t >= 1:
                    pe.wait_ge(c_qTs, t)
                else:
                    pe.wait_ge(xwT_ready, 1)
                for c in range(C):
                    last = Tr(halfs(5)[:, P * c:P * c + P], qb[:, t % 2, P * c:P * c + P], identb[:, :])
                last.then_inc(c_xqTp, 1)
                pe.wait_ge(c_xqTs, t + 1)
                for i in range(C):
                    last = M(bank[5][:, 128:128 + D], qTb[:, t % 2, i, :], xwT[:, 0, i, :], start=i == 0, stop=i == C - 1)
                last.then_inc(c_qp, 1)
                pe.wait_ge(c_q, t + 1)
                for c in range(C):
                    last = Tr(bank[5][:, P * c:P * c + P], hbuf[:, t % 2, P * c:P * c + P], ident[:, :])
                last.then_inc(c_qTp, 1)

            def c_score(t):
                pe.wait_ge(c_qTs, t + 1)
                pe.wait_ge(keysm_ready, B * C)
                for k in range(T):
                    c, pair = divmod(k, 4)
                    n = T * t + k
                    if n >= 2:
                        pe.wait_ge(c_sm, 2 * (n - 1))
                    M(bank[k % 2][:, :], qT_sb[:, t % 2, c, :], keysm[:, t // TB, c, 2 * pair:2 * pair + 2, :],
                      start=True, stop=True).then_inc(c_s, 1)

            def c_tp(t, g):
                pe.wait_ge(c_p, XG * t + g + 1)
                for k in range(2):
                    n = 2 * g + k
                    m = T * t + n
                    if m >= 2:
                        pe.wait_ge(c_pTs, m - 1)
                    for i in range(4):
                        h, l = 2 * n + i // 2, i % 2
                        last = Tr(bank[2 + n % 2][:, P * i:P * i + P], scores[:, t % 2, h, P * l:P * l + P], ident[:, :])
                    last.then_inc(c_pTp, 1)

            def c_pv_(t, g):
                pe.wait_ge(c_pTs, T * t + 2 * g + 2)
                if g == 0 and t >= 1:
                    pe.wait_ge(c_pvs, t)
                for i in range(2 * XG):
                    j, l = divmod(i, 2)
                    h = XG * g + j
                    last = M(bank[4][0:XA, P * g:P * g + P], vaug[:, TB * (t // TB) + l, h, :], probT[:, h, l, :],
                             start=i == 0, stop=i == 2 * XG - 1)
                last.then_inc(c_pv, 1)

            def c_outp(t):
                pe.wait_ge(c_pvs, t + 1)
                if t >= 1:
                    pe.wait_ge(c_x3, t)
                for g in range(XG):
                    last = Tr(bank[6][:, XA * g:XA * g + XA], oT_sb[:, g, :], ident[0:XA, 0:XA])
                last.then_inc(c_oT, 1)
                pe.wait_ge(c_o, t + 1)
                for c in range(C):
                    last = Tr(halfs(6)[:, P * c:P * c + P], oq[:, P * c:P * c + P], identb[:, :])
                last.then_inc(c_oqTp, 1)
                pe.wait_ge(c_oqTs, t + 1)
                for i in range(C):
                    last = M(bank[6][:, 128:128 + D], oqT[:, i, :], xwT[:, 1, i, :], start=i == 0, stop=i == C - 1)
                last.then_inc(c_op, 1)

            pe.wait_ge(b_x2, T)
            c_front(0)
            c_score(0)
            for t in range(T):
                if t + 1 < T:
                    c_front(t + 1)
                    
                for g in range(XG):
                    c_tp(t, g)
                    if g >= 1:
                        c_pv_(t, g - 1)
                    if g == 0 and t + 1 < T:
                        c_score(t + 1)
                c_pv_(t, XG - 1)
                c_outp(t)

            def vo_make(key):
                kind, b, u = key
                n = VO[key]
                p = 6 + n % 2
                if n >= 2:
                    pe.wait_ge(d_vofree, n - 1)
                else:
                    pe.wait_ge(c_x3, T)
                if kind == "T":
                    t = TB * b + u
                    pe.wait_ge(d_xn, t + 1)
                    for c in range(C):
                        last = Tr(bank[p][:, P * c:P * c + P], hbuf[:, t % 2, P * c:P * c + P], ident[:, :])
                elif kind == "V":
                    l, q = divmod(u, NV // TB)
                    pe.wait_ge(d_vofree, VO["T", b, TB - 1] + 1)
                    pe.wait_ge(ld["vw"], 16)
                    t = TB * b + l
                    for i in range(C):
                        last = M(bank[p][:, :], ctxT_sb[:, i, P * t:P * t + P], vw[:, i, 512 * q:512 * q + 512],
                                 start=i == 0, stop=i == C - 1)
                else:
                    pe.wait_ge(ld["ow"], 16)
                    pe.wait_ge(d_as, NH * (b + 1))
                    for h in range(NH):
                        last = M(bank[p][:, 0:D], attnT[:, h, P * u:P * u + P], ow[:, h, :], start=h == 0,
                                 stop=h == NH - 1)
                last.then_inc(d_vo, 1)

            def d_qk(g):
                b, h = divmod(g, NH)
                pe.wait_ge(d_vofree, VO["T", b, TB - 1] + 1)
                if g >= 2:
                    pe.wait_ge(d_qs, g - 1)
                else:
                    pe.wait_ge(ld["qw"], 16)
                    pe.wait_ge(ld["kw"], 16)
                for k, w in enumerate((qw, kw)):
                    for i in range(C):
                        last = M(bank[g % 2][:, S * k:S * k + S], w[:, i, HD * h:HD * h + HD],
                                 ctxT_sb[:, i, S * b:S * b + S], start=i == 0, stop=i == C - 1)
                last.then_inc(d_qkp, 1)

            def d_score(g):
                pe.wait_ge(d_qs, g + 1)
                if g >= 2:
                    pe.wait_ge(d_nm, g - 1)
                q, k = qk[:, g % 2, 0:S], qk[:, g % 2, S:2 * S]
                M(bank[2 + g % 2][:, 0:P], q[:, 0:P], k[:, 0:P], start=True, stop=True)
                M(bank[2 + g % 2][:, P:3 * P], q[:, P:S], k[:, 0:S], start=True, stop=True).then_inc(d_s, 1)

            def d_tp(g):
                pe.wait_ge(d_p, g + 1)
                if g >= 1:
                    pe.wait_ge(d_pTs, g)
                for i in range(3):
                    last = Tr(bank[4][:, P * i:P * i + P], probD[:, g % 2, P * i:P * i + P], ident[:, :])
                last.then_inc(d_pTp, 1)

            def d_pv(g):
                b, h = divmod(g, NH)
                pe.wait_ge(d_pTs, g + 1)
                pe.wait_ge(d_vofree, VO["V", b, NV - 1] + 1)
                if g >= 1:
                    pe.wait_ge(d_as, g)
                M(bank[5][:, 0:S], vals[:, b % 2, 0, HD * h:HD * h + HD], probDT[:, g % 2, 0:S], start=True, stop=False)
                M(bank[5][:, P:S], vals[:, b % 2, 1, HD * h:HD * h + HD], probDT[:, g % 2, S:3 * P],
                  start=False, stop=True).then_inc(d_a, 1)

            G = B * NH
            for i in range(G + 4):
                b, h = divmod(i, NH)
                if i == 0:
                    for u in range(TB):
                        vo_make(("T", 0, u))
                    for u in range(NV):
                        vo_make(("V", 0, u))
                if h == 12 and b + 1 < B:
                    for u in range(TB):
                        vo_make(("T", b + 1, u))
                    for u in range(NV):
                        vo_make(("V", b + 1, u))
                if i < G:
                    d_qk(i)
                if 1 <= i <= G:
                    d_score(i - 1)
                if 2 <= i <= G + 1:
                    d_tp(i - 2)
                if 3 <= i <= G + 2:
                    d_pv(i - 3)
                if h == 3 and b >= 1:
                    for u in range(TB):
                        vo_make(("O", b - 1, u))

            def e_logits(t):
                pe.wait_ge(e_x2Ts, t + 1)
                if t >= 1:
                    pe.wait_ge(e_lgs, t)
                else:
                    pe.wait_ge(ld["gw"], 16)
                for i in range(C):
                    last = M(bank[5][:, 0:E1], ctxT_sb[:, i, P * t:P * t + P], gw[:, i, :], start=i == 0, stop=i == C - 1)
                last.then_inc(e_lg, 1)

            def e_tw(t):
                pe.wait_ge(e_w, t + 1)
                if t >= 1:
                    pe.wait_ge(e_wTs, t)
                Tr(halfs(6)[0:3 * E1, 0:P], lw[:, t % 2, :], identb[:, :]).then_inc(e_wTp, 1)

            pe.wait_ge(d_vofree, VO_END)
            for t in range(T):
                pe.wait_ge(e_x2, t + 1)
                if t >= 1:
                    pe.wait_ge(e_x2Ts, t)
                for c in range(C):
                    last = Tr(bank[4][:, P * c:P * c + P], hbuf[:, t % 2, P * c:P * c + P], ident[:, :])
                last.then_inc(e_x2Tp, 1)
                e_logits(t)
                if t >= 1:
                    e_tw(t - 1)
            e_tw(T - 1)

            def chunk(c):
                w = armR[:, place[c]:place[c] + WCH]
                return (w[:, 0:2 * P].rearrange("p (i n) -> p i n", i=C),
                        w[:, 2 * P:4 * P].rearrange("p (i n) -> p i n", i=C), w[:, 4 * P:WCH])

            def e_down(n):
                half, c = divmod(n, CH)
                r, rows = n % 2, P if c < CH - 1 else LAST
                pe.wait_ge(e_act, n + 1)
                if c == 0 and half == 1:
                    pe.wait_ge(e_yT, C)
                wd = chunk(c)[2]
                for k in range(C):
                    last = M(bank[6 + k][:, :], wd[0:rows, P * k:P * k + P], actE[0:rows, r, :], start=c == 0,
                             stop=c == CH - 1)
                last.then_inc(e_dn, 1)

            pe.wait_ge(e_wTs, T)
            pe.wait_ge(e_lgs, T)
            for n in range(2 * CH):
                half, c = divmod(n, CH)
                r, rows = n % 2, P if c < CH - 1 else LAST
                if n == 0:
                    pe.wait_ge(ld_moe[0], 16)
                    pe.wait_ge(ld["sel"], 16)
                if n == FIRST // 2:
                    pe.wait_ge(ld_moe[1], 16)
                if n == FIRST:
                    pe.wait_ge(ld_moe[2], 16)
                if n >= 2:
                    pe.wait_ge(e_gud, n - 1)
                for k in range(2):
                    w = chunk(c)[k]
                    for i in range(C):
                        last = M(bank[2 * r + k][0:rows, :], w[:, i, 0:rows],
                                 ctxT_sb[:, i, 512 * half:512 * half + 512], start=i == 0, stop=i == C - 1)
                last.then_inc(e_gu, 1)
                if c < ROUTED:
                    if n >= 2:
                        pe.wait_ge(e_act, n - 1)
                    M(bank[4 + r][:, :], sel[:, P * c:P * c + P], wTb[:, 512 * half:512 * half + 512],
                      start=True, stop=True).then_inc(e_wb, 1)
                if n >= 1:
                    e_down(n - 1)
            e_down(2 * CH - 1)
            for t in range(T):
                if t < 4:
                    pe.wait_ge(e_yT, C)
                else:
                    pe.wait_ge(e_yT, 2 * C)
                if t >= 2:
                    pe.wait_ge(e_out, t - 1)
                for c in range(C):
                    last = Tr(bank[t % 2][:, P * c:P * c + P], ctxT_sb[:, c, P * t:P * t + P], ident[:, :])
                last.then_inc(e_yt, 1)

def kernel(**inputs):
    import numpy as np
    import concourse.bacc as bacc
    from concourse.bass_utils import run_bass_kernel_spmd

    g = {k: np.asarray(v) for k, v in inputs.items()}

    def tiles(a):
        a = a.reshape(-1, P, a.shape[-1])
        return np.ascontiguousarray(a.transpose(1, 0, 2))

    def rows(v):
        return np.ascontiguousarray(np.broadcast_to(v.reshape(1, -1), (P, v.size)))

    def flat(a):
        return np.ascontiguousarray(a.reshape(P, -1))

    eye = np.eye(P, dtype=np.float32)
    tri = np.where(np.tril(np.ones((P, P), bool)), 0.0, -1e9 / SCALE).astype(np.float32)
    heads = (np.arange(P)[:, None] // XD == np.arange(8)[None, :]).astype(np.float32)
    expert = np.arange(ROUTED * P) // I1
    sel = np.where(expert[None, :] == (np.arange(3 * E1) % E1)[:, None], 0x3F80, 0).astype(np.uint16)

    w1, w2 = g["L1_ffn_w1"], g["L1_ffn_w2"]
    sgu, sdn = g["L1_ffn_sh_gu_w"], g["L1_ffn_sh_down_w"]
    pad = np.zeros((CH * P - E1 * I1 - SHI, D), np.float32)
    up = np.concatenate([w1[:, I1:, :].reshape(-1, D), sgu[SHI:], pad])
    gate = np.concatenate([w1[:, :I1, :].reshape(-1, D), sgu[:SHI], pad])
    down = np.concatenate([w2.transpose(0, 2, 1).reshape(-1, D), sdn.T, pad])
    moe = np.zeros((P, CH, WCH), np.float32)
    for k, w in enumerate((gate, up)):
        moe[:, :, 2 * P * k:2 * P * k + 2 * P] = w.reshape(CH, P, C, P).transpose(3, 0, 2, 1).reshape(P, CH, C * P)
    moe[:, :, 4 * P:] = down.reshape(CH, P, D).transpose(1, 0, 2)

    qw = g["L1_ffn_q_w"].reshape(NH, QHD, D)[:, :HD, :].reshape(NH * HD, D)
    kv = g["L1_ffn_kv_w"]
    arrays = {
        "x": tiles(g["x"].reshape(-1, D)),
        "itok": np.ascontiguousarray(g["itok_BxS_13_99985"].reshape(T, P).T),
        "ctxT": tiles(g["ctx_2048"].reshape(-1, D).T),
        "mask": np.ascontiguousarray(g["mask_BxSxS2_ff0"].reshape(T, P, S)),
        "gates": rows(np.concatenate([g["g_xattn"], g["g_ffn"]])),
        "w_gate": flat(tiles(g["L0_ffn_w_gate"].T)),
        "w_up": flat(tiles(g["L0_ffn_w_up"].T)),
        "w_down": flat(tiles(g["L0_ffn_w_down"].T)),
        "wq": tiles(g["L1_xattn_wq"]),
        "wkT": np.ascontiguousarray(np.stack([tiles(g["L1_xattn_wk"].T)] * 2, axis=1)),
        "wvT": tiles(g["L1_xattn_wv"].T),
        "wo": tiles(g["L1_xattn_wo"]),
        "bq": rows(g["L1_xattn_bq"]),
        "bkc": np.ascontiguousarray(g["L1_xattn_bk"].reshape(C, P).T),
        "bv": rows(g["L1_xattn_bv"]),
        "bo": rows(g["L1_xattn_bo"]),
        "ln1c": np.ascontiguousarray(g["L1_ffn_ln1_w"].reshape(C, P).T),
        "ln2c": np.ascontiguousarray(g["L1_ffn_ln2_w"].reshape(C, P).T),
        "qwT": tiles(qw.T),
        "kwT": tiles(kv[:NH * HD].T),
        "vwT": tiles(kv[NH * HD:2 * NH * HD].T),
        "owT": tiles(g["L1_ffn_o_w"].T),
        "gate_wT": tiles(g["L1_ffn_gate_w"].T),
        "w_moe": moe.reshape(P, -1),
        "ident_d": eye, "tri_d": tri, "headmask_d": heads, "sel_d": sel,
    }
    nc = bacc.Bacc("TRN2", target_bir_lowering=False, num_devices=1)
    aps = {}
    for n, a in arrays.items():
        aps[n] = nc.dram_tensor("in_" + n, a.shape, mybir.dt.from_np(a.dtype), kind="ExternalInput").ap()
    aps["sel_d"] = aps["sel_d"].bitcast(mybir.dt.bfloat16)
    out = nc.dram_tensor("out_y", (P, T, D), mybir.dt.float32, kind="ExternalOutput").ap()
    flamingo(nc, out=out, **aps)
    r = run_bass_kernel_spmd(nc, [{"in_" + n: a for n, a in arrays.items()}], core_ids=[0])
    y = r.results[0]["out_y"]
    return np.ascontiguousarray(y.transpose(1, 0, 2)).reshape(B, S, D)
```

```python
import concourse.bass as bass
from concourse import mybir
from contextlib import ExitStack

P = 128
B, S, D = 4, 256, 256
T = B * S // P
TB = S // P
C = D // P
E0 = 4
VOCAB = 12500
F0 = 1024
FC = F0 // P
XH, XD = 16, 16
XG = 4
XA = XG * XD + XG
NH, HD, QHD = 16, 128, 192
E1, TOPK, I1 = 16, 4, 176
SHI = 2 * I1
ROUTED = E1 * I1 // P
CH = -(-(E1 * I1 + SHI) // P)
LAST = E1 * I1 + SHI - (CH - 1) * P
WCH = 4 * P + D
MAGIC = 12582912.0
NEG = -3.0e38
SCALE = float(QHD) ** -0.5
XSCALE, WSCALE, QSCALE, HSCALE = 2.0 ** 6, 2.0 ** 8, 2.0 ** 6, 2.0 ** 2
ASCALE = HSCALE / (WSCALE * XSCALE) ** 2
YSCALE = 0.5 / (HSCALE * WSCALE)
AHEAD = 4

def flamingo(nc, x, itok, ctxT, mask, gates, w_gate, w_up, w_down, wq, wkT, wvT, wo, bq, bkc, bv, bo,
             ln1c, ln2c, qwT, kwT, vwT, owT, gate_wT, w_moe, ident_d, tri_d, headmask_d, sel_d, out):
    f32, bf16, fp16 = mybir.dt.float32, mybir.dt.bfloat16, mybir.dt.float16
    ALU, ACT, AX = mybir.AluOpType, mybir.ActivationFunctionType, mybir.AxisListType
    ctx = ExitStack()
    with ctx:
        def sb(name, shape, dt=f32):
            return ctx.enter_context(nc.sbuf_tensor(name, shape, dt))

        def sem(name):
            return ctx.enter_context(nc.semaphore(name))

        xs = sb("xs", [P, T, D])
        ctxT_sb = sb("ctxT_sb", [P, C, B * S])
        hid = sb("hid", [P, T, D])
        armK = sb("armK", [P, 16384])
        armR = sb("armR", [P, 20992])
        armW = sb("armW", [P, 3072])
        xw8 = sb("xw8", [P, 4 * C * D // 2])
        keysm = armK[:, 0:8192].rearrange("p (b c h s) -> p b c h s", b=2, c=C, h=8)
        kraw = armK[:, 8192:10240].rearrange("p (c n) -> p c n", c=C)
        temps = armK[:, 10240:16384]
        zbuf, ubuf, gubuf = (temps[:, 256 * i:256 * i + 256] for i in range(3))
        obuf = temps[:, 768:1024]
        thB = temps[:, 1024:2048].rearrange("p (j n) -> p j n", j=2)
        pB = temps[:, 2048:3072]
        qB = temps[:, 3072:3584].bitcast(bf16)
        qTB = temps[:, 3584:4096].bitcast(bf16).rearrange("p (c n) -> p c n", c=FC)
        oT_sb = temps[0:XA, 4096:4608].rearrange("p (g n) -> p g n", g=XG)
        oq = temps[:, 4608:4736].bitcast(bf16)
        oqT = temps[:, 4736:4864].bitcast(bf16).rearrange("p (c n) -> p c n", c=C)
        qTC = temps[:, 4864:5376].rearrange("p (r c n) -> p r c n", r=2, c=C)
        guT = temps[:, 5376:5632].rearrange("p (c n) -> p c n", c=C)
        sel = armK[0:3 * E1, 14336:14336 + ROUTED * P // 2].bitcast(bf16)
        wTb = armK[0:3 * E1, 15744:15744 + T * P // 2].bitcast(bf16)
        xT2 = armK[:, 12288:14336].bitcast(fp16).rearrange("p (k c n) -> p k c n", k=2, c=C)
        scores = armR[:, 0:8192].rearrange("p (r h s) -> p r h s", r=2, h=XH)
        vaug = armR[:, 8192:8192 + T * XH * XA].rearrange("p (t h a) -> p t h a", t=T, h=XH)
        probT = armR[:, 16896:20992].rearrange("p (h l n) -> p h l n", h=XH, l=TB)
        wraw = armR[:, 0:6144].rearrange("p (k n) -> p k n", k=3)
        xw = armR[:, 18944:20992].rearrange("p (k c n) -> p k c n", k=4, c=C)
        vals = armR[:, 0:8192].rearrange("p (r l n) -> p r l n", r=2, l=TB)
        attnT = armR[:, 8192:8704].bitcast(fp16).rearrange("p (r k n) -> p r k n", r=2, k=2)
        x2buf = armW[:, 2560:3072].rearrange("p (u n) -> p u n", u=TB)
        EARLY, FIRST = 10, 15
        SB = (4, 7)
        LOADS = ((0, EARLY), (EARLY, FIRST), (FIRST, 20), (20, CH))
        place = ([8704 + WCH * c for c in range(EARLY)] + [16896 + WCH * c for c in range(FIRST - EARLY)]
                 + [WCH * c for c in range(CH - FIRST)])

        PIECE = 4 * D
        PIECES = 4096 // PIECE
        PLACES = {}
        for n in range(PIECES):
            PLACES["k", n] = (armK, PIECE * n), (armK, PIECE * (n - 1) if n else 8192)
            PLACES["q", n] = (armK, 4096 + PIECE * n), (armK, 4096 + PIECE * (n - 1))
            PLACES["v", n] = (armR, 16896 + PIECE * n), (armR, 16896 + PIECE * (n - 1)) if n else (xw8, 0)
            PLACES["o", n] = ((armK, 9216 + PIECE * n) if n < 3 else (armR, 19968),
                              (armK, 9216 + PIECE * (n - 1) if n else 7168))
        for n in range(CH):
            PLACES["moe", n] = (armR, place[n]), (armR, place[n - 1]) if n else (xw8, 0)
        ORDER = ([("k", n) for n in range(PIECES)] + [("q", 0)] + [("v", n) for n in range(PIECES)]
                 + [("q", n) for n in range(1, PIECES)] + [("o", n) for n in range(PIECES)]
                 + [("moe", n) for n in range(CH)])
        SPLIT_AT = {0: ("v", 2), 1: ("v", 3), 2: ("q", 1), 3: ("q", 2), 4: ("q", 3), 5: ("o", 0), 7: ("o", 1), 9: ("o", 2),
                    11: ("o", 3)}
        for n in range(EARLY):
            SPLIT_AT[(B - 1) * NH + 2 + n] = ("moe", n)
        SPLIT = {key: n for n, key in enumerate(ORDER)}

        def raw_piece(kind, n):
            (arm, at), size = PLACES[kind, n][0], WCH if kind == "moe" else PIECE
            return arm[:, at:at + size]

        def split_piece(kind, n):
            (arm, at), size = PLACES[kind, n][1], WCH if kind == "moe" else PIECE
            return arm[:, at:at + size].bitcast(fp16).rearrange("p (k n) -> p k n", k=2)

        gub = armW[:, 0:2048].bitcast(bf16).rearrange("p (k c n) -> p k c n", k=2, c=C)
        dnb = armW[:, 2048:3072].bitcast(bf16).rearrange("p (c n) -> p c n", c=FC)
        qk = armW[:, 0:1024].bitcast(fp16).rearrange("p (r k n) -> p r k n", r=2, k=2)
        probD = armW[:, 1024:1792].rearrange("p (r n) -> p r n", r=2)
        probDT = armW[:, 1792:2560].rearrange("p (r n) -> p r n", r=2)
        thE = armW[:, 0:1024].rearrange("p (r n) -> p r n", r=2)
        actE = armW[:, 1024:2048].bitcast(fp16).rearrange("p (r k n) -> p r k n", r=2, k=2)

        ident = sb("ident", [P, P])
        identb = sb("identb", [P, P], bf16)
        ones = sb("ones", [P, P])
        tri = sb("tri", [P, P])
        trib = sb("trib", [P, P], bf16)
        headmask = sb("headmask", [P, 8])
        maskt = sb("maskt", [P, 2, S])
        hbuf = sb("hbuf", [P, 3, D])
        hT = sb("hT", [P, C, P])
        qb = sb("qb", [P, 2, D], bf16)
        qTb = sb("qTb", [P, 2, C, P], bf16)
        bqb, bvb, bob = sb("bqb", [P, D]), sb("bvb", [P, D]), sb("bob", [P, D])
        swb = sb("swb", [P, 4, P])
        xwb, xwT = (xw8[:, C * D * k:C * D * k + C * D].bitcast(bf16).rearrange("p (k c n) -> p k c n", k=2, c=C)
                    for k in range(2))
        gw = sb("gw", [P, C, E1])
        tok_i = sb("tok_i", [P, T], mybir.dt.int32)
        tok = sb("tok", [P, T])
        ge = sb("ge", [P, 3, T])
        em = sb("em", [P, E0, T])
        ey = sb("ey", [P, E0, T])
        gcol, tg = sb("gcol", [P, 4]), sb("tg", [P, 4])
        bk_sb, ln1_sb, ln2_sb = sb("bk_sb", [P, C]), sb("ln1_sb", [P, C]), sb("ln2_sb", [P, C])
        JOB = {}

        def ask(*keys):
            for key in keys:
                JOB[key] = len(JOB)

        ask(("A", 0), ("A", 1))
        for i in range(T + 2):
            if i >= 2:
                ask(("C", i - 2))
            if i < T:
                ask(("B", i))
            if i + 2 < T:
                ask(("A", i + 2))
        def ask_rows(b):
            ask(*((k, TB * b + u) for k in "DR" for u in range(TB)))

        ask_rows(0)
        for b in range(B + 1):
            if b + 1 < B:
                ask_rows(b + 1)
            if b >= 1:
                ask(*(("E", TB * (b - 1) + u) for u in range(TB)))
        JOBS = len(JOB)
        st, mv = sb("st", [P, 6]), sb("mv", [P, JOBS, 2])
        powin, rstd, nhalf = sb("powin", [P, JOBS]), sb("rstd", [P, JOBS]), sb("nhalf", [P, 1])
        wsum, wsc, thr = sb("wsum", [P, 3]), sb("wsc", [P, 3]), sb("thr", [P, 6])
        cb = sb("cb", [P, T, 8])
        xwc = sb("xwc", [P, 4, 4])
        cc = sb("cc", [P, T, 8])
        mxC, nmC = sb("mxC", [P, 2, XH]), sb("nmC", [P, 2, XH])
        rdC = sb("rdC", [P, XH])
        mxD, nmD, rsD, riD = (sb(n, [P, 2, 2]) for n in ("mxD", "nmD", "rsD", "riD"))
        lg = sb("lg", [P, 2, 8, E1])
        lw = sb("lw", [P, 2, 3 * E1], bf16)

        wqo = hid[:, 0:4, :].rearrange("p (k c) n -> p k c n", k=2)
        diag = hid[:, 4:6, :].rearrange("p a (i n) -> p (a i) n", i=2)

        bank = [ctx.enter_context(nc.psum_tensor(f"bank{i}", [P, 512], f32)) for i in range(8)]

        def halfs(i):
            return bank[i][:, :].bitcast(bf16)

        names = ("x0 x1 tok gates ctx wkv consts raw biases wqo cols tri ln gw sel qw kw vw ow ow_last").split()
        ld = {n: sem("ld_" + n) for n in names}
        ld_mask = [sem(f"ld_mask{i}") for i in range(2)]
        ld_moe = [sem(f"ld_moe{i}") for i in range(len(LOADS))]
        st_out = sem("st_out")
        vec_step, pow_in, pow_out = sem("vec_step"), sem("pow_in"), sem("pow_out")
        (identb_ready, tg_ready, ones_ready, vaug_zero, kproj, kraw_ready, keysm_ready, vproj, v_ready, wabs_ready,
         wsum_ready, ternary_ready, xwb_ready, xwT_psum, xwT_ready, diag_ready, swb_psum, swb_ready) = (
            sem(n) for n in ("identb_ready tg_ready ones_ready vaug_zero kproj kraw_ready keysm_ready vproj v_ready "
                             "wabs_ready wsum_ready ternary_ready xwb_ready xwT_psum xwT_ready diag_ready swb_psum "
                             "swb_ready").split())
        a_h, a_hTp, a_hTs, a_z, a_zsel, a_th, a_gu, a_guTp, a_guTs, a_y, a_x1 = (
            sem("a_" + n) for n in "h hTp hTs z zsel th gu guTp guTs y x1".split())
        b_xq, b_xqTp, b_xqTs, b_gu, b_th, b_p, b_q, b_qTp, b_qTs, b_d, b_x2 = (
            sem("b_" + n) for n in "xq xqTp xqTs gu th p q qTp qTs d x2".split())
        (c_xq, c_xqTp, c_xqTs, c_qp, c_q, c_qTp, c_qTs, c_s, c_sm, c_nm, c_p, c_pTp, c_pTs, c_pv, c_pvs, c_oT, c_o,
         c_oqTp, c_oqTs, c_op, c_x3) = (
            sem("c_" + n) for n in "xq xqTp xqTs qp q qTp qTs s sm nm p pTp pTs pv pvs oT o oqTp oqTs op x3".split())
        (d_h, d_xn, d_vo, d_vofree, d_qkp, d_qs, d_s, d_sm, d_nm, d_e, d_p, d_pTp, d_pTs, d_a, d_as) = (
            sem("d_" + n) for n in "h xn vo vofree qkp qs s sm nm e p pTp pTs a as".split())
        (e_x2, e_x2Tp, e_x2Ts, e_lg, e_lgs, e_ex, e_w, e_wTp, e_wTs, e_gu, e_wb, e_th, e_gud, e_act, e_dn, e_acc, e_yT,
         e_yt, e_out, e_prod, e_hi) = (
            sem("e_" + n) for n in "x2 x2Tp x2Ts lg lgs ex w wTp wTs gu wb th gud act dn acc yT yt out prod hi".split())
        w_hi, w_lo, d_xT2, d_qh, d_ah, trib_ready, d_op, d_added = (sem(n) for n in "w_hi w_lo d_xT2 d_qh d_ah trib_ready d_op d_added".split())

        NV = TB * (NH * HD // 512)
        VO = {}

        def vo_step(i, late):
            b, h = divmod(i, NH)
            if late:
                at = {7: ("X", 0), 8: ("X", 1), 9: ("G", 0), 10: ("G", 1), 15: ("W", 1)}
                return [(at[h][0], b - 1, at[h][1])] if b >= 1 and h in at else []
            if i == 0:
                return [(kind, 0, u) for kind in "TV" for u in range(TB)]
            todo = [("V", c, u) for c in range(B) for u in range(NV) if i == NH * c + 2 * u - 2]
            if b + 1 < B and h in (11, 13):
                todo.append(("T", b + 1, (h - 11) // 2))
            if b >= 1 and h == 15:
                todo.append(("W", b - 1, 0))
            return todo

        def vo_plan():
            order = [key for i in range(STEPS) for late in (False, True) for key in vo_step(i, late)] + LATE
            for n, key in enumerate(order):
                VO[key] = n
            return order

        STEPS = B * NH + 5
        LATE_AT = {at + u: (kind, B - 1, u) for kind, at in (("X", 2), ("G", 4), ("W", 11)) for u in range(TB)}
        LATE = list(LATE_AT.values())
        LATE_END = max(LATE_AT) + 1
        VO_ORDER = vo_plan()
        VO_END = len(VO_ORDER)

        XT2 = {key[:2]: 1 + n for n, key in enumerate([key for key in VO_ORDER if key[0] in "TX"])}

        def weights_bank(n):
            return 4 + n % 2 if n > LATE_END else 4

        def vo_bank(key):
            return 5 if key in LATE else 6

        MISC = {}
        READER = {"Th": a_hTs, "Tg": a_guTs, "TxB": b_xqTs, "TqB": b_qTs, "Dn": b_x2, "TxC": c_xqTs, "qp": c_q,
                  "TqC": c_qTs, "To": c_o, "Toq": c_oqTs, "op": c_x3}

        def misc_plan():
            uses = [("Th", 0)]
            for i in range(FRONT):
                for kind, t in (("TxB", i - 1), ("TqB", i - 2), ("Tg", i), ("To", i - 5), ("Dn", i - 2), ("Toq", i - 5),
                                ("Th", i + 1), ("op", i - 5), ("TxC", i - 2), ("qp", i - 2), ("TqC", i - 2)):
                    if 0 <= t < T:
                        uses.append((kind, t))
            for n, use in enumerate(uses):
                MISC[use] = n
            return uses

        FRONT = T + 5
        MISC_USES = misc_plan()

        def misc_bank(kind, t):
            return 2 + MISC[kind, t] % 2

        block = ctx.enter_context(nc.Block())

        @block.sync
        def _(sp):
            sp.dma_start(xs[:, 0:2, :], x[:, 0:2, :]).then_inc(ld["x0"], 16)
            sp.dma_start(ctxT_sb[:, :, :], ctxT).then_inc(ld["ctx"], 16)
            sp.dma_start(xw[:, 0:2, :, :], wkT).then_inc(ld["wkv"], 16)
            sp.dma_start(xw[:, 2, :, :], wvT).then_inc(ld["wkv"], 16)
            for k, w in enumerate((w_gate, w_up, w_down)):
                sp.dma_start(wraw[:, k, :], w).then_inc(ld["raw"], 16)
            sp.dma_start(xs[:, 2:T, :], x[:, 2:T, :]).then_inc(ld["x1"], 16)
            sp.dma_start(tri[:, :], tri_d).then_inc(ld["tri"], 16)
            for i in range(2):
                sp.dma_start(maskt[:, i, :], mask[i]).then_inc(ld_mask[i], 16)
            for t in range(2, T):
                sp.wait_ge(c_sm, XH * (t - 1))
                sp.dma_start(maskt[:, t % 2, :], mask[t]).then_inc(ld_mask[t % 2], 16)
            sp.wait_ge(c_s, T * (T - TB))
            sp.dma_start(armK[:, 0:4096], kwT).then_inc(ld["kw"], 16)
            sp.wait_ge(c_s, T * T)
            sp.dma_start(armK[:, 4096:8192], qwT).then_inc(ld["qw"], 16)
            sp.wait_ge(c_pv, XG * T)
            sp.dma_start(armR[:, 16896:20992], vwT).then_inc(ld["vw"], 16)
            sp.wait_ge(c_x3, T)
            sp.dma_start(armK[:, 9216:12288], owT[:, 0:3 * PIECE]).then_inc(ld["ow"], 16)
            sp.dma_start(sel, sel_d).then_inc(ld["sel"], 16)
            for k, (lo, hi) in enumerate(LOADS):
                if k == 1:
                    sp.wait_ge(w_lo, SPLIT["v", PIECES - 1] + 1)
                    sp.dma_start(raw_piece("o", PIECES - 1), owT[:, 3 * PIECE:4 * PIECE]).then_inc(ld["ow_last"], 16)
                    sp.wait_ge(w_lo, SPLIT["o", PIECES - 1] + 1)
                    sp.wait_ge(d_vo, VO["V", B - 1, NV - 1] + 1)
                if k == 2:
                    sp.wait_ge(d_a, B * NH)
                sp.dma_start(armR[:, place[lo]:place[lo] + WCH * (hi - lo)],
                             w_moe[:, WCH * lo:WCH * hi]).then_inc(ld_moe[k], 16)
            for t in range(T):
                sp.wait_ge(e_out, t + 1)
                sp.dma_start(out[:, t, :], xs[:, t, :]).then_inc(st_out, 16)
            sp.wait_ge(st_out, 16 * T)

        @block.gpsimd
        def _(pool):
            nc.gpsimd.memset(nhalf[:, :], -0.5).then_inc(ones_ready, 1)
            nc.gpsimd.memset(ones[:, :], 1.0).then_inc(ones_ready, 1)
            pool.wait_ge(ones_ready, 2)
            keys_at = {2: (0, 0), 3: (0, 1), 4: (1, 0), 5: (1, 1), JOB["C", 3]: (2, 0), JOB["B", 5]: (2, 1),
                       JOB["C", 5]: (3, 0), JOB["B", 7]: (3, 1)}
            for k in range(JOBS):
                pool.wait_ge(pow_in, k + 1)
                nc.gpsimd.tensor_tensor(rstd[:, k:k + 1], powin[:, k:k + 1], nhalf[:, :], ALU.pow).then_inc(pow_out, 1)
                if k == 1:
                    nc.gpsimd.memset(vaug[:, :, :, :], 0.0).then_inc(vaug_zero, 1)
                    pool.wait_ge(vaug_zero, 1)
                    for j in range(XG):
                        v = vaug.rearrange("p t (g j) a -> p t g j a", j=XG)[:, :, :, j, XG * XD + j:XG * XD + j + 1]
                        nc.gpsimd.memset(v, 1.0).then_inc(vaug_zero, 1)
                if k in keys_at:
                    b, c = keys_at[k]
                    pool.wait_ge(kraw_ready, 2 * C)
                    if k == 2:
                        pool.wait_ge(ld["consts"], 32)
                    if b >= 2:
                        pool.wait_ge(c_s, T * TB * (b - 1))
                    nc.gpsimd.tensor_tensor(
                        keysm[:, b % 2, c, :, :], kraw[:, c, None, S * b:S * b + S].broadcast_to([P, 8, S]),
                        headmask[:, :, None].broadcast_to([P, 8, S]), ALU.mult).then_inc(keysm_ready, 1)

        @block.vector
        def _(dve):
            steps = [0]

            def run(ins):
                steps[0] += 1
                ins.then_inc(vec_step, 1)

            def settle():
                dve.wait_ge(vec_step, steps[0])

            def step(ins):
                run(ins)
                settle()

            V = nc.vector

            def ln_stats(job, src, eps):
                job = JOB[job]
                step(V.bn_stats(st[:, :], src))
                step(V.bn_aggr(mv[:, job, :], st[:, :]))
                V.tensor_scalar(powin[:, job:job + 1], mv[:, job, 1:2], eps, None, ALU.add).then_inc(pow_in, 1)

            def ln_norm(job, src, dst):
                job = JOB[job]
                dve.wait_ge(pow_out, job + 1)
                return V.tensor_scalar(dst, src, mv[:, job, 0:1], rstd[:, job:job + 1], ALU.subtract, ALU.mult)

            dve.wait_ge(ld["consts"], 32)
            V.tensor_copy(identb[:, :], ident[:, :]).then_inc(identb_ready, 1)
            dve.wait_ge(ld["x0"], 16)
            ln_stats(("A", 0), xs[:, 0, :], 1e-5)
            ln_stats(("A", 1), xs[:, 1, :], 1e-5)
            dve.wait_ge(ld["tok"], 16)
            step(V.tensor_copy(tok[:, :], tok_i[:, :]))
            for e in range(1, E0):
                run(V.tensor_scalar(ge[:, e - 1, :], tok[:, :], float(e * (VOCAB // E0)), None, ALU.is_ge))
            settle()
            run(V.tensor_scalar(em[:, 0, :], ge[:, 0, :], -1.0, 1.0, ALU.mult, ALU.add))
            run(V.tensor_tensor(em[:, 1, :], ge[:, 0, :], ge[:, 1, :], ALU.subtract))
            run(V.tensor_tensor(em[:, 2, :], ge[:, 1, :], ge[:, 2, :], ALU.subtract))
            run(V.tensor_copy(em[:, 3, :], ge[:, 2, :]))
            settle()
            dve.wait_ge(tg_ready, 1)
            step(V.tensor_scalar(ey[:, :, :], em[:, :, :], tg[:, 0:1], 0.5, ALU.mult, ALU.mult))
            ln_norm(("A", 0), xs[:, 0, :], hbuf[:, 0, :]).then_inc(a_h, 1)
            def values(t):
                if t == 0:
                    dve.wait_ge(vaug_zero, 1 + XG)
                    dve.wait_ge(ld["biases"], 48)
                dve.wait_ge(vproj, t + 1)
                for j in range(XG):
                    o = vaug[:, t, :, :].rearrange("p (g j) a -> p g j a", j=XG)[:, :, j, XD * j:XD * j + XD]
                    i0 = bank[6 + t % 2][:, 0:D].rearrange("p (g j d) -> p g j d", j=XG, d=XD)[:, :, j, :]
                    i1 = bvb[:, :].rearrange("p (g j d) -> p g j d", j=XG, d=XD)[:, :, j, :]
                    V.tensor_tensor(o, i0, i1, ALU.add).then_inc(v_ready, 1)

            def int8_weights():
                dve.wait_ge(ld["wqo"], 32)
                rows4 = [wqo[:, k, c, :] for k in range(2) for c in range(C)]
                for i, w in enumerate(rows4):
                    run(V.tensor_reduce(xwc[:, i, 0:1], w, AX.X, ALU.max, apply_absolute_value=True))
                settle()
                step(V.tensor_scalar(xwc[:, :, 1:2], xwc[:, :, 0:1], 1.0 / 127, 1e-8, ALU.mult, ALU.max))
                step(V.reciprocal(xwc[:, :, 2:3], xwc[:, :, 1:2]))
                for i, w in enumerate(rows4):
                    V.tensor_scalar(diag[:, i, :], ident[:, :], xwc[:, i, 1:2], None, ALU.mult).then_inc(diag_ready, 1)
                    run(V.tensor_scalar(w, w, xwc[:, i, 2:3], MAGIC, ALU.mult, ALU.add))
                settle()
                for i, w in enumerate(rows4):
                    V.tensor_scalar(xwb[:, i // C, i % C, :], w, MAGIC, None, ALU.subtract).then_inc(xwb_ready, 1)

            def ternary_scales():
                dve.wait_ge(wsum_ready, 1)
                step(V.tensor_scalar(wsc[:, :], bank[5][:, 0:3], 1.0 / (F0 * D), 1e-5, ALU.mult, ALU.add))
                run(V.tensor_scalar(thr[:, 0:3], wsc[:, :], 0.5, None, ALU.mult))
                run(V.tensor_scalar(thr[:, 3:6], wsc[:, :], -0.5, None, ALU.mult))
                settle()

            def ternary(k):
                dst = (gub[:, 0, :, :], gub[:, 1, :, :], dnb[:, :, :])[k].rearrange("p c n -> p (c n)")
                step(V.tensor_scalar(dst, wraw[:, k, :], thr[:, 3 + k:4 + k], None, ALU.is_lt))
                V.scalar_tensor_tensor(dst, wraw[:, k, :], thr[:, k:k + 1], dst, ALU.is_gt,
                                       ALU.subtract).then_inc(ternary_ready, 1)

            def int8_scales():
                dve.wait_ge(swb_psum, 1)
                V.tensor_scalar(swb[:, 0:2, :], bank[5][:, 0:256], 0.25, None, ALU.mult).then_inc(swb_ready, 1)
                V.tensor_copy(swb[:, 2:4, :], bank[5][:, 256:512]).then_inc(swb_ready, 1)
                V.tensor_scalar(bqb[:, :], bqb[:, :], 0.25, None, ALU.mult).then_inc(swb_ready, 1)

            def a_norm(t):
                if t >= 1:
                    dve.wait_ge(a_hTp, t)
                ln_norm(("A", t), xs[:, t, :], hbuf[:, 0, :]).then_inc(a_h, 1)

            def zsel(t):
                dve.wait_ge(a_z, 2 * t + 2)
                step(V.tensor_scalar(zbuf, bank[0][:, 0:D], em[:, 0, t:t + 1], None, ALU.mult))
                for e in range(1, E0):
                    ins = V.scalar_tensor_tensor(zbuf, bank[e // 2][:, D * (e % 2):D * (e % 2) + D],
                                                 em[:, e, t:t + 1], zbuf, ALU.mult, ALU.add)
                    step(ins) if e < E0 - 1 else ins.then_inc(a_zsel, 1)

            def a_gated(t):
                dve.wait_ge(a_th, t + 1)
                if t >= 1:
                    dve.wait_ge(a_guTp, t)
                step(V.scalar_tensor_tensor(gubuf, ubuf, 1.0, zbuf, ALU.add, ALU.mult))
                V.tensor_tensor(gubuf, gubuf, zbuf, ALU.mult).then_inc(a_gu, 1)

            def x1(t):
                dve.wait_ge(a_y, t + 1)
                for e in range(E0):
                    ins = V.scalar_tensor_tensor(xs[:, t, :], bank[e // 2][:, D * (e % 2):D * (e % 2) + D],
                                                 ey[:, e, t:t + 1], xs[:, t, :], ALU.mult, ALU.add)
                    step(ins) if e < E0 - 1 else ins.then_inc(a_x1, 1)

            def quant_scale(h, cols, eps_op, eps):
                step(V.tensor_reduce(cols[:, 0:1], h, AX.X, ALU.max, apply_absolute_value=True))
                step(V.tensor_scalar(cols[:, 1:2], cols[:, 0:1], 1.0 / 127, eps, ALU.mult, eps_op))
                step(V.reciprocal(cols[:, 2:3], cols[:, 1:2]))

            def quant_round(h, cols, dst):
                step(V.tensor_scalar(h, h, cols[:, 2:3], MAGIC, ALU.mult, ALU.add))
                return V.tensor_scalar(dst, h, MAGIC, None, ALU.subtract)

            def b_front(t):
                h = hbuf[:, 1, :]
                dve.wait_ge(a_x1, t + 1)
                ln_stats(("B", t), xs[:, t, :], 1e-5)
                step(ln_norm(("B", t), xs[:, t, :], h))
                quant_scale(h, cb[:, t, :], ALU.add, 1e-5)
                run(V.tensor_scalar(cb[:, t, 3:4], wsc[:, 0:1], cb[:, t, 1:2], 0.5, ALU.mult, ALU.mult))
                run(V.tensor_scalar(cb[:, t, 4:5], wsc[:, 1:2], cb[:, t, 1:2], None, ALU.mult))
                if t >= 1:
                    dve.wait_ge(b_xqTp, t)
                quant_round(h, cb[:, t, :], qb[:, 0, :]).then_inc(b_xq, 1)
                step(V.tensor_tensor(cb[:, t, 5:6], cb[:, t, 3:4], cb[:, t, 4:5], ALU.mult))

            def b_hidden(t, j):
                n = 2 * t + j
                dve.wait_ge(b_th, n + 1)
                step(V.scalar_tensor_tensor(thB[:, j, :], thB[:, j, :], 1.0, bank[0][:, :], ALU.add, ALU.mult))
                V.tensor_tensor(pB[:, 512 * j:512 * j + 512], thB[:, j, :], bank[1][:, :], ALU.mult).then_inc(b_p, 1)

            def b_quant(t):
                dve.wait_ge(b_p, 2 * t + 2)
                col = cb[:, t, :]
                step(V.tensor_reduce(col[:, 6:7], pB, AX.X, ALU.max, apply_absolute_value=True))
                step(V.tensor_scalar(col[:, 6:7], col[:, 6:7], col[:, 5:6], 1.0 / 127, ALU.mult, ALU.mult))
                step(V.tensor_scalar(col[:, 6:7], col[:, 6:7], 1e-5, None, ALU.add))
                step(V.reciprocal(col[:, 7:8], col[:, 6:7]))
                run(V.tensor_scalar(col[:, 7:8], col[:, 7:8], col[:, 5:6], None, ALU.mult))
                step(V.tensor_scalar(col[:, 0:1], col[:, 6:7], wsc[:, 2:3], tg[:, 2:3], ALU.mult, ALU.mult))
                step(V.tensor_scalar(pB, pB, col[:, 7:8], MAGIC, ALU.mult, ALU.add))
                if t >= 1:
                    dve.wait_ge(b_qTp, t)
                V.tensor_scalar(qB, pB, MAGIC, None, ALU.subtract).then_inc(b_q, 1)

            def b_back(t):
                dve.wait_ge(b_d, t + 1)
                V.scalar_tensor_tensor(xs[:, t, :], bank[misc_bank("Dn", t)][:, 0:D], cb[:, t, 0:1], xs[:, t, :],
                                       ALU.mult, ALU.add).then_inc(b_x2, 1)

            def c_front(t):
                h = hbuf[:, 2, :]
                dve.wait_ge(b_x2, t + 1)
                ln_stats(("C", t), xs[:, t, :], 1e-5)
                if t >= 1:
                    dve.wait_ge(c_qTp, t)
                step(ln_norm(("C", t), xs[:, t, :], h))
                quant_scale(h, cc[:, t, :], ALU.max, 1e-8)
                if t >= 1:
                    dve.wait_ge(c_xqTp, t)
                quant_round(h, cc[:, t, :], qb[:, 1, :]).then_inc(c_xq, 1)

            def c_query(t):
                dve.wait_ge(c_qp, t + 1)
                dve.wait_ge(c_xq, t + 1)
                h = hbuf[:, 2, :]
                step(V.scalar_tensor_tensor(h, bank[misc_bank("qp", t)][:, 0:D], cc[:, t, 1:2],
                                            swb[:, 0:2, :].rearrange("p a n -> p (a n)"), ALU.mult, ALU.mult))
                V.tensor_tensor(h, h, bqb[:, :], ALU.add).then_inc(c_q, 1)

            def c_scores(t, k):
                if k == 0:
                    dve.wait_ge(ld_mask[t % 2], 16 * (t // 2 + 1))
                    if t >= 2:
                        dve.wait_ge(c_pTp, T * (t - 1))
                dve.wait_ge(c_s, T * t + k + 1)
                for i in range(2):
                    h = 2 * k + i
                    V.tensor_tensor_reduce(
                        out=scores[:, t % 2, h, :], in0=bank[SB[k % 2]][:, S * i:S * i + S], in1=maskt[:, t % 2, :],
                        scale=1.0, scalar=NEG, op0=ALU.add, op1=ALU.max,
                        accum_out=mxC[:, t % 2, h:h + 1]).then_inc(c_sm, 1)
                if k % 2 == 1:
                    dve.wait_ge(c_sm, XH * t + 2 * k + 2)
                    V.tensor_scalar(nmC[:, t % 2, 2 * k - 2:2 * k + 2], mxC[:, t % 2, 2 * k - 2:2 * k + 2], -1.0,
                                    None, ALU.mult).then_inc(c_nm, 1)

            def c_out(t):
                dve.wait_ge(c_oT, t + 1)
                o4 = bank[misc_bank("To", t)][:, 0:XG * XA].rearrange("p (g a) -> p g a", g=XG)
                step(V.reciprocal(rdC[:, :].rearrange("p (g j) -> p g j", g=XG), o4[:, :, XG * XD:XA]))
                for g in range(XG):
                    run(V.tensor_tensor(obuf[:, 64 * g:64 * g + 64].rearrange("p (j d) -> p j d", d=XD),
                                        o4[:, g, 0:XG * XD].rearrange("p (j d) -> p j d", d=XD),
                                        rdC[:, 4 * g:4 * g + 4, None].broadcast_to([P, XG, XD]), ALU.mult))
                settle()
                quant_scale(obuf, cc[:, t, 4:8], ALU.max, 1e-8)
                quant_round(obuf, cc[:, t, 4:8], oq[:, :]).then_inc(c_o, 1)

            def c_back(t):
                dve.wait_ge(c_op, t + 1)
                step(V.scalar_tensor_tensor(obuf, bank[misc_bank("op", t)][:, 0:D], cc[:, t, 5:6],
                                            swb[:, 2:4, :].rearrange("p a n -> p (a n)"), ALU.mult, ALU.mult))
                step(V.tensor_tensor(obuf, obuf, bob[:, :], ALU.add))
                V.scalar_tensor_tensor(xs[:, t, :], obuf, tg[:, 1:2], xs[:, t, :], ALU.mult,
                                       ALU.add).then_inc(c_x3, 1)

            def d_stats(t):
                ln_stats(("D", t), xs[:, t, :], 1e-5)

            def d_square(t):
                j = JOB["R", t]
                if t < TB:
                    dve.wait_ge(a_hTp, T)
                    dve.wait_ge(b_xqTp, T)
                else:
                    dve.wait_ge(d_vo, VO["T", t // TB - 1, t % TB] + 1)
                step(ln_norm(("D", t), xs[:, t, :], hid[:, t, :]))
                step(V.tensor_tensor_reduce(out=hbuf[:, t % TB, :], in0=hid[:, t, :], in1=hid[:, t, :],
                                            scale=1.0 / D, scalar=0.0, op0=ALU.mult, op1=ALU.add,
                                            accum_out=mv[:, j, 1:2]))
                V.tensor_scalar(powin[:, j:j + 1], mv[:, j, 1:2], 1e-6, None, ALU.add).then_inc(pow_in, 1)

            def d_scale(t):
                j = JOB["R", t]
                dve.wait_ge(pow_out, j + 1)
                V.tensor_scalar(hbuf[:, t % TB, :], hid[:, t, :], rstd[:, j:j + 1], None, ALU.mult).then_inc(d_xn, 1)

            def vo_read(key):
                kind, b, u = key
                n = VO[key]
                p = vo_bank(key)
                t = TB * b + u
                if kind != "W":
                    dve.wait_ge(d_vo, n + 1)
                if kind in "TX":
                    if n == 0:
                        dve.wait_ge(ld["ln"], 32)
                    w = ln1_sb if kind == "T" else ln2_sb
                    run(V.tensor_scalar(ctxT_sb[:, 0, P * t:P * t + P], bank[p][:, 0:P], w[:, 0:1], None, ALU.mult))
                    V.tensor_scalar(ctxT_sb[:, 1, P * t:P * t + P], bank[p][:, P:2 * P], w[:, 1:2], None,
                                    ALU.mult).then_inc(d_vofree, 1)
                    dve.wait_ge(d_vofree, n + 1)
                    full, hi, lo = (a[:, :, P * t:P * t + P] for a in (ctxT_sb, xT2[:, 0], xT2[:, 1]))
                    step(V.tensor_scalar(hi, full, XSCALE, None, ALU.mult))
                    V.scalar_tensor_tensor(lo, full, XSCALE, hi, ALU.mult, ALU.subtract).then_inc(d_xT2, 1)
                elif kind == "V":
                    q, l = divmod(u, TB)
                    V.tensor_scalar(vals[:, b % 2, l, 512 * q:512 * q + 512], bank[p][:, :], 1 / (XSCALE * WSCALE),
                                    None, ALU.mult).then_inc(d_vofree, 1)
                elif kind == "G":
                    L = lg[:, u, :, :]
                    step(V.tensor_reduce(L[:, 0, 8:9], bank[p][:, 0:E1], AX.X, ALU.max, negate=True))
                    V.tensor_scalar(L[:, 1, :], bank[p][:, 0:E1], L[:, 0, 8:9], None, ALU.add).then_inc(d_vofree, 1)
                else:
                    dve.wait_ge(e_w, t + 1)
                    dve.wait_ge(ld["sel"], 16)
                    dve.wait_ge(d_vo, n + 1)
                    V.tensor_copy(wTb[:, P * t:P * t + P], halfs(p)[0:3 * E1, 0:P]).then_inc(d_vofree, 1)

            def split_lo(kind, n):
                w = split_piece(kind, n)
                dve.wait_ge(w_hi, SPLIT[kind, n] + 1)
                V.scalar_tensor_tensor(w[:, 1, :], raw_piece(kind, n), WSCALE, w[:, 0, :], ALU.mult,
                                       ALU.subtract).then_inc(w_lo, 1)

            int8_weights()
            for i in range(FRONT):
                a, g, m, s, o = (0 <= i - n < T for n in (0, 1, 2, 3, 5))
                if a:
                    zsel(i)
                if s:
                    c_scores(i - 3, 0)
                if i in (1, 2):
                    values(T // 2 * (i - 1) + 0)
                if a:
                    a_gated(i)
                if g:
                    b_hidden(i - 1, 0)
                if s:
                    c_scores(i - 3, 1)
                if i in (1, 2):
                    values(T // 2 * (i - 1) + 1)
                if o:
                    c_out(i - 5)
                if i == FRONT - 1:
                    for u in range(TB):
                        vo_read(("T", 0, u))
                if s:
                    c_scores(i - 3, 2)
                if i in (1, 2):
                    values(T // 2 * (i - 1) + 2)
                if m:
                    b_back(i - 2)
                    c_front(i - 2)
                if i + 1 < T:
                    a_norm(i + 1)
                if i == 0:
                    ternary_scales()
                    ternary(0)
                    ternary(1)
                if a:
                    x1(i)
                if s:
                    c_scores(i - 3, 3)
                if i in (1, 2):
                    values(T // 2 * (i - 1) + 3)
                if o:
                    c_back(i - 5)
                if g:
                    b_hidden(i - 1, 1)
                if s:
                    c_scores(i - 3, 4)
                if i in (FRONT - 4, FRONT - 3):
                    split_lo("k", 2 * (i - FRONT + 4))
                if m:
                    c_query(i - 2)
                if s:
                    c_scores(i - 3, 5)
                if a:
                    b_front(i)
                if s:
                    c_scores(i - 3, 6)
                if i == 0:
                    dve.wait_ge(ld["x1"], 16)
                if g:
                    b_quant(i - 1)
                if i == 1:
                    ternary(2)
                    int8_scales()
                if s:
                    c_scores(i - 3, 7)
                if i in (FRONT - 4, FRONT - 3):
                    split_lo("k", 2 * (i - FRONT + 4) + 1)
                if i + 2 < T:
                    ln_stats(("A", i + 2), xs[:, i + 2, :], 1e-5)
                if i == FRONT - 3:
                    for stage in (d_stats, d_square, d_scale):
                        for u in range(TB):
                            stage(u)
                if i == FRONT - 1:
                    split_lo("q", 0)

            def d_softmax(g):
                r = g % 2
                dve.wait_ge(d_s, g + 1)
                run(V.tensor_reduce(mxD[:, r, 0:1], bank[2 + r][:, 0:P], AX.X, ALU.max))
                step(V.tensor_reduce(mxD[:, r, 1:2], bank[2 + r][:, P:3 * P], AX.X, ALU.max))
                V.tensor_scalar(nmD[:, r, :], mxD[:, r, :], -SCALE / QSCALE ** 2, None, ALU.mult).then_inc(d_nm, 1)

            def d_normalise(g):
                r = g % 2
                dve.wait_ge(d_e, 2 * g + 2)
                step(V.reciprocal(riD[:, r, :], rsD[:, r, :]))
                run(V.tensor_scalar(probD[:, r, 0:P], probD[:, r, 0:P], riD[:, r, 0:1], None, ALU.mult))
                V.tensor_scalar(probD[:, r, P:3 * P], probD[:, r, P:3 * P], riD[:, r, 1:2], None,
                                ALU.mult).then_inc(d_p, 1)

            def d_qk_lo(g):
                dve.wait_ge(d_qh, g + 1)
                V.scalar_tensor_tensor(qk[:, g % 2, 1, :], bank[g % 2][:, :], QSCALE / (XSCALE * WSCALE),
                                       qk[:, g % 2, 0, :], ALU.mult, ALU.subtract).then_inc(d_qs, 1)

            def d_attn_lo(g):
                dve.wait_ge(d_ah, g + 1)
                V.scalar_tensor_tensor(attnT[:, g % 2, 1, :], bank[5][:, 0:S], QSCALE, attnT[:, g % 2, 0, :],
                                       ALU.mult, ALU.subtract).then_inc(d_as, 1)

            def d_add(b):
                dve.wait_ge(d_op, NH * (b + 1))
                for u in range(TB):
                    ins = V.scalar_tensor_tensor(hid[:, TB * b + u, :], bank[7][:, D * u:D * u + D],
                                                 1 / (QSCALE * WSCALE), hid[:, TB * b + u, :], ALU.mult, ALU.add)
                    run(ins) if u < TB - 1 else ins.then_inc(d_added, 1)
                dve.wait_ge(d_added, b + 1)

            def e_square(t):
                j = JOB["E", t]
                if t >= TB:
                    dve.wait_ge(d_vo, VO["X", t // TB - 1, t % TB] + 1)
                step(V.tensor_tensor_reduce(out=x2buf[:, t % TB, :], in0=hid[:, t, :], in1=hid[:, t, :], scale=1.0 / D,
                                            scalar=0.0, op0=ALU.mult, op1=ALU.add, accum_out=mv[:, j, 1:2]))
                V.tensor_scalar(powin[:, j:j + 1], mv[:, j, 1:2], 1e-6, None, ALU.add).then_inc(pow_in, 1)

            def e_scale(t):
                j = JOB["E", t]
                dve.wait_ge(pow_out, j + 1)
                V.tensor_scalar(x2buf[:, t % TB, :], hid[:, t, :], rstd[:, j:j + 1], None, ALU.mult).then_inc(e_x2, 1)

            def e_route(t):
                r = t % 2
                L = lg[:, r, :, :]
                mx8, pr, keep, w, r1, r2 = (L[:, i, :] for i in range(6))
                dve.wait_ge(e_ex, t + 1)
                step(V.tensor_reduce(mx8[:, 9:10], pr, AX.X, ALU.add))
                step(V.reciprocal(mx8[:, 10:11], mx8[:, 9:10]))
                step(V.tensor_scalar(pr, pr, mx8[:, 10:11], None, ALU.mult))
                step(V.max(mx8[:, 0:8], pr))
                step(V.memset(mx8[:, TOPK:8], 2.0))
                step(V.match_replace(out=keep, in_to_replace=mx8[:, 0:8], in_values=pr, imm_value=-1.0))
                step(V.tensor_scalar(keep, keep, 0.0, None, ALU.is_lt))

            def e_weights(t):
                r = t % 2
                L = lg[:, r, :, :]
                mx8, pr, keep, w, r1, r2 = (L[:, i, :] for i in range(6))
                step(V.tensor_tensor(w, keep, pr, ALU.mult))
                step(V.tensor_reduce(mx8[:, 9:10], w, AX.X, ALU.add))
                step(V.reciprocal(mx8[:, 10:11], mx8[:, 9:10]))
                step(V.tensor_scalar(w, w, mx8[:, 10:11], None, ALU.mult))
                if t >= 2:
                    dve.wait_ge(d_vo, VO["W", t // TB - 1, r] + 1)
                step(V.tensor_copy(lw[:, r, 0:E1], w))
                step(V.tensor_tensor(r1, w, lw[:, r, 0:E1], ALU.subtract))
                step(V.tensor_copy(lw[:, r, E1:2 * E1], r1))
                step(V.tensor_tensor(r2, r1, lw[:, r, E1:2 * E1], ALU.subtract))
                V.tensor_copy(lw[:, r, 2 * E1:3 * E1], r2).then_inc(e_w, 1)

            dve.wait_ge(ld["tri"], 16)
            V.tensor_copy(trib[:, :], tri[:, :]).then_inc(trib_ready, 1)
            G = B * NH
            for i in range(STEPS):
                b, h = divmod(i, NH)
                if 4 <= i < G + 4:
                    d_attn_lo(i - 4)
                if i == 0:
                    d_qk_lo(0)
                    split_lo("v", 0)
                    split_lo("v", 1)
                for key in vo_step(i, False):
                    if key[:2] != ("T", 0):
                        vo_read(key)
                if 1 <= i <= G:
                    d_softmax(i - 1)
                if 1 <= i < G:
                    d_qk_lo(i)
                for key in vo_step(i, True):
                    vo_read(key)
                if 1 <= i <= G:
                    d_normalise(i - 1)
                if i in SPLIT_AT:
                    split_lo(*SPLIT_AT[i])
                for u in range(TB):
                    before, after = TB * (b - 1) + u, TB * (b + 1) + u
                    if b >= 1 and h in (5, 6):
                        (e_square, e_scale)[h - 5](before)
                    if b + 1 < B and h in (u, 2 + u, 4 + u):
                        (d_stats, d_square, d_scale)[h // 2](after)
                    if b >= 1 and h in (11 + u, 13 + u):
                        (e_route, e_weights)[(h - 11) // 2](before)
                if b >= 1 and h == 4:
                    d_add(b - 1)

            for n in range(2 * CH):
                half, c = divmod(n, CH)
                r, rows = n % 2, P if c < CH - 1 else LAST
                g = thE[0:rows, r, :]
                dve.wait_ge(e_th, n + 1)
                step(V.scalar_tensor_tensor(g, g, 1.0, bank[2 * r][0:rows, :], ALU.add, ALU.mult))
                if c < ROUTED:
                    V.tensor_tensor(g, g, bank[2 * r + 1][0:rows, :], ALU.mult).then_inc(e_gud, 1)
                    dve.wait_ge(e_gud, n + 1)
                    dve.wait_ge(e_wb, half * ROUTED + c + 1)
                    V.tensor_tensor(g, g, bank[weights_bank(n)][:, :], ALU.mult).then_inc(e_prod, 1)
                else:
                    V.scalar_tensor_tensor(g, g, ASCALE, bank[2 * r + 1][0:rows, :], ALU.mult,
                                           ALU.mult).then_inc(e_gud, 1)
                if EARLY <= n + AHEAD < CH:
                    split_lo("moe", n + AHEAD)
                for u in range(TB):
                    t = T - TB + u
                    if n in (0, 1):
                        (e_square, e_scale)[n](t)
                    if n in (7 + u, 9 + u):
                        (e_route, e_weights)[(n - 7) // 2](t)
                if n in LATE_AT:
                    vo_read(LATE_AT[n])
                dve.wait_ge(e_hi, n + 1)
                V.tensor_tensor(actE[0:rows, r, 1, :], g, actE[0:rows, r, 0, :], ALU.subtract).then_inc(e_act, 1)
            for t in range(T):
                dve.wait_ge(e_yt, t + 1)
                step(V.scalar_tensor_tensor(hid[:, t, :], bank[t % 2][:, 0:D], YSCALE, hid[:, t, :], ALU.mult, ALU.add))
                V.scalar_tensor_tensor(xs[:, t, :], hid[:, t, :], tg[:, 3:4], xs[:, t, :], ALU.mult,
                                       ALU.add).then_inc(e_out, 1)

        @block.scalar
        def _(act):
            A = nc.scalar
            for dst, src, n in ((ident[:, :], ident_d, "consts"), (headmask[:, :], headmask_d, "consts"),
                                (gcol[:, :], gates, "gates"), (bk_sb[:, :], bkc, "cols"), (tok_i[:, :], itok, "tok"),
                                (hid[:, 0:2, :], wq, "wqo"), (hid[:, 2:4, :], wo, "wqo"),
                                (gw[:, :, :], gate_wT, "gw"), (bvb[:, :], bv, "biases"), (bqb[:, :], bq, "biases"),
                                (bob[:, :], bo, "biases"), (ln1_sb[:, :], ln1c, "ln"), (ln2_sb[:, :], ln2c, "ln"),
                                ):
                act.dma_start(dst, src).then_inc(ld[n], 16)
            act.wait_ge(ld["gates"], 16)
            A.activation(tg[:, :], gcol[:, :], ACT.Tanh).then_inc(tg_ready, 1)
            def copy(dst, src, s):
                A.copy(dst, src).then_inc(s, 1)

            def a_hT(t):
                act.wait_ge(a_hTp, t + 1)
                if t >= 1:
                    act.wait_ge(a_z, 2 * t)
                copy(hT[:, :, :], bank[misc_bank("Th", t)][:, 0:D], a_hTs)

            def a_tanh(t):
                act.wait_ge(a_zsel, t + 1)
                if t >= 1:
                    act.wait_ge(a_gu, t)
                A.activation(ubuf, zbuf, ACT.Tanh, scale=0.5).then_inc(a_th, 1)

            def a_guT(t):
                act.wait_ge(a_guTp, t + 1)
                if t >= 1:
                    act.wait_ge(a_y, t)
                copy(guT[:, :, :], bank[misc_bank("Tg", t)][:, 0:D], a_guTs)

            def b_xT(t):
                act.wait_ge(b_xqTp, t + 1)
                if t >= 1:
                    act.wait_ge(b_gu, 2 * t)
                copy(qTb[:, 0, :, :], halfs(misc_bank("TxB", t))[:, 0:D], b_xqTs)

            def b_tanh(t, j):
                n = 2 * t + j
                act.wait_ge(b_gu, n + 1)
                act.wait_ge(b_xq, t + 1)
                if n >= 2:
                    act.wait_ge(b_p, n - 1)
                A.activation(thB[:, j, :], bank[0][:, :], ACT.Tanh, scale=cb[:, t, 3:4]).then_inc(b_th, 1)

            def b_qT(t):
                act.wait_ge(b_qTp, t + 1)
                if t >= 1:
                    act.wait_ge(b_d, t)
                copy(qTB, halfs(misc_bank("TqB", t))[:, 0:F0], b_qTs)

            def c_xT(t):
                act.wait_ge(c_xqTp, t + 1)
                if t >= 1:
                    act.wait_ge(c_qp, t)
                copy(qTb[:, 1, :, :], halfs(misc_bank("TxC", t))[:, 0:D], c_xqTs)

            def c_qT(t):
                act.wait_ge(c_qTp, t + 1)
                if t >= 2:
                    act.wait_ge(c_s, T * (t - 1))
                copy(qTC[:, t % 2, :, :], bank[misc_bank("TqC", t)][:, 0:D], c_qTs)

            def c_exp(t, g):
                act.wait_ge(c_nm, XG * t + g + 1)
                for h in range(XG * g, XG * g + XG):
                    sc = scores[:, t % 2, h, :]
                    ins = A.activation(sc, sc, ACT.Exp, bias=nmC[:, t % 2, h:h + 1])
                ins.then_inc(c_p, 1)

            def c_pT(t, n):
                act.wait_ge(c_pTp, T * t + n + 1)
                if t >= 1:
                    act.wait_ge(c_pv, XG * (t - 1) + n // 2 + 1)
                copy(probT[:, 2 * n:2 * n + 2, :, :], bank[5][:, :], c_pTs)

            def c_oT_(t):
                act.wait_ge(c_pv, XG * (t + 1))
                if t >= 1:
                    act.wait_ge(c_oT, t)
                copy(oT_sb[:, :, :], bank[6][0:XA, :], c_pvs)

            def c_oqT(t):
                act.wait_ge(c_oqTp, t + 1)
                if t >= 1:
                    act.wait_ge(c_op, t)
                copy(oqT[:, :, :], halfs(misc_bank("Toq", t))[:, 0:D], c_oqTs)

            def keys():
                act.wait_ge(ld["cols"], 16)
                for k in range(2 * C):
                    c, half = divmod(k, 2)
                    act.wait_ge(kproj, k + 1)
                    A.activation(kraw[:, c, 512 * half:512 * half + 512], bank[6 + k % 2][:, :], ACT.Identity,
                                 bias=bk_sb[:, c:c + 1]).then_inc(kraw_ready, 1)

            def magnitudes():
                act.wait_ge(ld["raw"], 48)
                for k in range(3):
                    if k:
                        act.wait_ge(wabs_ready, k)
                    A.activation(armR[:, 6144:8192], wraw[:, k, :], ACT.Abs,
                                 accum_out=wsum[:, k:k + 1]).then_inc(wabs_ready, 1)

            def split_hi(kind, n):
                for k, (lo, hi) in enumerate(LOADS):
                    if (kind, n) == ("moe", lo):
                        act.wait_ge(ld_moe[k], 16)
                if kind in "kqv" and n == 0:
                    act.wait_ge(ld[kind + "w"], 16)
                if kind == "o":
                    act.wait_ge(ld["ow_last" if n == PIECES - 1 else "ow"], 16)
                if (kind, n) == ("k", 0):
                    act.wait_ge(keysm_ready, C * B)
                if (kind, n) == ("v", 0):
                    act.wait_ge(c_op, T)
                if (kind, n) == ("moe", 0):
                    act.wait_ge(d_vo, VO["V", B - 1, TB - 1] + 1)
                if SPLIT[kind, n]:
                    act.wait_ge(w_lo, SPLIT[kind, n])
                A.activation(split_piece(kind, n)[:, 0, :], raw_piece(kind, n), ACT.Copy,
                             scale=WSCALE).then_inc(w_hi, 1)

            a_hT(0)
            keys()
            for i in range(FRONT):
                a, g, m, s, r, o = (0 <= i - n < T for n in range(6))
                if g:
                    b_xT(i - 1)
                if a:
                    a_tanh(i)
                if i == 0:
                    magnitudes()
                if r:
                    c_pT(i - 4, 0)
                if g:
                    b_tanh(i - 1, 0)
                if m:
                    b_qT(i - 2)
                if r:
                    c_pT(i - 4, 1)
                if a:
                    a_guT(i)
                if r:
                    c_pT(i - 4, 2)
                if s:
                    c_exp(i - 3, 0)
                if o:
                    c_oqT(i - 5)
                if r:
                    c_pT(i - 4, 3)
                if i + 1 < T:
                    a_hT(i + 1)
                if i == 1:
                    act.wait_ge(xwT_psum, 1)
                    copy(xwT.rearrange("p k c n -> p (k c n)"), halfs(4)[:, 0:1024], xwT_ready)
                if m:
                    c_xT(i - 2)
                if g:
                    b_tanh(i - 1, 1)
                if s:
                    c_exp(i - 3, 1)
                if i in (FRONT - 4, FRONT - 3):
                    split_hi("k", 2 * (i - FRONT + 4))
                if r:
                    c_pT(i - 4, 4)
                    c_pT(i - 4, 5)
                if m:
                    c_qT(i - 2)
                if s:
                    c_exp(i - 3, 2)
                if r:
                    c_pT(i - 4, 6)
                if r:
                    c_pT(i - 4, 7)
                    c_oT_(i - 4)
                if s:
                    c_exp(i - 3, 3)
                if i in (FRONT - 4, FRONT - 3):
                    split_hi("k", 2 * (i - FRONT + 4) + 1)
                if i == FRONT - 1:
                    split_hi("q", 0)

            def route_exp(b):
                for u in range(TB):
                    act.wait_ge(d_vofree, VO["G", b, u] + 1)
                    A.activation(lg[:, u, 1, :], lg[:, u, 1, :], ACT.Exp).then_inc(e_ex, 1)

            G = B * NH
            act.wait_ge(ternary_ready, 3)
            for i in range(STEPS):
                b, h = divmod(i, NH)
                if 4 <= i < G + 4:
                    g = i - 4
                    act.wait_ge(d_a, g + 1)
                    if g >= 2:
                        act.wait_ge(d_op, g - 1)
                    A.activation(attnT[:, g % 2, 0, :], bank[5][:, 0:S], ACT.Copy, scale=QSCALE).then_inc(d_ah, 1)
                if h == 11 and b >= 1:
                    route_exp(b - 1)
                if i < G:
                    act.wait_ge(d_qkp, i + 1)
                    if i >= 2:
                        act.wait_ge(d_s, i - 1)
                    A.activation(qk[:, i % 2, 0, :], bank[i % 2][:, :], ACT.Copy,
                                 scale=QSCALE / (XSCALE * WSCALE)).then_inc(d_qh, 1)
                if i == 0:
                    split_hi("v", 0)
                    split_hi("v", 1)
                if 2 <= i < G + 2:
                    g = i - 2
                    act.wait_ge(d_pTp, g + 1)
                    if g >= 2:
                        act.wait_ge(d_a, g - 1)
                    copy(probDT[:, g % 2, :], bank[4][:, 0:3 * P], d_pTs)
                if 1 <= i < G + 1:
                    g = i - 1
                    r = g % 2
                    act.wait_ge(d_nm, g + 1)
                    if g >= 2:
                        act.wait_ge(d_pTp, g - 1)
                    A.activation(probD[:, r, 0:P], bank[2 + r][:, 0:P], ACT.Exp, bias=nmD[:, r, 0:1],
                                 scale=SCALE / QSCALE ** 2, accum_out=rsD[:, r, 0:1]).then_inc(d_e, 1)
                    A.activation(probD[:, r, P:3 * P], bank[2 + r][:, P:3 * P], ACT.Exp, bias=nmD[:, r, 1:2],
                                 scale=SCALE / QSCALE ** 2, accum_out=rsD[:, r, 1:2]).then_inc(d_e, 1)
                if i in SPLIT_AT:
                    split_hi(*SPLIT_AT[i])

            for n in range(2 * CH):
                half, c = divmod(n, CH)
                r, rows = n % 2, P if c < CH - 1 else LAST
                act.wait_ge(e_gu, n + 1)
                if n >= 2:
                    act.wait_ge(e_act, n - 1)
                A.activation(thE[0:rows, r, :], bank[2 * r][0:rows, :], ACT.Tanh,
                             scale=0.5 / (WSCALE * XSCALE)).then_inc(e_th, 1)
                if EARLY <= n + AHEAD < CH:
                    split_hi("moe", n + AHEAD)
                if n == 6:
                    route_exp(B - 1)
                if c < ROUTED:
                    act.wait_ge(e_prod, half * ROUTED + c + 1)
                else:
                    act.wait_ge(e_gud, n + 1)
                if n >= 2:
                    act.wait_ge(e_dn, n - 1)
                copy(actE[0:rows, r, 0, :], thE[0:rows, r, :], e_hi)
                if c == CH - 1:
                    act.wait_ge(e_dn, n + 1)
                    for k in range(C):
                        copy(ctxT_sb[:, k, 512 * half:512 * half + 512], bank[6 + k][:, :], e_yT)

        @block.tensor
        def _(pe):
            M = nc.tensor.matmul
            Tr = nc.tensor.transpose

            def keys():
                pe.wait_ge(ld["wkv"], 32)
                for k in range(2 * C):
                    c, half = divmod(k, 2)
                    if k >= 2:
                        pe.wait_ge(kraw_ready, k - 1)
                    for i in range(C):
                        last = M(bank[6 + k % 2][:, :], xw[:, 0, i, P * c:P * c + P],
                                 ctxT_sb[:, i, 512 * half:512 * half + 512], start=i == 0, stop=i == C - 1)
                    last.then_inc(kproj, 1)

            def values(t):
                if t < 2:
                    pe.wait_ge(kraw_ready, 3 + t)
                else:
                    pe.wait_ge(v_ready, XG * (t - 1))
                for i in range(C):
                    last = M(bank[6 + t % 2][:, 0:D], ctxT_sb[:, i, P * t:P * t + P], xw[:, 2, i, :],
                             start=i == 0, stop=i == C - 1)
                last.then_inc(vproj, 1)

            PARTS = ((0, 0), (0, 1), (1, 0))

            def misc(kind, t):
                n = MISC[kind, t]
                if n >= 2:
                    before, tile = MISC_USES[n - 2]
                    pe.wait_ge(READER[before], tile + 1)
                return misc_bank(kind, t)

            def transposes(p, src, n, identity, done):
                for c in range(n):
                    last = Tr(p[:, P * c:P * c + P], src[:, P * c:P * c + P], identity)
                last.then_inc(done, 1)

            def a_th_(t):
                p = misc("Th", t)
                pe.wait_ge(a_h, t + 1)
                transposes(bank[p], hbuf[:, 0, :], C, ident[:, :], a_hTp)

            def a_zz(t):
                pe.wait_ge(a_hTs, t + 1)
                if t >= 2:
                    pe.wait_ge(b_p, 2 * t - 2)
                elif t == 1:
                    pe.wait_ge(a_x1, 1)
                for half in range(2):
                    for i in range(C):
                        last = M(bank[half][:, :], hT[:, i, :], ctxT_sb[:, i, 512 * half:512 * half + 512],
                                 start=i == 0, stop=i == C - 1)
                    last.then_inc(a_z, 1)

            def a_tgu(t):
                p = misc("Tg", t)
                pe.wait_ge(a_gu, t + 1)
                transposes(bank[p], gubuf, C, ident[:, :], a_guTp)

            def a_yy(t):
                pe.wait_ge(a_guTs, t + 1)
                if t >= 1:
                    pe.wait_ge(b_p, 2 * t - 1)
                else:
                    pe.wait_ge(a_zsel, 1)
                for half in range(2):
                    for i in range(C):
                        last = M(bank[half][:, :], guT[:, i, :], ctxT_sb[:, i, 512 * half:512 * half + 512],
                                 start=i == 0, stop=i == C - 1)
                last.then_inc(a_y, 1)

            def b_tx(t):
                p = misc("TxB", t)
                pe.wait_ge(b_xq, t + 1)
                transposes(halfs(p), qb[:, 0, :], C, identb[:, :], b_xqTp)

            def b_gate_up(t, j):
                n = 2 * t + j
                pe.wait_ge(b_xqTs, t + 1)
                pe.wait_ge(ternary_ready, 2)
                if t + 1 < T:
                    pe.wait_ge(a_x1 if j else a_zsel, t + 2)
                if n:
                    pe.wait_ge(b_p, n)
                for k in range(2):
                    for i in range(C):
                        last = M(bank[k][:, :], qTb[:, 0, i, :], gub[:, k, i, 512 * j:512 * j + 512],
                                 start=i == 0, stop=i == C - 1)
                last.then_inc(b_gu, 1)

            def b_tq(t):
                p = misc("TqB", t)
                pe.wait_ge(b_q, t + 1)
                transposes(halfs(p), qB, FC, identb[:, :], b_qTp)

            def b_down(t):
                p = misc("Dn", t)
                pe.wait_ge(b_qTs, t + 1)
                pe.wait_ge(ternary_ready, 3)
                for c in range(FC):
                    last = M(bank[p][:, 0:D], qTB[:, c, :], dnb[:, c, :], start=c == 0, stop=c == FC - 1)
                last.then_inc(b_d, 1)

            def c_tx(t):
                p = misc("TxC", t)
                pe.wait_ge(c_xq, t + 1)
                transposes(halfs(p), qb[:, 1, :], C, identb[:, :], c_xqTp)

            def c_project(t):
                p = misc("qp", t)
                pe.wait_ge(c_xqTs, t + 1)
                pe.wait_ge(xwT_ready, 1)
                pe.wait_ge(swb_ready, 3)
                for i in range(C):
                    last = M(bank[p][:, 0:D], qTb[:, 1, i, :], xwT[:, 0, i, :], start=i == 0, stop=i == C - 1)
                last.then_inc(c_qp, 1)

            def c_tq(t):
                p = misc("TqC", t)
                pe.wait_ge(c_q, t + 1)
                transposes(bank[p], hbuf[:, 2, :], C, ident[:, :], c_qTp)

            def c_score(t, k):
                c, pair = divmod(k, 4)
                n = T * t + k
                if k == 0:
                    pe.wait_ge(c_qTs, t + 1)
                    pe.wait_ge(keysm_ready, C * (t // TB + 1))
                if n >= 2:
                    pe.wait_ge(c_sm, 2 * (n - 1))
                M(bank[SB[k % 2]][:, :], qTC[:, t % 2, c, :], keysm[:, t // TB % 2, c, 2 * pair:2 * pair + 2, :],
                  start=True, stop=True).then_inc(c_s, 1)

            def c_tp(t, n):
                m = T * t + n
                pe.wait_ge(c_p, XG * t + n // 2 + 1)
                if m >= 1:
                    pe.wait_ge(c_pTs, m)
                for i in range(4):
                    h, l = 2 * n + i // 2, i % 2
                    last = Tr(bank[5][:, P * i:P * i + P], scores[:, t % 2, h, P * l:P * l + P], ident[:, :])
                last.then_inc(c_pTp, 1)

            def c_pv_(t, g):
                pe.wait_ge(c_pTs, T * t + 2 * g + 2)
                if t == 0 and g == 0:
                    pe.wait_ge(v_ready, XG * T)
                if g == 0 and t >= 1:
                    pe.wait_ge(c_pvs, t)
                for i in range(2 * XG):
                    j, l = divmod(i, 2)
                    h = XG * g + j
                    last = M(bank[6][0:XA, P * g:P * g + P], vaug[:, TB * (t // TB) + l, h, :], probT[:, h, l, :],
                             start=i == 0, stop=i == 2 * XG - 1)
                last.then_inc(c_pv, 1)

            def c_to(t):
                p = misc("To", t)
                pe.wait_ge(c_pvs, t + 1)
                for g in range(XG):
                    last = Tr(bank[p][:, XA * g:XA * g + XA], oT_sb[:, g, :], ident[0:XA, 0:XA])
                last.then_inc(c_oT, 1)

            def c_toq(t):
                p = misc("Toq", t)
                pe.wait_ge(c_o, t + 1)
                transposes(halfs(p), oq, C, identb[:, :], c_oqTp)

            def c_outp(t):
                p = misc("op", t)
                pe.wait_ge(c_oqTs, t + 1)
                for i in range(C):
                    last = M(bank[p][:, 0:D], oqT[:, i, :], xwT[:, 1, i, :], start=i == 0, stop=i == C - 1)
                last.then_inc(c_op, 1)

            def vo_make(key):
                kind, b, u = key
                n = VO[key]
                p = vo_bank(key)
                if n:
                    pe.wait_ge(d_vofree, n)
                else:
                    pe.wait_ge(c_pvs, T)
                t = TB * b + u
                if kind in "TX":
                    pe.wait_ge(d_xn if kind == "T" else e_x2, t + 1)
                    h = hbuf[:, u, :] if kind == "T" else x2buf[:, u, :]
                    for c in range(C):
                        last = Tr(bank[p][:, P * c:P * c + P], h[:, P * c:P * c + P], ident[:, :])
                elif kind == "G":
                    pe.wait_ge(d_vofree, VO["X", b, u] + 1)
                    pe.wait_ge(ld["gw"], 16)
                    for i in range(C):
                        last = M(bank[p][:, 0:E1], ctxT_sb[:, i, P * t:P * t + P], gw[:, i, :], start=i == 0,
                                 stop=i == C - 1)
                elif kind == "W":
                    pe.wait_ge(e_w, t + 1)
                    last = Tr(halfs(p)[0:3 * E1, 0:P], lw[:, u, :], identb[:, :])
                elif kind == "V":
                    q, l = divmod(u, TB)
                    pe.wait_ge(d_xT2, XT2["T", b])
                    pe.wait_ge(w_lo, SPLIT["v", q] + 1)
                    t, w = TB * b + l, split_piece("v", q)
                    for i in range(C):
                        for m, (x_, w_) in enumerate(PARTS):
                            last = M(bank[p][:, :], xT2[:, x_, i, P * t:P * t + P], w[:, w_, 512 * i:512 * i + 512],
                                     start=i == 0 and m == 0, stop=i == C - 1 and m == 2)
                last.then_inc(d_vo, 1)

            def d_qk(g):
                b, h = divmod(g, NH)
                pe.wait_ge(d_xT2, XT2["T", b])
                if g >= 2:
                    pe.wait_ge(d_qs, g - 1)
                else:
                    pe.wait_ge(b_p, 2 * T)
                q, at = divmod(h, NH // PIECES)
                if b == 0 and at == 0:
                    pe.wait_ge(w_lo, SPLIT["q", q] + 1)
                for k, kind in enumerate("qk"):
                    for i in range(C):
                        for m, (w_, x_) in enumerate(PARTS):
                            last = M(bank[g % 2][:, S * k:S * k + S],
                                     split_piece(kind, q)[:, w_, 512 * i + HD * at:512 * i + HD * at + HD],
                                     xT2[:, x_, i, S * b:S * b + S], start=i == 0 and m == 0,
                                     stop=i == C - 1 and m == 2)
                last.then_inc(d_qkp, 1)

            pe.wait_ge(identb_ready, 1)
            a_th_(0)
            pe.wait_ge(ld["ctx"], 16)
            for i in range(FRONT):
                a, g, m, s, r, o = (0 <= i - n < T for n in range(6))

                def unit(k):
                    if s:
                        c_score(i - 3, k)
                    if i in (1, 2) and k < T // 2:
                        values(T // 2 * (i - 1) + k)
                    if r:
                        if k in (2, 4, 6):
                            c_pv_(i - 4, k // 2 - 1)
                        c_tp(i - 4, k)

                if a:
                    a_zz(i)
                if i == 0:
                    keys()
                if g:
                    b_tx(i - 1)
                if m:
                    b_tq(i - 2)
                unit(0)
                if g:
                    b_gate_up(i - 1, 0)
                unit(1)
                if a:
                    a_tgu(i)
                if o:
                    c_to(i - 5)
                unit(2)
                if m:
                    b_down(i - 2)
                if i == 0:
                    pe.wait_ge(wabs_ready, 3)
                    pe.wait_ge(ones_ready, 2)
                    M(bank[5][:, 0:3], ones[:, :], wsum[:, :], start=True, stop=True).then_inc(wsum_ready, 1)
                    pe.wait_ge(xwb_ready, 4)
                    for k in range(2):
                        for c in range(C):
                            for n in range(C):
                                at = 512 * k + D * n + P * c
                                last = Tr(halfs(4)[:, at:at + P], xwb[:, k, c, P * n:P * n + P], identb[:, :])
                    last.then_inc(xwT_psum, 1)
                if a:
                    a_yy(i)
                if i == FRONT - 1:
                    for u in range(TB):
                        vo_make(("T", 0, u))
                if o:
                    c_toq(i - 5)
                unit(3)
                if i + 1 < T:
                    a_th_(i + 1)
                if o:
                    c_outp(i - 5)
                if m:
                    c_tx(i - 2)
                if g:
                    b_gate_up(i - 1, 1)
                unit(4)
                if i == 1:
                    pe.wait_ge(diag_ready, 4)
                    pe.wait_ge(ternary_ready, 1)
                    for n in range(4):
                        last = M(bank[5][:, P * n:P * n + P], ones[:, :], diag[:, n, :], start=True, stop=True)
                    last.then_inc(swb_psum, 1)
                if m:
                    c_project(i - 2)
                unit(5)
                if m:
                    c_tq(i - 2)
                unit(6)
                unit(7)
                if r:
                    c_pv_(i - 4, XG - 1)
                if i == FRONT - 1:
                    d_qk(0)

            def d_score(g):
                pe.wait_ge(d_qs, g + 1)
                if g >= 2:
                    pe.wait_ge(d_e, 2 * g - 2)
                else:
                    pe.wait_ge(c_x3, T)
                    pe.wait_ge(trib_ready, 1)
                s, v = bank[2 + g % 2], qk[:, g % 2]
                for m, (q, k) in enumerate(PARTS):
                    M(s[:, 0:P], v[:, q, 0:P], v[:, k, S:S + P], start=m == 0, stop=False)
                M(s[:, 0:P], identb[:, :], trib[:, :], start=False, stop=True)
                for m, (q, k) in enumerate(PARTS):
                    M(s[:, P:3 * P], v[:, q, P:S], v[:, k, S:2 * S], start=m == 0, stop=False)
                M(s[:, 2 * P:3 * P], identb[:, :], trib[:, :], start=False, stop=True).then_inc(d_s, 1)

            def d_tp(g):
                pe.wait_ge(d_p, g + 1)
                if g >= 1:
                    pe.wait_ge(d_pTs, g)
                for i in range(3):
                    last = Tr(bank[4][:, P * i:P * i + P], probD[:, g % 2, P * i:P * i + P], ident[:, :])
                last.then_inc(d_pTp, 1)

            def d_pv(g):
                b, h = divmod(g, NH)
                pe.wait_ge(d_pTs, g + 1)
                pe.wait_ge(d_vofree, VO["V", b, TB * (h // (NH // PIECES)) + TB - 1] + 1)
                if g >= 1:
                    pe.wait_ge(d_as, g)
                M(bank[5][:, 0:S], vals[:, b % 2, 0, HD * h:HD * h + HD], probDT[:, g % 2, 0:S], start=True, stop=False)
                M(bank[5][:, P:S], vals[:, b % 2, 1, HD * h:HD * h + HD], probDT[:, g % 2, S:3 * P],
                  start=False, stop=True).then_inc(d_a, 1)

            def d_project(g):
                b, h = divmod(g, NH)
                pe.wait_ge(d_as, g + 1)
                q, at = divmod(h, NH // PIECES)
                if b == 0 and at == 0:
                    pe.wait_ge(w_lo, SPLIT["o", q] + 1)
                if g == 0:
                    pe.wait_ge(c_sm, XH * T)
                elif h == 0:
                    pe.wait_ge(d_added, b)
                for u in range(TB):
                    for m, (x_, w_) in enumerate(PARTS):
                        last = M(bank[7][:, D * u:D * u + D], attnT[:, g % 2, x_, P * u:P * u + P],
                                 split_piece("o", q)[:, w_, D * at:D * at + D],
                                 start=h == 0 and m == 0 and u == 0, stop=h == NH - 1 and m == 2 and u == TB - 1)
                last.then_inc(d_op, 1)

            G = B * NH
            for i in range(STEPS):
                b, h = divmod(i, NH)
                for key in vo_step(i, False):
                    if key[:2] != ("T", 0):
                        vo_make(key)
                if 1 <= i < G:
                    d_qk(i)
                if 1 <= i <= G:
                    d_score(i - 1)
                for key in vo_step(i, True):
                    vo_make(key)
                if 2 <= i <= G + 1:
                    d_tp(i - 2)
                if 3 <= i <= G + 2:
                    d_pv(i - 3)
                if 5 <= i < G + 5:
                    d_project(i - 5)

            def e_down(n):
                half, c = divmod(n, CH)
                r, rows = n % 2, P if c < CH - 1 else LAST
                pe.wait_ge(e_act, n + 1)
                if n == 0:
                    pe.wait_ge(d_added, B)
                if c == 0 and half == 1:
                    pe.wait_ge(e_yT, C)
                w = split_piece("moe", c)[0:rows, :, 4 * P:WCH]
                for k in range(C):
                    for m, (a, b) in enumerate(PARTS):
                        last = M(bank[6 + k][:, :], w[:, a, P * k:P * k + P], actE[0:rows, r, b, :],
                                 start=c == 0 and m == 0, stop=c == CH - 1 and m == 2)
                last.then_inc(e_dn, 1)

            for n in range(2 * CH):
                half, c = divmod(n, CH)
                r, rows = n % 2, P if c < CH - 1 else LAST
                if half == 0:
                    pe.wait_ge(w_lo, SPLIT["moe", n] + 1)
                if n == LATE_END + 1:
                    pe.wait_ge(d_vofree, VO_END)
                if n == 0:
                    pe.wait_ge(ld["sel"], 16)
                if n >= 2:
                    pe.wait_ge(e_gud, n - 1)
                for k in range(2):
                    for i in range(C):
                        at = 2 * P * k + P * i
                        for m, (a, b) in enumerate(PARTS):
                            last = M(bank[2 * r + k][0:rows, :], split_piece("moe", c)[:, a, at:at + rows],
                                     xT2[:, b, i, 512 * half:512 * half + 512], start=i == 0 and m == 0,
                                     stop=i == C - 1 and m == 2)
                last.then_inc(e_gu, 1)
                if c < ROUTED:
                    if 1 <= n <= LATE_END + 1:
                        pe.wait_ge(e_prod, n)
                    elif n >= 2:
                        pe.wait_ge(e_act, n - 1)
                    M(bank[weights_bank(n)][:, :], sel[:, P * c:P * c + P], wTb[:, 512 * half:512 * half + 512],
                      start=True, stop=True).then_inc(e_wb, 1)
                if n >= 1:
                    e_down(n - 1)
                if n in LATE_AT:
                    vo_make(LATE_AT[n])
            e_down(2 * CH - 1)
            for t in range(T):
                if t < 4:
                    pe.wait_ge(e_yT, C)
                else:
                    pe.wait_ge(e_yT, 2 * C)
                if t >= 2:
                    pe.wait_ge(e_out, t - 1)
                for c in range(C):
                    last = Tr(bank[t % 2][:, P * c:P * c + P], ctxT_sb[:, c, P * t:P * t + P], ident[:, :])
                last.then_inc(e_yt, 1)

def kernel(**inputs):
    import numpy as np
    import concourse.bacc as bacc
    from concourse.bass_utils import run_bass_kernel_spmd

    g = {k: np.asarray(v) for k, v in inputs.items()}

    def tiles(a):
        a = a.reshape(-1, P, a.shape[-1])
        return np.ascontiguousarray(a.transpose(1, 0, 2))

    def rows(v):
        return np.ascontiguousarray(np.broadcast_to(v.reshape(1, -1), (P, v.size)))

    def flat(a):
        return np.ascontiguousarray(a.reshape(P, -1))

    def pieces(w):
        return flat(w.reshape(4, -1, C, P).transpose(3, 0, 2, 1))

    eye = np.eye(P, dtype=np.float32)
    tri = np.where(np.tril(np.ones((P, P), bool)), 0.0, -1e9 / SCALE * QSCALE ** 2).astype(np.float32)
    heads = (np.arange(P)[:, None] // XD == np.arange(8)[None, :]).astype(np.float32)
    expert = np.arange(ROUTED * P) // I1
    sel = np.where(expert[None, :] == (np.arange(3 * E1) % E1)[:, None],
                   np.float32(ASCALE).view(np.uint32) >> 16, 0).astype(np.uint16)

    w1, w2 = g["L1_ffn_w1"], g["L1_ffn_w2"]
    sgu, sdn = g["L1_ffn_sh_gu_w"], g["L1_ffn_sh_down_w"]
    pad = np.zeros((CH * P - E1 * I1 - SHI, D), np.float32)
    up = np.concatenate([w1[:, I1:, :].reshape(-1, D), sgu[SHI:], pad])
    gate = np.concatenate([w1[:, :I1, :].reshape(-1, D), sgu[:SHI], pad])
    down = np.concatenate([w2.transpose(0, 2, 1).reshape(-1, D), sdn.T, pad])
    moe = np.zeros((P, CH, WCH), np.float32)
    for k, w in enumerate((gate, up)):
        moe[:, :, 2 * P * k:2 * P * k + 2 * P] = w.reshape(CH, P, C, P).transpose(3, 0, 2, 1).reshape(P, CH, C * P)
    moe[:, :, 4 * P:] = down.reshape(CH, P, D).transpose(1, 0, 2)

    qw = g["L1_ffn_q_w"].reshape(NH, QHD, D)[:, :HD, :].reshape(NH * HD, D)
    kv = g["L1_ffn_kv_w"]
    arrays = {
        "x": tiles(g["x"].reshape(-1, D)),
        "itok": np.ascontiguousarray(g["itok_BxS_13_99985"].reshape(T, P).T),
        "ctxT": tiles(g["ctx_2048"].reshape(-1, D).T),
        "mask": np.ascontiguousarray(g["mask_BxSxS2_ff0"].reshape(T, P, S)),
        "gates": rows(np.concatenate([g["g_xattn"], g["g_ffn"]])),
        "w_gate": flat(tiles(g["L0_ffn_w_gate"].T)),
        "w_up": flat(tiles(g["L0_ffn_w_up"].T)),
        "w_down": flat(tiles(g["L0_ffn_w_down"].T)),
        "wq": tiles(g["L1_xattn_wq"]),
        "wkT": np.ascontiguousarray(np.stack([tiles(g["L1_xattn_wk"].T)] * 2, axis=1)),
        "wvT": tiles(g["L1_xattn_wv"].T),
        "wo": tiles(g["L1_xattn_wo"]),
        "bq": rows(g["L1_xattn_bq"]),
        "bkc": np.ascontiguousarray(g["L1_xattn_bk"].reshape(C, P).T),
        "bv": rows(g["L1_xattn_bv"]),
        "bo": rows(g["L1_xattn_bo"]),
        "ln1c": np.ascontiguousarray(g["L1_ffn_ln1_w"].reshape(C, P).T),
        "ln2c": np.ascontiguousarray(g["L1_ffn_ln2_w"].reshape(C, P).T),
        "qwT": pieces(qw),
        "kwT": pieces(kv[:NH * HD]),
        "vwT": pieces(kv[NH * HD:2 * NH * HD]),
        "owT": flat(tiles(g["L1_ffn_o_w"].T)),
        "gate_wT": tiles(g["L1_ffn_gate_w"].T),
        "w_moe": moe.reshape(P, -1),
        "ident_d": eye, "tri_d": tri, "headmask_d": heads, "sel_d": sel,
    }
    nc = bacc.Bacc("TRN2", target_bir_lowering=False, num_devices=1)
    aps = {}
    for n, a in arrays.items():
        aps[n] = nc.dram_tensor("in_" + n, a.shape, mybir.dt.from_np(a.dtype), kind="ExternalInput").ap()
    aps["sel_d"] = aps["sel_d"].bitcast(mybir.dt.bfloat16)
    out = nc.dram_tensor("out_y", (P, T, D), mybir.dt.float32, kind="ExternalOutput").ap()
    flamingo(nc, out=out, **aps)
    r = run_bass_kernel_spmd(nc, [{"in_" + n: a for n, a in arrays.items()}], core_ids=[0])
    y = r.results[0]["out_y"]
    return np.ascontiguousarray(y.transpose(1, 0, 2)).reshape(B, S, D)
```

```python
import concourse.bass as bass
from concourse import mybir
from contextlib import ExitStack

P = 128
B, S, D = 4, 256, 256
T = B * S // P
TB = S // P
C = D // P
E0 = 4
VOCAB = 12500
F0 = 1024
FC = F0 // P
XH, XD = 16, 16
XG = 4
XA = XG * XD + XG
NH, HD, QHD = 16, 128, 192
E1, TOPK, I1 = 16, 4, 176
SHI = 2 * I1
ROUTED = E1 * I1 // P
CH = -(-(E1 * I1 + SHI) // P)
LAST = E1 * I1 + SHI - (CH - 1) * P
WCH = 4 * P + D
MAGIC = 12582912.0
NEG = -3.0e38
SCALE = float(QHD) ** -0.5
XSCALE, WSCALE, QSCALE, HSCALE = 2.0 ** 6, 2.0 ** 8, 2.0 ** 6, 2.0 ** 2
ASCALE = HSCALE / (WSCALE * XSCALE) ** 2
YSCALE = 0.5 / (HSCALE * WSCALE)
AHEAD = 4

def flamingo(nc, x, itok, ctxT, mask, gates, w_gate, w_up, w_down, wq, wkT, wvT, wo, bq, bk, bv, bo,
             ln1c, ln2c, qwT, kwT, vwT, owT, gate_wT, w_moe, ident_d, tri_d, sel_d, out):
    f32, bf16, fp16 = mybir.dt.float32, mybir.dt.bfloat16, mybir.dt.float16
    ALU, ACT, AX = mybir.AluOpType, mybir.ActivationFunctionType, mybir.AxisListType
    ctx = ExitStack()
    with ctx:
        def sb(name, shape, dt=f32):
            return ctx.enter_context(nc.sbuf_tensor(name, shape, dt))

        def sem(name):
            return ctx.enter_context(nc.semaphore(name))

        xs = sb("xs", [P, T, D])
        ctxT_sb = sb("ctxT_sb", [P, C, B * S])
        hid = sb("hid", [P, T, D])
        armK = sb("armK", [P, 16384])
        armR = sb("armR", [P, 20992])
        armW = sb("armW", [P, 3072])
        xw8 = sb("xw8", [P, 4 * C * D // 2])
        keysT = armK[:, 0:8192].bitcast(fp16).rearrange("p (b k j n) -> p b k j n", b=B, k=XH // 2, j=2)
        bkb = armK[:, 8192:8448]
        stage = armK[:, 9216:10240].bitcast(fp16).rearrange("p (w n) -> p w n", w=2)
        kstage, qstage = stage[:, 0, :], stage[:, 1, :]
        temps = armK[:, 10240:16384]
        zbuf, ubuf, gubuf = (temps[:, 256 * i:256 * i + 256] for i in range(3))
        obuf = temps[:, 768:1024]
        thB = temps[:, 1024:2048].rearrange("p (j n) -> p j n", j=2)
        pB = temps[:, 2048:3072]
        qB = temps[:, 3072:3584].bitcast(bf16)
        qTB = temps[:, 3584:4096].bitcast(bf16).rearrange("p (c n) -> p c n", c=FC)
        oT_sb = temps[0:XA, 4096:4608].rearrange("p (g n) -> p g n", g=XG)
        oq = temps[:, 4608:4736].bitcast(bf16)
        oqT = temps[:, 4736:4864].bitcast(bf16).rearrange("p (c n) -> p c n", c=C)
        qTC = temps[:, 4864:5888].bitcast(fp16).rearrange("p (r k n) -> p r k n", r=2, k=XH // 2)
        guT = temps[:, 5888:6144].rearrange("p (c n) -> p c n", c=C)
        sel = armK[0:3 * E1, 14336:14336 + ROUTED * P // 2].bitcast(bf16)
        wTb = armK[0:3 * E1, 15744:15744 + T * P // 2].bitcast(bf16)
        xT2 = armK[:, 12288:14336].bitcast(fp16).rearrange("p (k c n) -> p k c n", k=2, c=C)
        scores = armR[:, 0:8192].rearrange("p (r h s) -> p r h s", r=2, h=XH)
        vaug = armR[:, 8192:8192 + T * XH * XA].rearrange("p (t h a) -> p t h a", t=T, h=XH)
        probT = armR[:, 16896:20992].rearrange("p (h l n) -> p h l n", h=XH, l=TB)
        wraw = armR[:, 0:6144].rearrange("p (k n) -> p k n", k=3)
        xw = armR[:, 18944:20992].rearrange("p (k c n) -> p k c n", k=4, c=C)
        vals = armR[:, 0:8192].rearrange("p (r l n) -> p r l n", r=2, l=TB)
        attnT = armR[:, 8192:8704].bitcast(fp16).rearrange("p (r k n) -> p r k n", r=2, k=2)
        x2buf = armW[:, 2560:3072].rearrange("p (u n) -> p u n", u=TB)
        EARLY, FIRST = 10, 15
        SB = (4, 7)
        LOADS = ((0, EARLY), (EARLY, FIRST), (FIRST, 20), (20, CH))
        place = ([8704 + WCH * c for c in range(EARLY)] + [16896 + WCH * c for c in range(FIRST - EARLY)]
                 + [WCH * c for c in range(CH - FIRST)])

        PIECE = 4 * D
        PIECES = 4096 // PIECE
        PLACES = {}
        for n in range(PIECES):
            PLACES["k", n] = (armK, PIECE * n), (armK, PIECE * (n - 1) if n else 8192)
            PLACES["q", n] = (armK, 4096 + PIECE * n), (armK, 4096 + PIECE * (n - 1))
            PLACES["v", n] = (armR, 16896 + PIECE * n), (armR, 16896 + PIECE * (n - 1)) if n else (xw8, 0)
            PLACES["o", n] = ((armK, 9216 + PIECE * n) if n < 3 else (armR, 19968),
                              (armK, 9216 + PIECE * (n - 1) if n else 7168))
        for n in range(CH):
            PLACES["moe", n] = (armR, place[n]), (armR, place[n - 1]) if n else (xw8, 0)
        ORDER = ([("k", n) for n in range(PIECES)] + [("q", 0)] + [("v", n) for n in range(PIECES)]
                 + [("q", n) for n in range(1, PIECES)] + [("o", n) for n in range(PIECES)]
                 + [("moe", n) for n in range(CH)])
        SPLIT_AT = {0: ("v", 2), 1: ("v", 3), 2: ("q", 1), 3: ("q", 2), 4: ("q", 3),
                    5: ("o", 0), 7: ("o", 1), 9: ("o", 2), 11: ("o", 3)}
        for n in range(EARLY):
            SPLIT_AT[(B - 1) * NH + 2 + n] = ("moe", n)
        SPLIT = {key: n for n, key in enumerate(ORDER)}

        def raw_piece(kind, n):
            (arm, at), size = PLACES[kind, n][0], WCH if kind == "moe" else PIECE
            return arm[:, at:at + size]

        def split_piece(kind, n):
            (arm, at), size = PLACES[kind, n][1], WCH if kind == "moe" else PIECE
            return arm[:, at:at + size].bitcast(fp16).rearrange("p (k n) -> p k n", k=2)

        gub = armW[:, 0:2048].bitcast(bf16).rearrange("p (k c n) -> p k c n", k=2, c=C)
        dnb = armW[:, 2048:3072].bitcast(bf16).rearrange("p (c n) -> p c n", c=FC)
        qk = armW[:, 0:1024].bitcast(fp16).rearrange("p (r k n) -> p r k n", r=2, k=2)
        probD = armW[:, 1024:1792].rearrange("p (r n) -> p r n", r=2)
        probDT = armW[:, 1792:2560].rearrange("p (r n) -> p r n", r=2)
        thE = armW[:, 0:1024].rearrange("p (r n) -> p r n", r=2)
        actE = armW[:, 1024:2048].bitcast(fp16).rearrange("p (r k n) -> p r k n", r=2, k=2)

        ident = sb("ident", [P, P])
        identb = sb("identb", [P, P], bf16)
        identh = sb("identh", [P, P], fp16)
        ones = sb("ones", [P, P])
        tri = sb("tri", [P, P])
        trib = sb("trib", [P, P], bf16)
        maskt = sb("maskt", [P, 2, S])
        hbuf = sb("hbuf", [P, 3, D])
        hT = sb("hT", [P, C, P])
        qb = sb("qb", [P, 2, D], bf16)
        qTb = sb("qTb", [P, 2, C, P], bf16)
        bqb, bvb, bob = sb("bqb", [P, D]), sb("bvb", [P, D]), sb("bob", [P, D])
        swb = sb("swb", [P, 4, P])
        xwb, xwT = (xw8[:, C * D * k:C * D * k + C * D].bitcast(bf16).rearrange("p (k c n) -> p k c n", k=2, c=C)
                    for k in range(2))
        gw = sb("gw", [P, C, E1])
        tok_i = sb("tok_i", [P, T], mybir.dt.int32)
        tok = sb("tok", [P, T])
        ge = sb("ge", [P, 3, T])
        em = sb("em", [P, E0, T])
        ey = sb("ey", [P, E0, T])
        gcol, tg = sb("gcol", [P, 4]), sb("tg", [P, 4])
        ln1_sb, ln2_sb = sb("ln1_sb", [P, C]), sb("ln2_sb", [P, C])
        JOB = {}

        def ask(*keys):
            for key in keys:
                JOB[key] = len(JOB)

        ask(("A", 0), ("A", 1))
        for i in range(T + 2):
            if i >= 2:
                ask(("C", i - 2))
            if i < T:
                ask(("B", i))
            if i + 2 < T:
                ask(("A", i + 2))
        def ask_rows(b):
            ask(*((k, TB * b + u) for k in "DR" for u in range(TB)))

        ask_rows(0)
        for b in range(B + 1):
            if b + 1 < B:
                ask_rows(b + 1)
            if b >= 1:
                ask(*(("E", TB * (b - 1) + u) for u in range(TB)))
        JOBS = len(JOB)
        BIAS_AT = {JOB["B", t + 2] if t + 2 < T else JOB["C", t] + 1: t for t in range(T)}
        st, mv = sb("st", [P, 6]), sb("mv", [P, JOBS, 2])
        powin, rstd, nhalf = sb("powin", [P, JOBS]), sb("rstd", [P, JOBS]), sb("nhalf", [P, 1])
        wsum, wsc, thr = sb("wsum", [P, 3]), sb("wsc", [P, 3]), sb("thr", [P, 6])
        magic = sb("magic", [P, 1])
        cb = sb("cb", [P, T, 8])
        xwc = sb("xwc", [P, 4, 4])
        cc = sb("cc", [P, T, 8])
        mxC, nmC = sb("mxC", [P, 2, XH]), sb("nmC", [P, 2, XH])
        rdC = sb("rdC", [P, XH])
        mxD, nmD, rsD, riD = (sb(n, [P, 2, 2]) for n in ("mxD", "nmD", "rsD", "riD"))
        lg = sb("lg", [P, 2, 8, E1])
        lw = sb("lw", [P, 2, 3 * E1], bf16)

        wqo = hid[:, 0:4, :].rearrange("p (k c) n -> p k c n", k=2)
        diag = hid[:, 4:6, :].rearrange("p a (i n) -> p (a i) n", i=2)

        bank = [ctx.enter_context(nc.psum_tensor(f"bank{i}", [P, 512], f32)) for i in range(8)]

        def halfs(i):
            return bank[i][:, :].bitcast(bf16)

        names = ("x0 x1 tok gates ctx wkv consts raw biases wqo tri ln gw sel qw kw vw ow ow_last").split()
        ld = {n: sem("ld_" + n) for n in names}
        ld_mask = [sem(f"ld_mask{i}") for i in range(2)]
        ld_moe = [sem(f"ld_moe{i}") for i in range(len(LOADS))]
        st_out = sem("st_out")
        vec_step, pow_in, pow_out = sem("vec_step"), sem("pow_in"), sem("pow_out")
        identb_ready, tg_ready, ones_ready, magic_ready, trib_ready = (
            sem(n) for n in "identb_ready tg_ready ones_ready magic_ready trib_ready".split())
        vaug_zero, stage_zero, keys_zero, kproj, keys_staged, keys_T, keysT_ready, vproj, v_ready = (
            sem(n) for n in "vaug_zero stage_zero keys_zero kproj keys_staged keys_T keysT_ready vproj v_ready".split())
        wabs_ready, wsum_ready, ternary_ready, xwb_ready, xwT_psum, xwT_ready, diag_ready, swb_psum, swb_ready = (
            sem(n) for n in ("wabs_ready wsum_ready ternary_ready xwb_ready xwT_psum xwT_ready diag_ready swb_psum "
                             "swb_ready").split())
        a_h, a_hTp, a_z, a_zsel, a_th, a_gu, a_guTp, a_guTs, a_hTs, a_y, a_x1 = (
            sem("a_" + n) for n in "h hTp z zsel th gu guTp guTs hTs y x1".split())
        b_xq, b_xqTp, b_xqTs, b_gu, b_th, b_p, b_cols, b_scaled, b_q, b_qTp, b_qTs, b_d, b_x2 = (
            sem("b_" + n) for n in "xq xqTp xqTs gu th p cols scaled q qTp qTs d x2".split())
        c_xq, c_xqTp, c_xqTs, c_qp, c_qf, c_qhi, c_q, c_qTp, c_qTs, c_s, c_sm, c_nm, c_p, c_pTp, c_pTs = (
            sem("c_" + n) for n in "xq xqTp xqTs qp qf qhi q qTp qTs s sm nm p pTp pTs".split())
        c_pv, c_pvs, c_oT, c_o, c_oqTp, c_oqTs, c_op, c_biased, c_x3 = (
            sem("c_" + n) for n in "pv pvs oT o oqTp oqTs op biased x3".split())
        w_hi, w_lo = sem("w_hi"), sem("w_lo")
        d_xn, d_vo, d_vofree, d_xT2, d_qkp, d_qh, d_qs, d_s, d_nm, d_e, d_p, d_pTp, d_pTs = (
            sem("d_" + n) for n in "xn vo vofree xT2 qkp qh qs s nm e p pTp pTs".split())
        d_a, d_ah, d_as, d_op, d_added = (sem("d_" + n) for n in "a ah as op added".split())
        e_x2, e_ex, e_w, e_gu, e_gud, e_wb, e_th, e_prod, e_hi, e_act, e_dn, e_yT, e_yt, e_out = (
            sem("e_" + n) for n in "x2 ex w gu gud wb th prod hi act dn yT yt out".split())

        NV = TB * (NH * HD // 512)
        VO = {}

        def vo_step(i, late):
            b, h = divmod(i, NH)
            if late:
                at = {7: ("X", 0), 8: ("X", 1), 9: ("G", 0), 10: ("G", 1), 15: ("W", 1)}
                return [(at[h][0], b - 1, at[h][1])] if b >= 1 and h in at else []
            if i == 0:
                return [(kind, 0, u) for kind in "TV" for u in range(TB)]
            todo = [("V", c, u) for c in range(B) for u in range(NV) if i == NH * c + 2 * u - 2]
            if b + 1 < B and h in (11, 13):
                todo.append(("T", b + 1, (h - 11) // 2))
            if b >= 1 and h == 15:
                todo.append(("W", b - 1, 0))
            return todo

        def vo_plan():
            order = [key for i in range(STEPS) for late in (False, True) for key in vo_step(i, late)] + LATE
            for n, key in enumerate(order):
                VO[key] = n
            return order

        STEPS = B * NH + 5
        LATE_AT = {at + u: (kind, B - 1, u) for kind, at in (("X", 2), ("G", 4), ("W", 11)) for u in range(TB)}
        LATE = list(LATE_AT.values())
        LATE_END = max(LATE_AT) + 1
        VO_ORDER = vo_plan()
        VO_END = len(VO_ORDER)

        XT2 = {key[:2]: 1 + n for n, key in enumerate([key for key in VO_ORDER if key[0] in "TX"])}

        OUT_AT = {CH + ROUTED + t: t for t in range(CH - ROUTED)}
        OUT_NOW = len(OUT_AT)

        def weights_bank(n):
            return 4 + n % 2 if n > LATE_END else 4

        def vo_bank(key):
            return 5 if key in LATE else 6

        MISC = {}
        READER = {"Th": a_hTs, "Tg": a_guTs, "TxB": b_xqTs, "TqB": b_qTs, "Dn": b_x2, "TxC": c_xqTs, "qp": c_qf,
                  "TqC": c_qTs, "To": c_o, "Toq": c_oqTs, "op": c_x3}

        def misc_plan():
            uses = [("Th", 0)]
            for i in range(FRONT):
                for kind, t in (("TxB", i - 1), ("TqB", i - 2), ("Tg", i), ("To", i - 5), ("Dn", i - 2), ("Toq", i - 5),
                                ("Th", i + 1), ("op", i - 5), ("TxC", i - 2), ("qp", i - 2), ("TqC", i - 2)):
                    if 0 <= t < T:
                        uses.append((kind, t))
            for n, use in enumerate(uses):
                MISC[use] = n
            return uses

        FRONT = T + 5
        MISC_USES = misc_plan()

        KEY_SPLITS = range(FRONT - 6, FRONT - 2)
        KV = {}
        for i, tiles in ((1, range(0, 3)), (2, range(3, 6)), (3, range(6, 8))):
            for k, item in enumerate([("K", t) for t in tiles] + [("V", t) for t in tiles]):
                KV[i, k] = item

        def misc_bank(kind, t):
            return 2 + MISC[kind, t] % 2

        block = ctx.enter_context(nc.Block())

        @block.sync
        def _(sp):
            sp.dma_start(xs[:, 0:2, :], x[:, 0:2, :]).then_inc(ld["x0"], 16)
            sp.dma_start(ctxT_sb[:, :, :], ctxT).then_inc(ld["ctx"], 16)
            sp.dma_start(xw[:, 0, :, :], wkT).then_inc(ld["wkv"], 16)
            sp.dma_start(xw[:, 1, :, :], wvT).then_inc(ld["wkv"], 16)
            for k, w in enumerate((w_gate, w_up, w_down)):
                sp.dma_start(wraw[:, k, :], w).then_inc(ld["raw"], 16)
            sp.dma_start(xs[:, 2:T, :], x[:, 2:T, :]).then_inc(ld["x1"], 16)
            sp.dma_start(tri[:, :], tri_d).then_inc(ld["tri"], 16)
            for i in range(2):
                sp.dma_start(maskt[:, i, :], mask[i]).then_inc(ld_mask[i], 16)
            for t in range(2, T):
                sp.wait_ge(c_sm, XH * (t - 1))
                sp.dma_start(maskt[:, t % 2, :], mask[t]).then_inc(ld_mask[t % 2], 16)
                if t == T // 2 + 1:
                    sp.wait_ge(c_s, T * T // 2)
                    sp.dma_start(armK[:, 0:4096], kwT).then_inc(ld["kw"], 16)
            sp.wait_ge(c_s, T * T)
            sp.dma_start(armK[:, 4096:8192], qwT).then_inc(ld["qw"], 16)
            sp.wait_ge(c_pv, XG * T)
            sp.dma_start(armR[:, 16896:20992], vwT).then_inc(ld["vw"], 16)
            sp.wait_ge(c_x3, T)
            sp.dma_start(armK[:, 9216:12288], owT[:, 0:3 * PIECE]).then_inc(ld["ow"], 16)
            sp.dma_start(sel, sel_d).then_inc(ld["sel"], 16)
            for k, (lo, hi) in enumerate(LOADS):
                if k == 1:
                    sp.wait_ge(w_lo, SPLIT["v", PIECES - 1] + 1)
                    sp.dma_start(raw_piece("o", PIECES - 1), owT[:, 3 * PIECE:4 * PIECE]).then_inc(ld["ow_last"], 16)
                    sp.wait_ge(w_lo, SPLIT["o", PIECES - 1] + 1)
                    sp.wait_ge(d_vo, VO["V", B - 1, NV - 1] + 1)
                if k == 2:
                    sp.wait_ge(d_a, B * NH)
                sp.dma_start(armR[:, place[lo]:place[lo] + WCH * (hi - lo)],
                             w_moe[:, WCH * lo:WCH * hi]).then_inc(ld_moe[k], 16)
            for t in range(T):
                sp.wait_ge(e_out, t + 1)
                sp.dma_start(out[:, t, :], xs[:, t, :]).then_inc(st_out, 16)
            sp.wait_ge(st_out, 16 * T)

        @block.gpsimd
        def _(pool):
            nc.gpsimd.memset(magic[:, :], MAGIC).then_inc(magic_ready, 1)
            nc.gpsimd.memset(nhalf[:, :], -0.5).then_inc(ones_ready, 1)
            nc.gpsimd.memset(ones[:, :], 1.0).then_inc(ones_ready, 1)
            pool.wait_ge(ones_ready, 2)
            nc.gpsimd.memset(armK[:, 9216:10240], 0.0).then_inc(stage_zero, 1)
            for k in range(JOBS):
                pool.wait_ge(pow_in, k + 1)
                nc.gpsimd.tensor_tensor(rstd[:, k:k + 1], powin[:, k:k + 1], nhalf[:, :], ALU.pow).then_inc(pow_out, 1)
                if k in BIAS_AT:
                    t = BIAS_AT[k]
                    pool.wait_ge(swb_ready, 4)
                    pool.wait_ge(c_xq, t + 1)
                    nc.gpsimd.tensor_tensor(xs[:, t, :], xs[:, t, :], bob[:, :], ALU.add).then_inc(c_biased, 1)
                if k == 1:
                    nc.gpsimd.memset(vaug[:, :, :, :], 0.0).then_inc(vaug_zero, 1)
                    nc.gpsimd.memset(armK[:, 0:8192], 0.0).then_inc(keys_zero, 1)
                    pool.wait_ge(vaug_zero, 1)
                    for j in range(XG):
                        v = vaug.rearrange("p t (g j) a -> p t g j a", j=XG)[:, :, :, j, XG * XD + j:XG * XD + j + 1]
                        nc.gpsimd.memset(v, 1.0).then_inc(vaug_zero, 1)

        @block.vector
        def _(dve):
            steps = [0]

            def run(ins):
                steps[0] += 1
                ins.then_inc(vec_step, 1)

            def settle():
                dve.wait_ge(vec_step, steps[0])

            def step(ins):
                run(ins)
                settle()

            V = nc.vector

            def ln_stats(job, src, eps):
                job = JOB[job]
                step(V.bn_stats(st[:, :], src))
                step(V.bn_aggr(mv[:, job, :], st[:, :]))
                V.tensor_scalar(powin[:, job:job + 1], mv[:, job, 1:2], eps, None, ALU.add).then_inc(pow_in, 1)

            def ln_norm(job, src, dst):
                job = JOB[job]
                dve.wait_ge(pow_out, job + 1)
                return V.tensor_scalar(dst, src, mv[:, job, 0:1], rstd[:, job:job + 1], ALU.subtract, ALU.mult)

            dve.wait_ge(ld["consts"], 16)
            V.tensor_copy(identb[:, :], ident[:, :]).then_inc(identb_ready, 1)
            V.tensor_copy(identh[:, :], ident[:, :]).then_inc(identb_ready, 1)
            dve.wait_ge(ld["x0"], 16)
            ln_stats(("A", 0), xs[:, 0, :], 1e-5)
            ln_stats(("A", 1), xs[:, 1, :], 1e-5)
            dve.wait_ge(ld["tok"], 16)
            step(V.tensor_copy(tok[:, :], tok_i[:, :]))
            for e in range(1, E0):
                run(V.tensor_scalar(ge[:, e - 1, :], tok[:, :], float(e * (VOCAB // E0)), None, ALU.is_ge))
            settle()
            run(V.tensor_scalar(em[:, 0, :], ge[:, 0, :], -1.0, 1.0, ALU.mult, ALU.add))
            run(V.tensor_tensor(em[:, 1, :], ge[:, 0, :], ge[:, 1, :], ALU.subtract))
            run(V.tensor_tensor(em[:, 2, :], ge[:, 1, :], ge[:, 2, :], ALU.subtract))
            run(V.tensor_copy(em[:, 3, :], ge[:, 2, :]))
            settle()
            dve.wait_ge(tg_ready, 1)
            step(V.tensor_scalar(ey[:, :, :], em[:, :, :], tg[:, 0:1], 0.5, ALU.mult, ALU.mult))
            ln_norm(("A", 0), xs[:, 0, :], hbuf[:, 0, :]).then_inc(a_h, 1)
            def stacked(rows, stage, hi, lo):
                rows = rows.rearrange("p (h d) -> p h d", d=XD)
                s = stage.rearrange("p (h k d) -> p h k d", h=XH, d=XD)
                step(V.tensor_copy(s[:, :, hi, :], rows[:, :, None, :].broadcast_to([P, XH, 2, XD])))
                return V.tensor_tensor(s[:, :, lo, :], rows, s[:, :, 0, :], ALU.subtract)

            def keys(t):
                if t == 0:
                    dve.wait_ge(ld["biases"], 64)
                    dve.wait_ge(stage_zero, 1)
                dve.wait_ge(kproj, t + 1)
                step(V.tensor_tensor(obuf, bank[6][:, 0:D], bkb, ALU.add))
                if t:
                    dve.wait_ge(keys_T, t)
                stacked(obuf, kstage, slice(0, 3, 2), 1).then_inc(keys_staged, 1)

            def values(t):
                if t == 0:
                    dve.wait_ge(vaug_zero, 1 + XG)
                    dve.wait_ge(ld["biases"], 64)
                dve.wait_ge(vproj, t + 1)
                for j in range(XG):
                    o = vaug[:, t, :, :].rearrange("p (g j) a -> p g j a", j=XG)[:, :, j, XD * j:XD * j + XD]
                    i0 = bank[6][:, 0:D].rearrange("p (g j d) -> p g j d", j=XG, d=XD)[:, :, j, :]
                    i1 = bvb[:, :].rearrange("p (g j d) -> p g j d", j=XG, d=XD)[:, :, j, :]
                    V.tensor_tensor(o, i0, i1, ALU.add).then_inc(v_ready, 1)

            def keys_or_values(i, k):
                if (i, k) in KV:
                    kind, t = KV[i, k]
                    (keys if kind == "K" else values)(t)

            def int8_weights():
                dve.wait_ge(ld["wqo"], 32)
                rows4 = [wqo[:, k, c, :] for k in range(2) for c in range(C)]
                for i, w in enumerate(rows4):
                    run(V.tensor_reduce(xwc[:, i, 0:1], w, AX.X, ALU.max, apply_absolute_value=True))
                settle()
                step(V.tensor_scalar(xwc[:, :, 1:2], xwc[:, :, 0:1], 1.0 / 127, 1e-8, ALU.mult, ALU.max))
                step(V.reciprocal(xwc[:, :, 2:3], xwc[:, :, 1:2]))
                for i, w in enumerate(rows4):
                    V.tensor_scalar(diag[:, i, :], ident[:, :], xwc[:, i, 1:2], None, ALU.mult).then_inc(diag_ready, 1)
                    run(V.tensor_scalar(w, w, xwc[:, i, 2:3], MAGIC, ALU.mult, ALU.add))
                settle()
                for i, w in enumerate(rows4):
                    V.tensor_scalar(xwb[:, i // C, i % C, :], w, MAGIC, None, ALU.subtract).then_inc(xwb_ready, 1)

            def ternary_scales():
                dve.wait_ge(wsum_ready, 1)
                step(V.tensor_scalar(wsc[:, :], bank[7][:, 0:3], 1.0 / (F0 * D), 1e-5, ALU.mult, ALU.add))
                run(V.tensor_scalar(thr[:, 0:3], wsc[:, :], 0.5, None, ALU.mult))
                run(V.tensor_scalar(thr[:, 3:6], wsc[:, :], -0.5, None, ALU.mult))
                settle()

            def ternary(k):
                dst = (gub[:, 0, :, :], gub[:, 1, :, :], dnb[:, :, :])[k].rearrange("p c n -> p (c n)")
                step(V.tensor_scalar(dst, wraw[:, k, :], thr[:, 3 + k:4 + k], None, ALU.is_lt))
                V.scalar_tensor_tensor(dst, wraw[:, k, :], thr[:, k:k + 1], dst, ALU.is_gt,
                                       ALU.subtract).then_inc(ternary_ready, 1)

            def int8_scales():
                dve.wait_ge(swb_psum, 1)
                V.tensor_scalar(swb[:, 0:2, :], bank[7][:, 0:256], 0.25, None, ALU.mult).then_inc(swb_ready, 1)
                V.tensor_scalar(swb[:, 2:4, :], bank[7][:, 256:512], tg[:, 1:2], None, ALU.mult).then_inc(swb_ready, 1)
                V.tensor_scalar(bob[:, :], bob[:, :], tg[:, 1:2], None, ALU.mult).then_inc(swb_ready, 1)
                V.tensor_scalar(bqb[:, :], bqb[:, :], 0.25, None, ALU.mult).then_inc(swb_ready, 1)

            def a_norm(t):
                if t >= 1:
                    dve.wait_ge(a_hTp, t)
                ln_norm(("A", t), xs[:, t, :], hbuf[:, 0, :]).then_inc(a_h, 1)

            def zsel(t):
                dve.wait_ge(a_z, 2 * t + 2)
                step(V.tensor_scalar(zbuf, bank[0][:, 0:D], em[:, 0, t:t + 1], None, ALU.mult))
                for e in range(1, E0):
                    ins = V.scalar_tensor_tensor(zbuf, bank[e // 2][:, D * (e % 2):D * (e % 2) + D],
                                                 em[:, e, t:t + 1], zbuf, ALU.mult, ALU.add)
                    step(ins) if e < E0 - 1 else ins.then_inc(a_zsel, 1)

            def a_gated(t):
                dve.wait_ge(a_th, t + 1)
                if t >= 1:
                    dve.wait_ge(a_guTp, t)
                step(V.scalar_tensor_tensor(gubuf, ubuf, 1.0, zbuf, ALU.add, ALU.mult))
                V.tensor_tensor(gubuf, gubuf, zbuf, ALU.mult).then_inc(a_gu, 1)

            def x1(t):
                dve.wait_ge(a_y, t + 1)
                for e in range(E0):
                    ins = V.scalar_tensor_tensor(xs[:, t, :], bank[e // 2][:, D * (e % 2):D * (e % 2) + D],
                                                 ey[:, e, t:t + 1], xs[:, t, :], ALU.mult, ALU.add)
                    step(ins) if e < E0 - 1 else ins.then_inc(a_x1, 1)

            def quant_scale(h, cols, eps_op, eps):
                step(V.tensor_reduce(cols[:, 0:1], h, AX.X, ALU.max, apply_absolute_value=True))
                step(V.tensor_scalar(cols[:, 1:2], cols[:, 0:1], 1.0 / 127, eps, ALU.mult, eps_op))
                step(V.reciprocal(cols[:, 2:3], cols[:, 1:2]))

            def quant_round(h, cols, dst):
                step(V.tensor_scalar(h, h, cols[:, 2:3], MAGIC, ALU.mult, ALU.add))
                return V.tensor_scalar(dst, h, MAGIC, None, ALU.subtract)

            def b_stats(t):
                dve.wait_ge(a_x1, t + 1)
                ln_stats(("B", t), xs[:, t, :], 1e-5)

            def b_front(t):
                h = hbuf[:, 1, :]
                step(ln_norm(("B", t), xs[:, t, :], h))
                quant_scale(h, cb[:, t, :], ALU.add, 1e-5)
                run(V.tensor_scalar(cb[:, t, 3:4], wsc[:, 0:1], cb[:, t, 1:2], 0.5, ALU.mult, ALU.mult))
                run(V.tensor_scalar(cb[:, t, 4:5], wsc[:, 1:2], cb[:, t, 1:2], None, ALU.mult))
                if t >= 1:
                    dve.wait_ge(b_xqTp, t)
                quant_round(h, cb[:, t, :], qb[:, 0, :]).then_inc(b_xq, 1)
                step(V.tensor_tensor(cb[:, t, 5:6], cb[:, t, 3:4], cb[:, t, 4:5], ALU.mult))

            def b_hidden(t, j):
                n = 2 * t + j
                dve.wait_ge(b_th, n + 1)
                step(V.scalar_tensor_tensor(thB[:, j, :], thB[:, j, :], 1.0, bank[0][:, :], ALU.add, ALU.mult))
                V.tensor_tensor(pB[:, 512 * j:512 * j + 512], thB[:, j, :], bank[1][:, :], ALU.mult).then_inc(b_p, 1)

            def b_quant(t):
                dve.wait_ge(b_p, 2 * t + 2)
                col = cb[:, t, :]
                step(V.tensor_reduce(col[:, 6:7], pB, AX.X, ALU.max, apply_absolute_value=True))
                step(V.tensor_scalar(col[:, 6:7], col[:, 6:7], col[:, 5:6], 1.0 / 127, ALU.mult, ALU.mult))
                step(V.tensor_scalar(col[:, 6:7], col[:, 6:7], 1e-5, None, ALU.add))
                step(V.reciprocal(col[:, 7:8], col[:, 6:7]))
                run(V.tensor_scalar(col[:, 7:8], col[:, 7:8], col[:, 5:6], None, ALU.mult))
                V.tensor_scalar(col[:, 0:1], col[:, 6:7], wsc[:, 2:3], tg[:, 2:3], ALU.mult,
                                ALU.mult).then_inc(b_cols, 1)

            def b_round(t):
                dve.wait_ge(b_scaled, t + 1)
                if t >= 1:
                    dve.wait_ge(b_qTp, t)
                V.tensor_scalar(qB, pB, MAGIC, None, ALU.subtract).then_inc(b_q, 1)

            def b_back(t):
                dve.wait_ge(b_d, t + 1)
                V.scalar_tensor_tensor(xs[:, t, :], bank[misc_bank("Dn", t)][:, 0:D], cb[:, t, 0:1], xs[:, t, :],
                                       ALU.mult, ALU.add).then_inc(b_x2, 1)

            def c_stats(t):
                dve.wait_ge(b_x2, t + 1)
                ln_stats(("C", t), xs[:, t, :], 1e-5)

            def c_front(t):
                h = hbuf[:, 2, :]
                if t >= 1:
                    dve.wait_ge(c_qTp, t)
                step(ln_norm(("C", t), xs[:, t, :], h))
                quant_scale(h, cc[:, t, :], ALU.max, 1e-8)
                if t >= 1:
                    dve.wait_ge(c_xqTp, t)
                quant_round(h, cc[:, t, :], qb[:, 1, :]).then_inc(c_xq, 1)

            def c_query(t):
                dve.wait_ge(c_qp, t + 1)
                dve.wait_ge(c_xq, t + 1)
                h = hbuf[:, 2, :]
                step(V.scalar_tensor_tensor(h, bank[misc_bank("qp", t)][:, 0:D], cc[:, t, 1:2],
                                            swb[:, 0:2, :].rearrange("p a n -> p (a n)"), ALU.mult, ALU.mult))
                V.tensor_tensor(h, h, bqb[:, :], ALU.add).then_inc(c_qf, 1)

            def c_query_lo(t):
                dve.wait_ge(c_qhi, t + 1)
                rows = hbuf[:, 2, :].rearrange("p (h d) -> p h d", d=XD)
                s = qstage.rearrange("p (h k d) -> p h k d", h=XH, d=XD)
                V.tensor_tensor(s[:, :, 2, :], rows, s[:, :, 0, :], ALU.subtract).then_inc(c_q, 1)

            def c_scores(t, k):
                if k == 0:
                    dve.wait_ge(ld_mask[t % 2], 16 * (t // 2 + 1))
                    if t >= 2:
                        dve.wait_ge(c_pTp, T * (t - 1))
                dve.wait_ge(c_s, T * t + k + 1)
                for i in range(2):
                    h = 2 * k + i
                    V.tensor_tensor_reduce(
                        out=scores[:, t % 2, h, :], in0=bank[SB[k % 2]][:, S * i:S * i + S], in1=maskt[:, t % 2, :],
                        scale=1.0, scalar=NEG, op0=ALU.add, op1=ALU.max,
                        accum_out=mxC[:, t % 2, h:h + 1]).then_inc(c_sm, 1)
                if k % 2 == 1:
                    dve.wait_ge(c_sm, XH * t + 2 * k + 2)
                    V.tensor_scalar(nmC[:, t % 2, 2 * k - 2:2 * k + 2], mxC[:, t % 2, 2 * k - 2:2 * k + 2], -1.0,
                                    None, ALU.mult).then_inc(c_nm, 1)

            def c_out(t):
                dve.wait_ge(c_oT, t + 1)
                o4 = bank[misc_bank("To", t)][:, 0:XG * XA].rearrange("p (g a) -> p g a", g=XG)
                step(V.reciprocal(rdC[:, :].rearrange("p (g j) -> p g j", g=XG), o4[:, :, XG * XD:XA]))
                for g in range(XG):
                    run(V.tensor_tensor(obuf[:, 64 * g:64 * g + 64].rearrange("p (j d) -> p j d", d=XD),
                                        o4[:, g, 0:XG * XD].rearrange("p (j d) -> p j d", d=XD),
                                        rdC[:, 4 * g:4 * g + 4, None].broadcast_to([P, XG, XD]), ALU.mult))
                settle()
                quant_scale(obuf, cc[:, t, 4:8], ALU.max, 1e-8)
                quant_round(obuf, cc[:, t, 4:8], oq[:, :]).then_inc(c_o, 1)

            def c_back(t):
                dve.wait_ge(c_op, t + 1)
                step(V.scalar_tensor_tensor(obuf, bank[misc_bank("op", t)][:, 0:D], cc[:, t, 5:6],
                                            swb[:, 2:4, :].rearrange("p a n -> p (a n)"), ALU.mult, ALU.mult))
                dve.wait_ge(c_biased, t + 1)
                V.tensor_tensor(xs[:, t, :], obuf, xs[:, t, :], ALU.add).then_inc(c_x3, 1)

            def d_stats(t):
                ln_stats(("D", t), xs[:, t, :], 1e-5)

            def d_square(t):
                j = JOB["R", t]
                if t < TB:
                    dve.wait_ge(a_hTp, T)
                    dve.wait_ge(b_xqTp, T)
                else:
                    dve.wait_ge(d_vo, VO["T", t // TB - 1, t % TB] + 1)
                step(ln_norm(("D", t), xs[:, t, :], hid[:, t, :]))
                step(V.tensor_tensor_reduce(out=hbuf[:, t % TB, :], in0=hid[:, t, :], in1=hid[:, t, :],
                                            scale=1.0 / D, scalar=0.0, op0=ALU.mult, op1=ALU.add,
                                            accum_out=mv[:, j, 1:2]))
                V.tensor_scalar(powin[:, j:j + 1], mv[:, j, 1:2], 1e-6, None, ALU.add).then_inc(pow_in, 1)

            def d_scale(t):
                j = JOB["R", t]
                dve.wait_ge(pow_out, j + 1)
                V.tensor_scalar(hbuf[:, t % TB, :], hid[:, t, :], rstd[:, j:j + 1], None, ALU.mult).then_inc(d_xn, 1)

            def vo_read(key):
                kind, b, u = key
                n = VO[key]
                p = vo_bank(key)
                t = TB * b + u
                if kind != "W":
                    dve.wait_ge(d_vo, n + 1)
                if kind in "TX":
                    if n == 0:
                        dve.wait_ge(ld["ln"], 32)
                    w = ln1_sb if kind == "T" else ln2_sb
                    run(V.tensor_scalar(ctxT_sb[:, 0, P * t:P * t + P], bank[p][:, 0:P], w[:, 0:1], None, ALU.mult))
                    V.tensor_scalar(ctxT_sb[:, 1, P * t:P * t + P], bank[p][:, P:2 * P], w[:, 1:2], None,
                                    ALU.mult).then_inc(d_vofree, 1)
                    dve.wait_ge(d_vofree, n + 1)
                    full, hi, lo = (a[:, :, P * t:P * t + P] for a in (ctxT_sb, xT2[:, 0], xT2[:, 1]))
                    step(V.tensor_scalar(hi, full, XSCALE, None, ALU.mult))
                    V.scalar_tensor_tensor(lo, full, XSCALE, hi, ALU.mult, ALU.subtract).then_inc(d_xT2, 1)
                elif kind == "V":
                    q, l = divmod(u, TB)
                    V.tensor_scalar(vals[:, b % 2, l, 512 * q:512 * q + 512], bank[p][:, :], 1 / (XSCALE * WSCALE),
                                    None, ALU.mult).then_inc(d_vofree, 1)
                elif kind == "G":
                    L = lg[:, u, :, :]
                    step(V.tensor_reduce(L[:, 0, 8:9], bank[p][:, 0:E1], AX.X, ALU.max, negate=True))
                    V.tensor_scalar(L[:, 1, :], bank[p][:, 0:E1], L[:, 0, 8:9], None, ALU.add).then_inc(d_vofree, 1)
                else:
                    dve.wait_ge(e_w, t + 1)
                    dve.wait_ge(ld["sel"], 16)
                    dve.wait_ge(d_vo, n + 1)
                    V.tensor_copy(wTb[:, P * t:P * t + P], halfs(p)[0:3 * E1, 0:P]).then_inc(d_vofree, 1)

            def split_lo(kind, n):
                w = split_piece(kind, n)
                dve.wait_ge(w_hi, SPLIT[kind, n] + 1)
                V.scalar_tensor_tensor(w[:, 1, :], raw_piece(kind, n), WSCALE, w[:, 0, :], ALU.mult,
                                       ALU.subtract).then_inc(w_lo, 1)

            int8_weights()
            for i in range(FRONT):
                a, g, m, s, o = (0 <= i - n < T for n in (0, 1, 2, 3, 5))
                if a:
                    zsel(i)
                if s:
                    c_scores(i - 3, 0)
                keys_or_values(i, 0)
                if a:
                    a_gated(i)
                if s:
                    c_scores(i - 3, 1)
                if o:
                    c_out(i - 5)
                keys_or_values(i, 1)
                if g:
                    b_hidden(i - 1, 0)
                if m:
                    b_back(i - 2)
                if i == FRONT - 1:
                    for u in range(TB):
                        vo_read(("T", 0, u))
                if m:
                    c_stats(i - 2)
                if s:
                    c_scores(i - 3, 2)
                keys_or_values(i, 2)
                if i + 1 < T:
                    a_norm(i + 1)
                if i == 0:
                    ternary_scales()
                    ternary(0)
                    ternary(1)
                if m:
                    c_front(i - 2)
                if a:
                    x1(i)
                if s:
                    c_scores(i - 3, 3)
                if a:
                    b_stats(i)
                if o:
                    c_back(i - 5)
                keys_or_values(i, 3)
                if g:
                    b_hidden(i - 1, 1)
                if m:
                    c_query(i - 2)
                if s:
                    c_scores(i - 3, 4)
                keys_or_values(i, 4)
                if m:
                    c_query_lo(i - 2)
                if a:
                    b_front(i)
                if s:
                    c_scores(i - 3, 5)
                keys_or_values(i, 5)
                if g:
                    b_quant(i - 1)
                if s:
                    c_scores(i - 3, 6)
                if g:
                    b_round(i - 1)
                if i == 0:
                    dve.wait_ge(ld["x1"], 16)
                if i + 2 < T:
                    ln_stats(("A", i + 2), xs[:, i + 2, :], 1e-5)
                if s:
                    c_scores(i - 3, 7)
                if i == FRONT - 3:
                    for stage in (d_stats, d_square, d_scale):
                        for u in range(TB):
                            stage(u)
                if i == 1:
                    ternary(2)
                    int8_scales()
                if i in KEY_SPLITS:
                    split_lo("k", KEY_SPLITS.index(i))
                if i == FRONT - 1:
                    split_lo("q", 0)

            def d_softmax(g):
                r = g % 2
                dve.wait_ge(d_s, g + 1)
                run(V.tensor_reduce(mxD[:, r, 0:1], bank[2 + r][:, 0:P], AX.X, ALU.max))
                step(V.tensor_reduce(mxD[:, r, 1:2], bank[2 + r][:, P:3 * P], AX.X, ALU.max))
                V.tensor_scalar(nmD[:, r, :], mxD[:, r, :], -SCALE / QSCALE ** 2, None, ALU.mult).then_inc(d_nm, 1)

            def d_normalise(g):
                r = g % 2
                dve.wait_ge(d_e, 2 * g + 2)
                step(V.reciprocal(riD[:, r, :], rsD[:, r, :]))
                run(V.tensor_scalar(probD[:, r, 0:P], probD[:, r, 0:P], riD[:, r, 0:1], None, ALU.mult))
                V.tensor_scalar(probD[:, r, P:3 * P], probD[:, r, P:3 * P], riD[:, r, 1:2], None,
                                ALU.mult).then_inc(d_p, 1)

            def d_qk_lo(g):
                dve.wait_ge(d_qh, g + 1)
                V.scalar_tensor_tensor(qk[:, g % 2, 1, :], bank[g % 2][:, :], QSCALE / (XSCALE * WSCALE),
                                       qk[:, g % 2, 0, :], ALU.mult, ALU.subtract).then_inc(d_qs, 1)

            def d_attn_lo(g):
                dve.wait_ge(d_ah, g + 1)
                V.scalar_tensor_tensor(attnT[:, g % 2, 1, :], bank[5][:, 0:S], QSCALE, attnT[:, g % 2, 0, :],
                                       ALU.mult, ALU.subtract).then_inc(d_as, 1)

            def d_add(b):
                dve.wait_ge(d_op, NH * (b + 1))
                for u in range(TB):
                    ins = V.scalar_tensor_tensor(hid[:, TB * b + u, :], bank[7][:, D * u:D * u + D],
                                                 1 / (QSCALE * WSCALE), hid[:, TB * b + u, :], ALU.mult, ALU.add)
                    run(ins) if u < TB - 1 else ins.then_inc(d_added, 1)
                dve.wait_ge(d_added, b + 1)

            def e_square(t):
                j = JOB["E", t]
                if t >= TB:
                    dve.wait_ge(d_vo, VO["X", t // TB - 1, t % TB] + 1)
                step(V.tensor_tensor_reduce(out=x2buf[:, t % TB, :], in0=hid[:, t, :], in1=hid[:, t, :], scale=1.0 / D,
                                            scalar=0.0, op0=ALU.mult, op1=ALU.add, accum_out=mv[:, j, 1:2]))
                V.tensor_scalar(powin[:, j:j + 1], mv[:, j, 1:2], 1e-6, None, ALU.add).then_inc(pow_in, 1)

            def e_scale(t):
                j = JOB["E", t]
                dve.wait_ge(pow_out, j + 1)
                V.tensor_scalar(x2buf[:, t % TB, :], hid[:, t, :], rstd[:, j:j + 1], None, ALU.mult).then_inc(e_x2, 1)

            def e_route(t):
                r = t % 2
                L = lg[:, r, :, :]
                mx8, pr, keep, w, r1, r2 = (L[:, i, :] for i in range(6))
                dve.wait_ge(e_ex, t + 1)
                step(V.tensor_reduce(mx8[:, 9:10], pr, AX.X, ALU.add))
                step(V.reciprocal(mx8[:, 10:11], mx8[:, 9:10]))
                step(V.tensor_scalar(pr, pr, mx8[:, 10:11], None, ALU.mult))
                step(V.max(mx8[:, 0:8], pr))
                step(V.memset(mx8[:, TOPK:8], 2.0))
                step(V.match_replace(out=keep, in_to_replace=mx8[:, 0:8], in_values=pr, imm_value=-1.0))
                step(V.tensor_scalar(keep, keep, 0.0, None, ALU.is_lt))

            def e_weights(t):
                r = t % 2
                L = lg[:, r, :, :]
                mx8, pr, keep, w, r1, r2 = (L[:, i, :] for i in range(6))
                step(V.tensor_tensor(w, keep, pr, ALU.mult))
                step(V.tensor_reduce(mx8[:, 9:10], w, AX.X, ALU.add))
                step(V.reciprocal(mx8[:, 10:11], mx8[:, 9:10]))
                step(V.tensor_scalar(w, w, mx8[:, 10:11], None, ALU.mult))
                if t >= 2:
                    dve.wait_ge(d_vo, VO["W", t // TB - 1, r] + 1)
                step(V.tensor_copy(lw[:, r, 0:E1], w))
                step(V.tensor_tensor(r1, w, lw[:, r, 0:E1], ALU.subtract))
                step(V.tensor_copy(lw[:, r, E1:2 * E1], r1))
                step(V.tensor_tensor(r2, r1, lw[:, r, E1:2 * E1], ALU.subtract))
                V.tensor_copy(lw[:, r, 2 * E1:3 * E1], r2).then_inc(e_w, 1)

            dve.wait_ge(ld["tri"], 16)
            V.tensor_copy(trib[:, :], tri[:, :]).then_inc(trib_ready, 1)
            G = B * NH
            for i in range(STEPS):
                b, h = divmod(i, NH)
                if 4 <= i < G + 4:
                    d_attn_lo(i - 4)
                if i == 0:
                    d_qk_lo(0)
                    split_lo("v", 0)
                    split_lo("v", 1)
                for key in vo_step(i, False):
                    if key[:2] != ("T", 0):
                        vo_read(key)
                if 1 <= i <= G:
                    d_softmax(i - 1)
                if 1 <= i < G:
                    d_qk_lo(i)
                for key in vo_step(i, True):
                    vo_read(key)
                if 1 <= i <= G:
                    d_normalise(i - 1)
                if i in SPLIT_AT:
                    split_lo(*SPLIT_AT[i])
                for u in range(TB):
                    before, after = TB * (b - 1) + u, TB * (b + 1) + u
                    if b >= 1 and h in (5, 6):
                        (e_square, e_scale)[h - 5](before)
                    if b + 1 < B and h in (u, 2 + u, 4 + u):
                        (d_stats, d_square, d_scale)[h // 2](after)
                    if b >= 1 and h in (11 + u, 13 + u):
                        (e_route, e_weights)[(h - 11) // 2](before)
                if b >= 1 and h == 4:
                    d_add(b - 1)

            def output(t, p):
                dve.wait_ge(e_yt, t + 1)
                step(V.scalar_tensor_tensor(hid[:, t, :], bank[p][:, 0:D], YSCALE, hid[:, t, :], ALU.mult, ALU.add))
                V.scalar_tensor_tensor(xs[:, t, :], hid[:, t, :], tg[:, 3:4], xs[:, t, :], ALU.mult,
                                       ALU.add).then_inc(e_out, 1)

            for n in range(2 * CH):
                half, c = divmod(n, CH)
                r, rows = n % 2, P if c < CH - 1 else LAST
                g = thE[0:rows, r, :]
                dve.wait_ge(e_th, n + 1)
                step(V.scalar_tensor_tensor(g, g, 1.0, bank[2 * r][0:rows, :], ALU.add, ALU.mult))
                if c < ROUTED:
                    V.tensor_tensor(g, g, bank[2 * r + 1][0:rows, :], ALU.mult).then_inc(e_gud, 1)
                    dve.wait_ge(e_gud, n + 1)
                    dve.wait_ge(e_wb, half * ROUTED + c + 1)
                    V.tensor_tensor(g, g, bank[weights_bank(n)][:, :], ALU.mult).then_inc(e_prod, 1)
                else:
                    V.scalar_tensor_tensor(g, g, ASCALE, bank[2 * r + 1][0:rows, :], ALU.mult,
                                           ALU.mult).then_inc(e_gud, 1)
                if EARLY <= n + AHEAD < CH:
                    split_lo("moe", n + AHEAD)
                for u in range(TB):
                    t = T - TB + u
                    if n in (0, 1):
                        (e_square, e_scale)[n](t)
                    if n in (7 + u, 9 + u):
                        (e_route, e_weights)[(n - 7) // 2](t)
                if n in LATE_AT:
                    vo_read(LATE_AT[n])
                dve.wait_ge(e_hi, n + 1)
                V.tensor_tensor(actE[0:rows, r, 1, :], g, actE[0:rows, r, 0, :], ALU.subtract).then_inc(e_act, 1)
                if n in OUT_AT:
                    output(OUT_AT[n], 4 + n % 2)
            for t in range(OUT_NOW, T):
                output(t, t % 2)

        @block.scalar
        def _(act):
            A = nc.scalar
            for dst, src, n in ((ident[:, :], ident_d, "consts"),
                                (gcol[:, :], gates, "gates"), (tok_i[:, :], itok, "tok"),
                                (hid[:, 0:2, :], wq, "wqo"), (hid[:, 2:4, :], wo, "wqo"),
                                (gw[:, :, :], gate_wT, "gw"), (bvb[:, :], bv, "biases"),
                                (bqb[:, :], bq, "biases"), (bkb, bk, "biases"), (bob[:, :], bo, "biases"),
                                (ln1_sb[:, :], ln1c, "ln"), (ln2_sb[:, :], ln2c, "ln")):
                act.dma_start(dst, src).then_inc(ld[n], 16)
            act.wait_ge(ld["gates"], 16)
            A.activation(tg[:, :], gcol[:, :], ACT.Tanh).then_inc(tg_ready, 1)
            def copy(dst, src, s):
                A.copy(dst, src).then_inc(s, 1)

            def a_hT(t):
                act.wait_ge(a_hTp, t + 1)
                if t >= 1:
                    act.wait_ge(a_z, 2 * t)
                copy(hT[:, :, :], bank[misc_bank("Th", t)][:, 0:D], a_hTs)

            def a_tanh(t):
                act.wait_ge(a_zsel, t + 1)
                if t >= 1:
                    act.wait_ge(a_gu, t)
                A.activation(ubuf, zbuf, ACT.Tanh, scale=0.5).then_inc(a_th, 1)

            def a_guT(t):
                act.wait_ge(a_guTp, t + 1)
                if t >= 1:
                    act.wait_ge(a_y, t)
                copy(guT[:, :, :], bank[misc_bank("Tg", t)][:, 0:D], a_guTs)

            def b_xT(t):
                act.wait_ge(b_xqTp, t + 1)
                if t >= 1:
                    act.wait_ge(b_gu, 2 * t)
                copy(qTb[:, 0, :, :], halfs(misc_bank("TxB", t))[:, 0:D], b_xqTs)

            def b_tanh(t, j):
                n = 2 * t + j
                act.wait_ge(b_gu, n + 1)
                act.wait_ge(b_xq, t + 1)
                if n >= 2:
                    act.wait_ge(b_p, n - 1)
                A.activation(thB[:, j, :], bank[0][:, :], ACT.Tanh, scale=cb[:, t, 3:4]).then_inc(b_th, 1)

            def b_qT(t):
                act.wait_ge(b_qTp, t + 1)
                if t >= 1:
                    act.wait_ge(b_d, t)
                copy(qTB, halfs(misc_bank("TqB", t))[:, 0:F0], b_qTs)

            def b_scale(t):
                act.wait_ge(b_cols, t + 1)
                A.activation(pB, pB, ACT.Identity, bias=magic[:, 0:1], scale=cb[:, t, 7:8]).then_inc(b_scaled, 1)

            def c_xT(t):
                act.wait_ge(c_xqTp, t + 1)
                if t >= 1:
                    act.wait_ge(c_qp, t)
                copy(qTb[:, 1, :, :], halfs(misc_bank("TxC", t))[:, 0:D], c_xqTs)

            def c_query_hi(t):
                act.wait_ge(c_qf, t + 1)
                if t == 0:
                    act.wait_ge(stage_zero, 1)
                else:
                    act.wait_ge(c_qTp, t)
                rows = hbuf[:, 2, :].rearrange("p (h d) -> p h d", d=XD)
                s = qstage.rearrange("p (h k d) -> p h k d", h=XH, d=XD)
                copy(s[:, :, 0:2, :], rows[:, :, None, :].broadcast_to([P, XH, 2, XD]), c_qhi)

            def c_qT(t):
                act.wait_ge(c_qTp, t + 1)
                if t >= 2:
                    act.wait_ge(c_s, T * (t - 1))
                copy(qTC[:, t % 2, :, :], bank[misc_bank("TqC", t)][:, :].bitcast(fp16), c_qTs)

            def c_exp(t, k):
                if k % 2 == 0:
                    act.wait_ge(c_nm, XG * t + k // 2 + 1)
                for h in range(2 * k, 2 * k + 2):
                    sc = scores[:, t % 2, h, :]
                    ins = A.activation(sc, sc, ACT.Exp, bias=nmC[:, t % 2, h:h + 1])
                ins.then_inc(c_p, 1)

            def c_pT(t, n):
                act.wait_ge(c_pTp, T * t + n + 1)
                if t >= 1:
                    act.wait_ge(c_pv, XG * (t - 1) + n // 2 + 1)
                copy(probT[:, 2 * n:2 * n + 2, :, :], bank[5][:, :], c_pTs)

            def c_oT_(t):
                act.wait_ge(c_pv, XG * (t + 1))
                if t >= 1:
                    act.wait_ge(c_oT, t)
                copy(oT_sb[:, :, :], bank[6][0:XA, :], c_pvs)

            def c_oqT(t):
                act.wait_ge(c_oqTp, t + 1)
                if t >= 1:
                    act.wait_ge(c_op, t)
                copy(oqT[:, :, :], halfs(misc_bank("Toq", t))[:, 0:D], c_oqTs)

            def keys(t):
                act.wait_ge(keys_T, t + 1)
                b, l = divmod(t, TB)
                act.wait_ge(keys_zero, 1)
                for j in range(2):
                    rows = slice(64 * j, 64 * j + 64)
                    copy(keysT[rows, b, :, j, P * l:P * l + P],
                         bank[5][rows, :].bitcast(fp16).rearrange("p (k n) -> p k n", k=XH // 2), keysT_ready)

            def magnitudes():
                act.wait_ge(ld["raw"], 48)
                for k in range(3):
                    if k:
                        act.wait_ge(wabs_ready, k)
                    A.activation(armR[:, 6144:8192], wraw[:, k, :], ACT.Abs,
                                 accum_out=wsum[:, k:k + 1]).then_inc(wabs_ready, 1)

            def split_hi(kind, n):
                for k, (lo, hi) in enumerate(LOADS):
                    if (kind, n) == ("moe", lo):
                        act.wait_ge(ld_moe[k], 16)
                if kind in "kqv" and n == 0:
                    act.wait_ge(ld[kind + "w"], 16)
                if kind == "o":
                    act.wait_ge(ld["ow_last" if n == PIECES - 1 else "ow"], 16)
                if (kind, n) == ("k", 0):
                    act.wait_ge(keys_staged, T)
                if (kind, n) == ("v", 0):
                    act.wait_ge(c_op, T)
                if (kind, n) == ("moe", 0):
                    act.wait_ge(d_vo, VO["V", B - 1, TB - 1] + 1)
                if SPLIT[kind, n]:
                    act.wait_ge(w_lo, SPLIT[kind, n])
                A.activation(split_piece(kind, n)[:, 0, :], raw_piece(kind, n), ACT.Copy,
                             scale=WSCALE).then_inc(w_hi, 1)

            a_hT(0)
            for i in range(FRONT):
                a, g, m, s, r, o = (0 <= i - n < T for n in range(6))
                if g:
                    b_xT(i - 1)
                if i == 0:
                    magnitudes()
                if o:
                    c_oT_(i - 5)
                if r:
                    c_pT(i - 4, 0)
                if a:
                    a_tanh(i)
                if g:
                    b_tanh(i - 1, 0)
                if KV.get((i, 0), "V")[0] == "K":
                    keys(KV[i, 0][1])
                if m:
                    b_qT(i - 2)
                if a:
                    a_guT(i)
                if KV.get((i, 1), "V")[0] == "K":
                    keys(KV[i, 1][1])
                if r:
                    c_pT(i - 4, 1)
                if r:
                    c_pT(i - 4, 2)
                if s:
                    c_exp(i - 3, 0)
                if s:
                    c_exp(i - 3, 1)
                if o:
                    c_oqT(i - 5)
                if r:
                    c_pT(i - 4, 3)
                if KV.get((i, 2), "V")[0] == "K":
                    keys(KV[i, 2][1])
                if i + 1 < T:
                    a_hT(i + 1)
                if m:
                    c_xT(i - 2)
                if g:
                    b_tanh(i - 1, 1)
                if i == 1:
                    act.wait_ge(xwT_psum, 1)
                    copy(xwT.rearrange("p k c n -> p (k c n)"), halfs(4)[:, 0:1024], xwT_ready)
                if r:
                    c_pT(i - 4, 4)
                if m:
                    c_query_hi(i - 2)
                if r:
                    c_pT(i - 4, 5)
                if s:
                    c_exp(i - 3, 2)
                if s:
                    c_exp(i - 3, 3)
                if s:
                    c_exp(i - 3, 4)
                if g and i == 1:
                    act.wait_ge(magic_ready, 1)
                if m:
                    c_qT(i - 2)
                if g:
                    b_scale(i - 1)
                if r:
                    c_pT(i - 4, 6)
                if s:
                    c_exp(i - 3, 5)
                if r:
                    c_pT(i - 4, 7)
                if s:
                    c_exp(i - 3, 6)
                if s:
                    c_exp(i - 3, 7)
                if i == FRONT - 1:
                    split_hi("q", 0)
                if i in KEY_SPLITS:
                    split_hi("k", KEY_SPLITS.index(i))

            def route_exp(b):
                for u in range(TB):
                    act.wait_ge(d_vofree, VO["G", b, u] + 1)
                    A.activation(lg[:, u, 1, :], lg[:, u, 1, :], ACT.Exp).then_inc(e_ex, 1)

            G = B * NH
            act.wait_ge(ternary_ready, 3)
            for i in range(STEPS):
                b, h = divmod(i, NH)
                if 4 <= i < G + 4:
                    g = i - 4
                    act.wait_ge(d_a, g + 1)
                    if g >= 2:
                        act.wait_ge(d_op, g - 1)
                    A.activation(attnT[:, g % 2, 0, :], bank[5][:, 0:S], ACT.Copy, scale=QSCALE).then_inc(d_ah, 1)
                if h == 11 and b >= 1:
                    route_exp(b - 1)
                if i < G:
                    act.wait_ge(d_qkp, i + 1)
                    if i >= 2:
                        act.wait_ge(d_s, i - 1)
                    A.activation(qk[:, i % 2, 0, :], bank[i % 2][:, :], ACT.Copy,
                                 scale=QSCALE / (XSCALE * WSCALE)).then_inc(d_qh, 1)
                if i == 0:
                    split_hi("v", 0)
                    split_hi("v", 1)
                if 2 <= i < G + 2:
                    g = i - 2
                    act.wait_ge(d_pTp, g + 1)
                    if g >= 2:
                        act.wait_ge(d_a, g - 1)
                    copy(probDT[:, g % 2, :], bank[4][:, 0:3 * P], d_pTs)
                if 1 <= i < G + 1:
                    g = i - 1
                    r = g % 2
                    act.wait_ge(d_nm, g + 1)
                    if g >= 2:
                        act.wait_ge(d_pTp, g - 1)
                    A.activation(probD[:, r, 0:P], bank[2 + r][:, 0:P], ACT.Exp, bias=nmD[:, r, 0:1],
                                 scale=SCALE / QSCALE ** 2, accum_out=rsD[:, r, 0:1]).then_inc(d_e, 1)
                    A.activation(probD[:, r, P:3 * P], bank[2 + r][:, P:3 * P], ACT.Exp, bias=nmD[:, r, 1:2],
                                 scale=SCALE / QSCALE ** 2, accum_out=rsD[:, r, 1:2]).then_inc(d_e, 1)
                if i in SPLIT_AT:
                    split_hi(*SPLIT_AT[i])

            for n in range(2 * CH):
                half, c = divmod(n, CH)
                r, rows = n % 2, P if c < CH - 1 else LAST
                act.wait_ge(e_gu, n + 1)
                if n >= 2:
                    act.wait_ge(e_act, n - 1)
                A.activation(thE[0:rows, r, :], bank[2 * r][0:rows, :], ACT.Tanh,
                             scale=0.5 / (WSCALE * XSCALE)).then_inc(e_th, 1)
                if EARLY <= n + AHEAD < CH:
                    split_hi("moe", n + AHEAD)
                if n == 6:
                    route_exp(B - 1)
                if c < ROUTED:
                    act.wait_ge(e_prod, half * ROUTED + c + 1)
                else:
                    act.wait_ge(e_gud, n + 1)
                if n >= 2:
                    act.wait_ge(e_dn, n - 1)
                copy(actE[0:rows, r, 0, :], thE[0:rows, r, :], e_hi)
                if c == CH - 1:
                    act.wait_ge(e_dn, n + 1)
                    for k in range(C):
                        copy(ctxT_sb[:, k, 512 * half:512 * half + 512], bank[6 + k][:, :], e_yT)

        @block.tensor
        def _(pe):
            M = nc.tensor.matmul
            Tr = nc.tensor.transpose

            def key_value(item):
                n = list(KV.values()).index(item)
                if n == 0:
                    pe.wait_ge(ld["wkv"], 32)
                else:
                    before, tile = list(KV.values())[n - 1]
                    if before == "K":
                        pe.wait_ge(keys_staged, tile + 1)
                    else:
                        pe.wait_ge(v_ready, XG * (tile + 1))
                kind, t = item
                for i in range(C):
                    last = M(bank[6][:, 0:D], ctxT_sb[:, i, P * t:P * t + P], xw[:, 0 if kind == "K" else 1, i, :],
                             start=i == 0, stop=i == C - 1)
                last.then_inc(kproj if kind == "K" else vproj, 1)

            def keys_transposed(t):
                pe.wait_ge(keys_staged, t + 1)
                if t:
                    pe.wait_ge(keysT_ready, 2 * t)
                transposes(bank[5][:, :].bitcast(fp16), kstage, XH // 2, identh[:, :], keys_T)

            PARTS = ((0, 0), (0, 1), (1, 0))

            def misc(kind, t):
                n = MISC[kind, t]
                if n >= 2:
                    before, tile = MISC_USES[n - 2]
                    pe.wait_ge(READER[before], tile + 1)
                return misc_bank(kind, t)

            def transposes(p, src, n, identity, done):
                for c in range(n):
                    last = Tr(p[:, P * c:P * c + P], src[:, P * c:P * c + P], identity)
                last.then_inc(done, 1)

            def a_th_(t):
                p = misc("Th", t)
                pe.wait_ge(a_h, t + 1)
                transposes(bank[p], hbuf[:, 0, :], C, ident[:, :], a_hTp)

            def a_zz(t):
                pe.wait_ge(a_hTs, t + 1)
                if t >= 2:
                    pe.wait_ge(b_p, 2 * t - 2)
                elif t == 1:
                    pe.wait_ge(a_x1, 1)
                for half in range(2):
                    for i in range(C):
                        last = M(bank[half][:, :], hT[:, i, :], ctxT_sb[:, i, 512 * half:512 * half + 512],
                                 start=i == 0, stop=i == C - 1)
                    last.then_inc(a_z, 1)

            def a_tgu(t):
                p = misc("Tg", t)
                pe.wait_ge(a_gu, t + 1)
                transposes(bank[p], gubuf, C, ident[:, :], a_guTp)

            def a_yy(t):
                pe.wait_ge(a_guTs, t + 1)
                if t >= 1:
                    pe.wait_ge(b_p, 2 * t - 1)
                else:
                    pe.wait_ge(a_zsel, 1)
                for half in range(2):
                    for i in range(C):
                        last = M(bank[half][:, :], guT[:, i, :], ctxT_sb[:, i, 512 * half:512 * half + 512],
                                 start=i == 0, stop=i == C - 1)
                last.then_inc(a_y, 1)

            def b_tx(t):
                p = misc("TxB", t)
                pe.wait_ge(b_xq, t + 1)
                transposes(halfs(p), qb[:, 0, :], C, identb[:, :], b_xqTp)

            def b_gate_up(t, j):
                n = 2 * t + j
                pe.wait_ge(b_xqTs, t + 1)
                pe.wait_ge(ternary_ready, 2)
                if t + 1 < T:
                    pe.wait_ge(a_x1 if j else a_zsel, t + 2)
                if n:
                    pe.wait_ge(b_p, n)
                for k in range(2):
                    for i in range(C):
                        last = M(bank[k][:, :], qTb[:, 0, i, :], gub[:, k, i, 512 * j:512 * j + 512],
                                 start=i == 0, stop=i == C - 1)
                last.then_inc(b_gu, 1)

            def b_tq(t):
                p = misc("TqB", t)
                pe.wait_ge(b_q, t + 1)
                transposes(halfs(p), qB, FC, identb[:, :], b_qTp)

            def b_down(t):
                p = misc("Dn", t)
                pe.wait_ge(b_qTs, t + 1)
                pe.wait_ge(ternary_ready, 3)
                for c in range(FC):
                    last = M(bank[p][:, 0:D], qTB[:, c, :], dnb[:, c, :], start=c == 0, stop=c == FC - 1)
                last.then_inc(b_d, 1)

            def c_tx(t):
                p = misc("TxC", t)
                pe.wait_ge(c_xq, t + 1)
                transposes(halfs(p), qb[:, 1, :], C, identb[:, :], c_xqTp)

            def c_project(t):
                p = misc("qp", t)
                pe.wait_ge(c_xqTs, t + 1)
                pe.wait_ge(xwT_ready, 1)
                pe.wait_ge(swb_ready, 4)
                for i in range(C):
                    last = M(bank[p][:, 0:D], qTb[:, 1, i, :], xwT[:, 0, i, :], start=i == 0, stop=i == C - 1)
                last.then_inc(c_qp, 1)

            def c_tq(t):
                p = misc("TqC", t)
                pe.wait_ge(c_q, t + 1)
                transposes(bank[p][:, :].bitcast(fp16), qstage, XH // 2, identh[:, :], c_qTp)

            def c_score(t, k):
                n = T * t + k
                if k == 0:
                    pe.wait_ge(c_qTs, t + 1)
                    pe.wait_ge(keysT_ready, 2 * TB * (t // TB + 1))
                if n >= 2:
                    pe.wait_ge(c_sm, 2 * (n - 1))
                M(bank[SB[k % 2]][:, :], qTC[:, t % 2, k, :], keysT[:, t // TB, k, :, :],
                  start=True, stop=True).then_inc(c_s, 1)

            def c_tp(t, n):
                m = T * t + n
                pe.wait_ge(c_p, T * t + n + 1)
                if m >= 1:
                    pe.wait_ge(c_pTs, m)
                for i in range(4):
                    h, l = 2 * n + i // 2, i % 2
                    last = Tr(bank[5][:, P * i:P * i + P], scores[:, t % 2, h, P * l:P * l + P], ident[:, :])
                last.then_inc(c_pTp, 1)

            def c_pv_(t, g):
                pe.wait_ge(c_pTs, T * t + 2 * g + 2)
                if t == 0 and g == 0:
                    pe.wait_ge(v_ready, XG * T)
                if g == 0 and t >= 1:
                    pe.wait_ge(c_pvs, t)
                for i in range(2 * XG):
                    j, l = divmod(i, 2)
                    h = XG * g + j
                    last = M(bank[6][0:XA, P * g:P * g + P], vaug[:, TB * (t // TB) + l, h, :], probT[:, h, l, :],
                             start=i == 0, stop=i == 2 * XG - 1)
                last.then_inc(c_pv, 1)

            def c_to(t):
                p = misc("To", t)
                pe.wait_ge(c_pvs, t + 1)
                for g in range(XG):
                    last = Tr(bank[p][:, XA * g:XA * g + XA], oT_sb[:, g, :], ident[0:XA, 0:XA])
                last.then_inc(c_oT, 1)

            def c_toq(t):
                p = misc("Toq", t)
                pe.wait_ge(c_o, t + 1)
                transposes(halfs(p), oq, C, identb[:, :], c_oqTp)

            def c_outp(t):
                p = misc("op", t)
                pe.wait_ge(c_oqTs, t + 1)
                for i in range(C):
                    last = M(bank[p][:, 0:D], oqT[:, i, :], xwT[:, 1, i, :], start=i == 0, stop=i == C - 1)
                last.then_inc(c_op, 1)

            def vo_make(key):
                kind, b, u = key
                n = VO[key]
                p = vo_bank(key)
                if n:
                    pe.wait_ge(d_vofree, n)
                else:
                    pe.wait_ge(c_pvs, T)
                t = TB * b + u
                if kind in "TX":
                    pe.wait_ge(d_xn if kind == "T" else e_x2, t + 1)
                    h = hbuf[:, u, :] if kind == "T" else x2buf[:, u, :]
                    for c in range(C):
                        last = Tr(bank[p][:, P * c:P * c + P], h[:, P * c:P * c + P], ident[:, :])
                elif kind == "G":
                    pe.wait_ge(d_vofree, VO["X", b, u] + 1)
                    pe.wait_ge(ld["gw"], 16)
                    for i in range(C):
                        last = M(bank[p][:, 0:E1], ctxT_sb[:, i, P * t:P * t + P], gw[:, i, :], start=i == 0,
                                 stop=i == C - 1)
                elif kind == "W":
                    pe.wait_ge(e_w, t + 1)
                    last = Tr(halfs(p)[0:3 * E1, 0:P], lw[:, u, :], identb[:, :])
                elif kind == "V":
                    q, l = divmod(u, TB)
                    pe.wait_ge(d_xT2, XT2["T", b])
                    pe.wait_ge(w_lo, SPLIT["v", q] + 1)
                    t, w = TB * b + l, split_piece("v", q)
                    for i in range(C):
                        for m, (x_, w_) in enumerate(PARTS):
                            last = M(bank[p][:, :], xT2[:, x_, i, P * t:P * t + P], w[:, w_, 512 * i:512 * i + 512],
                                     start=i == 0 and m == 0, stop=i == C - 1 and m == 2)
                last.then_inc(d_vo, 1)

            def d_qk(g):
                b, h = divmod(g, NH)
                pe.wait_ge(d_xT2, XT2["T", b])
                if g >= 2:
                    pe.wait_ge(d_qs, g - 1)
                else:
                    pe.wait_ge(b_p, 2 * T)
                q, at = divmod(h, NH // PIECES)
                if b == 0 and at == 0:
                    pe.wait_ge(w_lo, SPLIT["q", q] + 1)
                for k, kind in enumerate("qk"):
                    for i in range(C):
                        for m, (w_, x_) in enumerate(PARTS):
                            last = M(bank[g % 2][:, S * k:S * k + S],
                                     split_piece(kind, q)[:, w_, 512 * i + HD * at:512 * i + HD * at + HD],
                                     xT2[:, x_, i, S * b:S * b + S], start=i == 0 and m == 0,
                                     stop=i == C - 1 and m == 2)
                last.then_inc(d_qkp, 1)

            pe.wait_ge(identb_ready, 2)
            a_th_(0)
            pe.wait_ge(ld["ctx"], 16)
            a_zz(0)
            for i in range(FRONT):
                a, g, m, s, r, o = (0 <= i - n < T for n in range(6))

                def unit(k):
                    if s:
                        c_score(i - 3, k)
                    if KV.get((i, k - 1), "V")[0] == "K":
                        keys_transposed(KV[i, k - 1][1])
                    if (i, k) in KV:
                        key_value(KV[i, k])
                    if r:
                        if k in (2, 4, 6):
                            c_pv_(i - 4, k // 2 - 1)
                        c_tp(i - 4, k)

                if m:
                    b_tq(i - 2)
                if g:
                    b_tx(i - 1)
                unit(0)
                if o:
                    c_pv_(i - 5, XG - 1)
                if g:
                    b_gate_up(i - 1, 0)
                unit(1)
                if o:
                    c_to(i - 5)
                if i == 0:
                    pe.wait_ge(wabs_ready, 3)
                    pe.wait_ge(ones_ready, 2)
                    M(bank[7][:, 0:3], ones[:, :], wsum[:, :], start=True, stop=True).then_inc(wsum_ready, 1)
                    pe.wait_ge(xwb_ready, 4)
                    for k in range(2):
                        for c in range(C):
                            for n in range(C):
                                at = 512 * k + D * n + P * c
                                last = Tr(halfs(4)[:, at:at + P], xwb[:, k, c, P * n:P * n + P], identb[:, :])
                    last.then_inc(xwT_psum, 1)
                if a:
                    a_tgu(i)
                if m:
                    b_down(i - 2)
                unit(2)
                if a:
                    a_yy(i)
                if i == FRONT - 1:
                    for u in range(TB):
                        vo_make(("T", 0, u))
                if o:
                    c_toq(i - 5)
                unit(3)
                if i + 1 < T:
                    a_th_(i + 1)
                if o:
                    c_outp(i - 5)
                if m:
                    c_tx(i - 2)
                if g:
                    b_gate_up(i - 1, 1)
                if i == 1:
                    pe.wait_ge(diag_ready, 4)
                    pe.wait_ge(ternary_ready, 1)
                    for n in range(4):
                        last = M(bank[7][:, P * n:P * n + P], ones[:, :], diag[:, n, :], start=True, stop=True)
                    last.then_inc(swb_psum, 1)
                unit(4)
                if m:
                    c_project(i - 2)
                unit(5)
                if i + 1 < T:
                    a_zz(i + 1)
                if m:
                    c_tq(i - 2)
                unit(6)
                if i == FRONT - 1:
                    d_qk(0)
                unit(7)

            def d_score(g):
                pe.wait_ge(d_qs, g + 1)
                if g >= 2:
                    pe.wait_ge(d_e, 2 * g - 2)
                else:
                    pe.wait_ge(c_x3, T)
                    pe.wait_ge(trib_ready, 1)
                s, v = bank[2 + g % 2], qk[:, g % 2]
                for m, (q, k) in enumerate(PARTS):
                    M(s[:, 0:P], v[:, q, 0:P], v[:, k, S:S + P], start=m == 0, stop=False)
                M(s[:, 0:P], identb[:, :], trib[:, :], start=False, stop=True)
                for m, (q, k) in enumerate(PARTS):
                    M(s[:, P:3 * P], v[:, q, P:S], v[:, k, S:2 * S], start=m == 0, stop=False)
                M(s[:, 2 * P:3 * P], identb[:, :], trib[:, :], start=False, stop=True).then_inc(d_s, 1)

            def d_tp(g):
                pe.wait_ge(d_p, g + 1)
                if g >= 1:
                    pe.wait_ge(d_pTs, g)
                for i in range(3):
                    last = Tr(bank[4][:, P * i:P * i + P], probD[:, g % 2, P * i:P * i + P], ident[:, :])
                last.then_inc(d_pTp, 1)

            def d_pv(g):
                b, h = divmod(g, NH)
                pe.wait_ge(d_pTs, g + 1)
                pe.wait_ge(d_vofree, VO["V", b, TB * (h // (NH // PIECES)) + TB - 1] + 1)
                if g >= 1:
                    pe.wait_ge(d_as, g)
                M(bank[5][:, 0:S], vals[:, b % 2, 0, HD * h:HD * h + HD], probDT[:, g % 2, 0:S], start=True, stop=False)
                M(bank[5][:, P:S], vals[:, b % 2, 1, HD * h:HD * h + HD], probDT[:, g % 2, S:3 * P],
                  start=False, stop=True).then_inc(d_a, 1)

            def d_project(g):
                b, h = divmod(g, NH)
                pe.wait_ge(d_as, g + 1)
                q, at = divmod(h, NH // PIECES)
                if b == 0 and at == 0:
                    pe.wait_ge(w_lo, SPLIT["o", q] + 1)
                if g == 0:
                    pe.wait_ge(c_sm, XH * T)
                elif h == 0:
                    pe.wait_ge(d_added, b)
                for u in range(TB):
                    for m, (x_, w_) in enumerate(PARTS):
                        last = M(bank[7][:, D * u:D * u + D], attnT[:, g % 2, x_, P * u:P * u + P],
                                 split_piece("o", q)[:, w_, D * at:D * at + D],
                                 start=h == 0 and m == 0 and u == 0, stop=h == NH - 1 and m == 2 and u == TB - 1)
                last.then_inc(d_op, 1)

            G = B * NH
            for i in range(STEPS):
                b, h = divmod(i, NH)
                for key in vo_step(i, False):
                    if key[:2] != ("T", 0):
                        vo_make(key)
                if 1 <= i < G:
                    d_qk(i)
                if 1 <= i <= G:
                    d_score(i - 1)
                for key in vo_step(i, True):
                    vo_make(key)
                if 2 <= i <= G + 1:
                    d_tp(i - 2)
                if 3 <= i <= G + 2:
                    d_pv(i - 3)
                if 5 <= i < G + 5:
                    d_project(i - 5)

            def e_down(n):
                half, c = divmod(n, CH)
                r, rows = n % 2, P if c < CH - 1 else LAST
                pe.wait_ge(e_act, n + 1)
                if n == 0:
                    pe.wait_ge(d_added, B)
                if c == 0 and half == 1:
                    pe.wait_ge(e_yT, C)
                w = split_piece("moe", c)[0:rows, :, 4 * P:WCH]
                for k in range(C):
                    for m, (a, b) in enumerate(PARTS):
                        last = M(bank[6 + k][:, :], w[:, a, P * k:P * k + P], actE[0:rows, r, b, :],
                                 start=c == 0 and m == 0, stop=c == CH - 1 and m == 2)
                last.then_inc(e_dn, 1)

            def output_rows(t, p):
                pe.wait_ge(e_yT, C * (t // (T // 2) + 1))
                if t >= 2:
                    pe.wait_ge(e_out, t - 1)
                for c in range(C):
                    last = Tr(bank[p][:, P * c:P * c + P], ctxT_sb[:, c, P * t:P * t + P], ident[:, :])
                last.then_inc(e_yt, 1)

            for n in range(2 * CH):
                half, c = divmod(n, CH)
                r, rows = n % 2, P if c < CH - 1 else LAST
                if half == 0:
                    pe.wait_ge(w_lo, SPLIT["moe", n] + 1)
                if n == LATE_END + 1:
                    pe.wait_ge(d_vofree, VO_END)
                if n == 0:
                    pe.wait_ge(ld["sel"], 16)
                if n >= 2:
                    pe.wait_ge(e_gud, n - 1)
                for k in range(2):
                    for i in range(C):
                        at = 2 * P * k + P * i
                        for m, (a, b) in enumerate(PARTS):
                            last = M(bank[2 * r + k][0:rows, :], split_piece("moe", c)[:, a, at:at + rows],
                                     xT2[:, b, i, 512 * half:512 * half + 512], start=i == 0 and m == 0,
                                     stop=i == C - 1 and m == 2)
                last.then_inc(e_gu, 1)
                if c < ROUTED:
                    if 1 <= n <= LATE_END + 1:
                        pe.wait_ge(e_prod, n)
                    elif n >= 2:
                        pe.wait_ge(e_act, n - 1)
                    M(bank[weights_bank(n)][:, :], sel[:, P * c:P * c + P], wTb[:, 512 * half:512 * half + 512],
                      start=True, stop=True).then_inc(e_wb, 1)
                if n >= 1:
                    e_down(n - 1)
                if n in LATE_AT:
                    vo_make(LATE_AT[n])
                if n in OUT_AT:
                    output_rows(OUT_AT[n], 4 + n % 2)
            e_down(2 * CH - 1)
            for t in range(OUT_NOW, T):
                output_rows(t, t % 2)

def kernel(**inputs):
    import numpy as np
    import concourse.bacc as bacc
    from concourse.bass_utils import run_bass_kernel_spmd

    g = {k: np.asarray(v) for k, v in inputs.items()}

    def tiles(a):
        a = a.reshape(-1, P, a.shape[-1])
        return np.ascontiguousarray(a.transpose(1, 0, 2))

    def rows(v):
        return np.ascontiguousarray(np.broadcast_to(v.reshape(1, -1), (P, v.size)))

    def flat(a):
        return np.ascontiguousarray(a.reshape(P, -1))

    def pieces(w):
        return flat(w.reshape(4, -1, C, P).transpose(3, 0, 2, 1))

    eye = np.eye(P, dtype=np.float32)
    tri = np.where(np.tril(np.ones((P, P), bool)), 0.0, -1e9 / SCALE * QSCALE ** 2).astype(np.float32)
    expert = np.arange(ROUTED * P) // I1
    sel = np.where(expert[None, :] == (np.arange(3 * E1) % E1)[:, None],
                   np.float32(ASCALE).view(np.uint32) >> 16, 0).astype(np.uint16)

    w1, w2 = g["L1_ffn_w1"], g["L1_ffn_w2"]
    sgu, sdn = g["L1_ffn_sh_gu_w"], g["L1_ffn_sh_down_w"]
    pad = np.zeros((CH * P - E1 * I1 - SHI, D), np.float32)
    up = np.concatenate([w1[:, I1:, :].reshape(-1, D), sgu[SHI:], pad])
    gate = np.concatenate([w1[:, :I1, :].reshape(-1, D), sgu[:SHI], pad])
    down = np.concatenate([w2.transpose(0, 2, 1).reshape(-1, D), sdn.T, pad])
    moe = np.zeros((P, CH, WCH), np.float32)
    for k, w in enumerate((gate, up)):
        moe[:, :, 2 * P * k:2 * P * k + 2 * P] = w.reshape(CH, P, C, P).transpose(3, 0, 2, 1).reshape(P, CH, C * P)
    moe[:, :, 4 * P:] = down.reshape(CH, P, D).transpose(1, 0, 2)

    qw = g["L1_ffn_q_w"].reshape(NH, QHD, D)[:, :HD, :].reshape(NH * HD, D)
    kv = g["L1_ffn_kv_w"]
    arrays = {
        "x": tiles(g["x"].reshape(-1, D)),
        "itok": np.ascontiguousarray(g["itok_BxS_13_99985"].reshape(T, P).T),
        "ctxT": tiles(g["ctx_2048"].reshape(-1, D).T),
        "mask": np.ascontiguousarray(g["mask_BxSxS2_ff0"].reshape(T, P, S)),
        "gates": rows(np.concatenate([g["g_xattn"], g["g_ffn"]])),
        "w_gate": flat(tiles(g["L0_ffn_w_gate"].T)),
        "w_up": flat(tiles(g["L0_ffn_w_up"].T)),
        "w_down": flat(tiles(g["L0_ffn_w_down"].T)),
        "wq": tiles(g["L1_xattn_wq"]),
        "wkT": tiles(g["L1_xattn_wk"].T),
        "wvT": tiles(g["L1_xattn_wv"].T),
        "wo": tiles(g["L1_xattn_wo"]),
        "bq": rows(g["L1_xattn_bq"]),
        "bk": rows(g["L1_xattn_bk"]),
        "bv": rows(g["L1_xattn_bv"]),
        "bo": rows(g["L1_xattn_bo"]),
        "ln1c": np.ascontiguousarray(g["L1_ffn_ln1_w"].reshape(C, P).T),
        "ln2c": np.ascontiguousarray(g["L1_ffn_ln2_w"].reshape(C, P).T),
        "qwT": pieces(qw),
        "kwT": pieces(kv[:NH * HD]),
        "vwT": pieces(kv[NH * HD:2 * NH * HD]),
        "owT": flat(tiles(g["L1_ffn_o_w"].T)),
        "gate_wT": tiles(g["L1_ffn_gate_w"].T),
        "w_moe": moe.reshape(P, -1),
        "ident_d": eye, "tri_d": tri, "sel_d": sel,
    }
    nc = bacc.Bacc("TRN2", target_bir_lowering=False, num_devices=1)
    aps = {}
    for n, a in arrays.items():
        aps[n] = nc.dram_tensor("in_" + n, a.shape, mybir.dt.from_np(a.dtype), kind="ExternalInput").ap()
    aps["sel_d"] = aps["sel_d"].bitcast(mybir.dt.bfloat16)
    out = nc.dram_tensor("out_y", (P, T, D), mybir.dt.float32, kind="ExternalOutput").ap()
    flamingo(nc, out=out, **aps)
    r = run_bass_kernel_spmd(nc, [{"in_" + n: a for n, a in arrays.items()}], core_ids=[0])
    y = r.results[0]["out_y"]
    return np.ascontiguousarray(y.transpose(1, 0, 2)).reshape(B, S, D)
```
